# Optimizing a Trainium2 kernel written in Bass

```python
import numpy as np
import jax
import jax.numpy as jnp

def _softmax(x, axis=-1):
    return jax.nn.softmax(x, axis=axis)

def _gelu(x):
    return jax.nn.gelu(x, approximate=True)

def _silu(x):
    return jax.nn.silu(x)

def _sigmoid(x):
    return jax.nn.sigmoid(x)

def _layernorm(x, axis=-1, eps=1e-05):
    m = jnp.mean(x, axis=axis, keepdims=True)
    v = jnp.var(x, axis=axis, keepdims=True)
    return (x - m) / jnp.sqrt(v + eps)

def _scatter_add(tgt, idx, src, axis=0):
    return tgt.at[idx].add(src)

def _segment_sum(src, seg, n):
    return jax.ops.segment_sum(src, seg, n)
kernel_name = 'mk_audio_tower_d1_tok_audfeat256_r4_bad35e'

def setup_inputs(seed: int=0):
    np.random.seed(seed)
    _w = jnp.asarray

    def _rec_inputs():
        import jax
        import jax.numpy as jnp
        _rk = jax.random.key(seed)
        x = jax.random.uniform(jax.random.fold_in(_rk, 1), (64, 4, 256), jnp.float32, 0.0, 0.999986)
        return x
    x = _rec_inputs()

    def _L0_tok_setup():
        import jax, jax.numpy as jnp
        import numpy as np
        T = 8
        key = jax.random.key(seed)
        ks = jax.random.split(key, 9)
        bs, dims, L, d = (16, 4, 512, 64)
        x = jax.random.uniform(ks[0], (bs, dims, L), dtype=jnp.float32)
        s_in = 1.0 / np.sqrt(dims)
        s_d = 1.0 / np.sqrt(d)
        W1 = jax.random.uniform(ks[1], (d, dims), minval=-s_in, maxval=s_in, dtype=jnp.float32)
        b1 = jax.random.uniform(ks[2], (d,), minval=-s_in, maxval=s_in, dtype=jnp.float32)
        W2 = jax.random.uniform(ks[3], (d, d), minval=-s_d, maxval=s_d, dtype=jnp.float32)
        b2 = jax.random.uniform(ks[4], (d,), minval=-s_d, maxval=s_d, dtype=jnp.float32)
        W3 = jax.random.uniform(ks[5], (d, dims), minval=-s_in, maxval=s_in, dtype=jnp.float32)
        b3 = jax.random.uniform(ks[6], (d,), minval=-s_in, maxval=s_in, dtype=jnp.float32)
        W4 = jax.random.uniform(ks[7], (d, d), minval=-s_d, maxval=s_d, dtype=jnp.float32)
        b4 = jax.random.uniform(ks[8], (d,), minval=-s_d, maxval=s_d, dtype=jnp.float32)
        return dict(x=x, W1=W1, b1=b1, W2=W2, b2=b2, W3=W3, b3=b3, W4=W4, b4=b4)
    _L0_tok_all = _L0_tok_setup()
    _L0_tok_in = {k: v for k, v in _L0_tok_all.items() if k in ('W1', 'b1', 'W2', 'b2', 'W3', 'b3', 'W4', 'b4')}
    del _L0_tok_all

    def _L0_attn_setup():
        import jax, jax.numpy as jnp
        import numpy as np

        def softcap(x, a=10.0):
            return a * jnp.tanh(x / a)
        key = jax.random.key(seed)
        B, T, D = (4, 512, 64)
        ks = jax.random.split(key, 5)
        w = lambda k, s: jax.random.normal(k, s, dtype=jnp.float32) * 0.02
        return {'x': jax.random.normal(ks[0], (B, T, D), dtype=jnp.float32), 'Wq': w(ks[1], (D, D)), 'bq': jnp.zeros((D,), jnp.float32), 'Wk': w(ks[2], (D, D)), 'bk': jnp.zeros((D,), jnp.float32), 'Wv': w(ks[3], (D, D)), 'bv': jnp.zeros((D,), jnp.float32), 'Wg': w(ks[4], (D, 3 * D)), 'bg': jnp.zeros((3 * D,), jnp.float32), 'input_bias': -jnp.ones((D,), jnp.float32), 'norm_scale': jnp.ones((D,), jnp.float32)}
    _L0_attn_all = _L0_attn_setup()
    _L0_attn_in = {k: v for k, v in _L0_attn_all.items() if k in ('Wq', 'bq', 'Wk', 'bk', 'Wv', 'bv', 'Wg', 'bg', 'input_bias', 'norm_scale')}
    del _L0_attn_all

    def _L0_ffn_setup():
        import jax, jax.numpy as jnp
        import numpy as np
        BN_EPS = 0.001

        def _bn(h, g, b, m, v):
            return g * (h - m) * jax.lax.rsqrt(v + BN_EPS) + b
        key = jax.random.key(seed)
        ks = jax.random.split(key, 8)
        B, F, Df = (64, 64, 64)
        E, H, D = (8, 64, 64)
        s1 = 1.0 / np.sqrt(Df)
        s2 = 1.0 / np.sqrt(H)
        return {'x': jax.random.normal(ks[0], (B, F, Df), jnp.float32), 'Wr': jax.random.normal(ks[1], (Df, E), jnp.float32) * s1, 'br': jnp.zeros((E,), jnp.float32), 'W1': jax.random.normal(ks[2], (E, Df, H), jnp.float32) * s1, 'b1': jnp.zeros((E, H), jnp.float32), 'g1': jnp.ones((E, H), jnp.float32), 'be1': jnp.zeros((E, H), jnp.float32), 'm1': jnp.zeros((E, H), jnp.float32), 'v1': jnp.ones((E, H), jnp.float32), 'W2': jax.random.normal(ks[3], (E, H, H), jnp.float32) * s2, 'b2': jnp.zeros((E, H), jnp.float32), 'g2': jnp.ones((E, H), jnp.float32), 'be2': jnp.zeros((E, H), jnp.float32), 'm2': jnp.zeros((E, H), jnp.float32), 'v2': jnp.ones((E, H), jnp.float32), 'Wo': jax.random.normal(ks[4], (E, H, D), jnp.float32) * s2, 'bo': jnp.zeros((E, D), jnp.float32)}
    _L0_ffn_all = _L0_ffn_setup()
    _L0_ffn_in = {k: v for k, v in _L0_ffn_all.items() if k in ('Wr', 'br', 'W1', 'b1', 'g1', 'be1', 'm1', 'v1', 'W2', 'b2', 'g2', 'be2', 'm2', 'v2', 'Wo', 'bo')}
    del _L0_ffn_all
    return {'x': x, 'L0_tok_W1': _L0_tok_in['W1'], 'L0_tok_b1': _L0_tok_in['b1'], 'L0_tok_W2': _L0_tok_in['W2'], 'L0_tok_b2': _L0_tok_in['b2'], 'L0_tok_W3': _L0_tok_in['W3'], 'L0_tok_b3': _L0_tok_in['b3'], 'L0_tok_W4': _L0_tok_in['W4'], 'L0_tok_b4': _L0_tok_in['b4'], 'L0_attn_Wq': _L0_attn_in['Wq'], 'L0_attn_bq': _L0_attn_in['bq'], 'L0_attn_Wk': _L0_attn_in['Wk'], 'L0_attn_bk': _L0_attn_in['bk'], 'L0_attn_Wv': _L0_attn_in['Wv'], 'L0_attn_bv': _L0_attn_in['bv'], 'L0_attn_Wg': _L0_attn_in['Wg'], 'L0_attn_bg': _L0_attn_in['bg'], 'L0_attn_input_bias': _L0_attn_in['input_bias'], 'L0_attn_norm_scale': _L0_attn_in['norm_scale'], 'L0_ffn_Wr': _L0_ffn_in['Wr'], 'L0_ffn_br': _L0_ffn_in['br'], 'L0_ffn_W1': _L0_ffn_in['W1'], 'L0_ffn_b1': _L0_ffn_in['b1'], 'L0_ffn_g1': _L0_ffn_in['g1'], 'L0_ffn_be1': _L0_ffn_in['be1'], 'L0_ffn_m1': _L0_ffn_in['m1'], 'L0_ffn_v1': _L0_ffn_in['v1'], 'L0_ffn_W2': _L0_ffn_in['W2'], 'L0_ffn_b2': _L0_ffn_in['b2'], 'L0_ffn_g2': _L0_ffn_in['g2'], 'L0_ffn_be2': _L0_ffn_in['be2'], 'L0_ffn_m2': _L0_ffn_in['m2'], 'L0_ffn_v2': _L0_ffn_in['v2'], 'L0_ffn_Wo': _L0_ffn_in['Wo'], 'L0_ffn_bo': _L0_ffn_in['bo']}

def reference(x, L0_tok_W1, L0_tok_b1, L0_tok_W2, L0_tok_b2, L0_tok_W3, L0_tok_b3, L0_tok_W4, L0_tok_b4, L0_attn_Wq, L0_attn_bq, L0_attn_Wk, L0_attn_bk, L0_attn_Wv, L0_attn_bv, L0_attn_Wg, L0_attn_bg, L0_attn_input_bias, L0_attn_norm_scale, L0_ffn_Wr, L0_ffn_br, L0_ffn_W1, L0_ffn_b1, L0_ffn_g1, L0_ffn_be1, L0_ffn_m1, L0_ffn_v1, L0_ffn_W2, L0_ffn_b2, L0_ffn_g2, L0_ffn_be2, L0_ffn_m2, L0_ffn_v2, L0_ffn_Wo, L0_ffn_bo):
    import jax
    import jax.numpy as jnp

    def _L0_tok_ref(x, W1, b1, W2, b2, W3, b3, W4, b4):
        import jax, jax.numpy as jnp
        import numpy as np
        T = 8
        a = jnp.einsum('bdl,od->blo', x, W1) + b1
        bs, L, d = a.shape
        zcol = jnp.zeros((bs, 1, d), a.dtype)
        shift_r = lambda v: jnp.concatenate([zcol, v[:, :-1]], axis=1)
        shift_l = lambda v: jnp.concatenate([v[:, 1:], zcol], axis=1)
        up = jnp.zeros_like(a)
        down = jnp.zeros_like(a)
        for _ in range(T):
            up = jax.nn.relu(a + shift_r(up) @ W2.T + b2)
            down = jax.nn.relu(a + shift_l(down) @ W2.T + b2)
        c = jnp.einsum('bdl,od->blo', x, W3) + b3
        miu = jax.nn.relu(c + (shift_r(up) @ W4.T + b4) + (shift_l(down) @ W4.T + b4))
        return miu

    def _L0_attn_ref(x, Wq, bq, Wk, bk, Wv, bv, Wg, bg, input_bias, norm_scale):
        import jax, jax.numpy as jnp
        import numpy as np

        def softcap(x, a=10.0):
            return a * jnp.tanh(x / a)
        B, T, D = x.shape
        inv_sqrt_d = 1.0 / jnp.sqrt(jnp.asarray(D, jnp.float32))
        q = x @ Wq + bq
        k = (x @ Wk + bk) * inv_sqrt_d
        v = x @ Wv + bv
        gates = x @ Wg + bg
        i_pre, f_pre, o_pre = jnp.split(gates, 3, axis=-1)
        log_i = softcap(i_pre + input_bias)
        log_f = -jax.nn.softplus(f_pre)

        def step(carry, inp):
            M, n, m = carry
            qt, kt, vt, li, lf, op = inp
            m_next = jnp.maximum(lf + m, li)
            i_s = jnp.exp(li - m_next)
            f_s = jnp.exp(lf + m - m_next)
            M = f_s[:, :, None] * M + i_s[:, :, None] * (vt[:, :, None] * kt[:, None, :])
            n = f_s * n + i_s * kt
            h_raw = jnp.einsum('bij,bj->bi', M, qt)
            denom = jnp.maximum(jnp.abs(jnp.einsum('bi,bi->b', n, qt))[:, None], 1e-06)
            h = jax.nn.sigmoid(op) * (h_raw / denom)
            return ((M, n, m_next), h)
        M0 = jnp.zeros((B, D, D), jnp.float32)
        n0 = jnp.zeros((B, D), jnp.float32)
        m0 = jnp.zeros((B, D), jnp.float32)
        xs = tuple((jnp.swapaxes(a, 0, 1) for a in (q, k, v, log_i, log_f, o_pre)))
        _, hs = jax.lax.scan(step, (M0, n0, m0), xs)
        out = jnp.swapaxes(hs, 0, 1)
        rms = jnp.sqrt(jnp.mean(out * out, axis=-1, keepdims=True) + 1e-08)
        return out / rms * norm_scale

    def _L0_ffn_ref(x, Wr, br, W1, b1, g1, be1, m1, v1, W2, b2, g2, be2, m2, v2, Wo, bo):
        import jax, jax.numpy as jnp
        import numpy as np
        BN_EPS = 0.001

        def _bn(h, g, b, m, v):
            return g * (h - m) * jax.lax.rsqrt(v + BN_EPS) + b
        feat = jnp.mean(x, axis=0)
        w = jax.nn.softmax(feat @ Wr + br, axis=-1)
        h = jnp.einsum('bfd,edh->bfeh', x, W1) + b1
        h = jax.nn.relu(_bn(h, g1, be1, m1, v1))
        h = jnp.einsum('bfeh,ehk->bfek', h, W2) + b2
        h = jax.nn.relu(_bn(h, g2, be2, m2, v2))
        y = jnp.einsum('bfeh,ehd->bfed', h, Wo) + bo
        return jnp.einsum('bfed,fe->bfd', y, w)
    h = _L0_tok_ref(x, L0_tok_W1, L0_tok_b1, L0_tok_W2, L0_tok_b2, L0_tok_W3, L0_tok_b3, L0_tok_W4, L0_tok_b4)
    h = h + _L0_attn_ref(_layernorm(h, axis=-1), L0_attn_Wq, L0_attn_bq, L0_attn_Wk, L0_attn_bk, L0_attn_Wv, L0_attn_bv, L0_attn_Wg, L0_attn_bg, L0_attn_input_bias, L0_attn_norm_scale)
    h = h + _L0_ffn_ref(_layernorm(h, axis=-1), L0_ffn_Wr, L0_ffn_br, L0_ffn_W1, L0_ffn_b1, L0_ffn_g1, L0_ffn_be1, L0_ffn_m1, L0_ffn_v1, L0_ffn_W2, L0_ffn_b2, L0_ffn_g2, L0_ffn_be2, L0_ffn_m2, L0_ffn_v2, L0_ffn_Wo, L0_ffn_bo)
    return h

_drawn_inputs = setup_inputs


def setup_inputs(seed=0):
    import zlib

    import numpy as np

    out = dict(_drawn_inputs(seed))
    spreads = {'L0_attn_bq': (0.0, 0.1),
     'L0_attn_bk': (0.0, 0.1),
     'L0_attn_bv': (0.0, 0.1),
     'L0_attn_bg': (0.0, 0.1),
     'L0_attn_input_bias': (-1.0, 0.6),
     'L0_attn_norm_scale': (1.0, 0.2),
     'L0_ffn_br': (0.0, 0.585),
     'L0_ffn_b1': (0.0, 0.402),
     'L0_ffn_g1': (1.0, 0.2),
     'L0_ffn_be1': (0.0, 0.339),
     'L0_ffn_m1': (0.0, 0.361),
     'L0_ffn_v1': (1.0, 0.6),
     'L0_ffn_b2': (0.0, 0.293),
     'L0_ffn_g2': (1.0, 0.2),
     'L0_ffn_be2': (0.0, 0.291),
     'L0_ffn_m2': (0.0, 0.273),
     'L0_ffn_v2': (1.0, 0.6),
     'L0_ffn_bo': (0.0, 0.1)}
    factors = {}
    for name, (base, spread) in spreads.items():
        noise = np.random.default_rng([zlib.crc32(name.encode()), seed]).standard_normal(out[name].shape)
        drawn = base * np.exp(spread * noise) if base else spread * noise
        out[name] = jnp.asarray(drawn.astype(out[name].dtype))
    for name, factor in factors.items():
        out[name] = (out[name] * factor).astype(out[name].dtype)
    return out
```

```python
from contextlib import ExitStack

import concourse.bass as bass
from concourse import mybir

F32 = mybir.dt.float32
ALU = mybir.AluOpType
ACT = mybir.ActivationFunctionType
AX_X = mybir.AxisListType.X

P = 128
D = 64
T = 256
NB = 64
GB = 8
SB = GB // 2
G = NB // GB
PC = SB * T
HC = PC // 2
C = 128
REF = 0.45
E = 8
EP = E // 2
UW = T + 1
FC = 512
NFC = NB // 2 * T // FC
TOK_EPS, RMS_EPS, BN_EPS = 1e-5, 1e-8, 1e-3
ROWS = ["tok_b1", "tok_b2", "tok_b3", "tok_b4", "bq", "bk", "bv", "bgi", "bgf", "bgo", "input_bias", "norm_scale"]
BN_ROWS = ["b1", "g1", "be1", "m1", "v1", "b2", "g2", "be2", "m2", "v2"]
NR = len(BN_ROWS) * EP + len(ROWS)


def build(nc, x, tok_W1, tok_b1, tok_W2, tok_b2, tok_W3, tok_b3, tok_W4, tok_b4, Wq, bq, Wk, bk, Wv, bv,
          Wg, bg, input_bias, norm_scale, Wr, br, W1, b1, g1, be1, m1, v1, W2, b2, g2, be2, m2, v2, Wo, bo, out):
    with ExitStack() as ctx:
        def sb(name, shape):
            return ctx.enter_context(nc.sbuf_tensor(name, shape, F32))

        def sem(name):
            return ctx.enter_context(nc.semaphore(name))

        ident = sb("ident", [P, P])
        mean_mat = sb("mean_mat", [P, P])
        center_mat = sb("center_mat", [P, P])
        sum_mat = sb("sum_mat", [P, P])
        causal = sb("causal", [P, 3 * C])
        rows = sb("rows", [NR, P])
        cols = sb("cols", [P, NR])
        wac = sb("wac", [4, P])
        w2_raw = sb("w2_raw", [P, P])
        w4_raw = sb("w4_raw", [D, P])
        w2T = sb("w2T", [P, P])
        w4T = sb("w4T", [P, D])
        wproj = sb("wproj", [P, 6, P])
        fw1 = sb("fw1", [P, 2, EP, P])
        fw2 = sb("fw2", [P, EP, P])
        fwo = sb("fwo", [P, EP, D])
        wr = sb("wr", [P, E])
        br_row = sb("br_row", [1, E])
        ones_row = sb("ones_row", [1, P])
        bo_w = sb("bo_w", [E, P])
        col2 = sb("col2", [P, 8])
        bn_s = sb("bn_s", [P, 2, EP])
        bn_t = sb("bn_t", [P, 2, EP])

        HH = sb("HH", [P, NB // 2 * T])
        XN2 = sb("XN2", [P, NB // 2 * T])
        feat = sb("feat", [P, T])
        decay_ends = sb("decay_ends", [P, G * GB])

        X = sb("X", [4, GB * T])
        A = sb("A", [P, GB * T])
        CT = sb("CT", [P, PC])
        Z = sb("Z", [P, GB * T])
        U = sb("U", [P, GB * UW])
        UF = sb("UF", [P, GB * UW])

        SQ = sb("SQ", [P, PC])
        XC = sb("XC", [P, PC])
        RS_FS = sb("RS_FS", [P, PC])
        LF = sb("LF", [P, PC])
        LI = sb("LI", [P, PC])
        K_NN = sb("K_NN", [P, PC])
        KZ = sb("KZ", [P, 2, PC])
        Q = sb("Q", [P, PC])
        V = sb("V", [P, PC])
        EO = sb("EO", [P, PC])
        M = sb("M", [P, SB * UW])
        IS_HR = sb("IS_HR", [P, PC])
        NC_ = sb("NC_", [P, PC])
        ND = sb("ND", [P, PC])
        UT = sb("UT", [P, PC])
        AT = sb("AT", [P, GB, 3 * C])
        lam = sb("lam", [P, GB])
        zeros = sb("zeros", [P, C])
        ones = sb("ones", [P, 1])
        side = sb("side", [P, 2])

        H1 = [A[:, 0:1024].rearrange("p (s c) -> p s c", s=2), A[:, 1024:2048].rearrange("p (s c) -> p s c", s=2)]
        H2 = [Z[:, 0:1024].rearrange("p (s c) -> p s c", s=2), Z[:, 1024:2048].rearrange("p (s c) -> p s c", s=2)]
        WM = AT[:, 0:4, 0:T]
        BOW = LF[:, 0:T]
        wb = K_NN[:, :].rearrange("p (t c) -> p t c", t=2)
        wn = M[:, 0:16].rearrange("p (t e) -> p t e", t=2)
        wx = M[:, 16:32].rearrange("p (t e) -> p t e", t=2)
        wmx, wsm, wrc = M[:, 32:34], M[:, 34:36], M[:, 36:38]
        wt = Q[0:E, 0:T]
        R1 = [SQ[:, 0:512], SQ[:, 512:1024]]
        RES = [XC[:, 0:512], XC[:, 512:1024]]
        OUTT = [V[:, 512 * f:512 * f + 512].rearrange("p (s n c) -> p s n c", s=2, n=2) for f in range(2)]

        TB = [ctx.enter_context(nc.psum_tensor(f"TB{j}", [P, 512], F32)) for j in range(4)]
        QB = [ctx.enter_context(nc.psum_tensor(f"QB{j}", [P, 512], F32)) for j in range(4)]

        U3 = U[:, :].rearrange("p (n c) -> p n c", c=UW)
        UF3 = UF[:, :].rearrange("p (n c) -> p n c", c=UW)
        A3 = A[:, :].rearrange("p (n c) -> p n c", c=T)
        Z3 = Z[:, :].rearrange("p (n c) -> p n c", c=T)
        M3 = M[:, :].rearrange("p (n c) -> p n c", c=UW)
        NC3 = NC_[:, :].rearrange("p (n c) -> p n c", c=C)
        ND3 = ND[:, :].rearrange("p (n c) -> p n c", c=C)
        HR3 = IS_HR[:, :].rearrange("p (n c) -> p n c", c=T)
        half = [slice(0, D), slice(D, P)]

        def hs(h):
            return slice(HC * h, HC * h + HC)

        def tc(j):
            return slice(512 * j, 512 * j + 512)

        def rowsof(ap, c=T):
            return ap.rearrange("p (n c) -> p n c", c=c)

        def hh(a, h):
            return HH[:, bass.ds(a * PC + HC * h, HC)]

        def xn2(a, h):
            return XN2[:, bass.ds(a * PC + HC * h, HC)]

        def col(name):
            i = len(BN_ROWS) * EP + ROWS.index(name)
            return cols[:, i:i + 1]

        def bn_cols(name):
            i = BN_ROWS.index(name) * EP
            return cols[:, i:i + EP]

        neg_bf, bias_i, neg_bo, a_bias, c_bias = (col2[:, i:i + 1] for i in range(5))

        mix_loaded = sem("mix_loaded")
        rows_loaded = sem("rows_loaded")
        bn_loaded = sem("bn_loaded")
        att_loaded = sem("att_loaded")
        ffn_loaded = sem("ffn_loaded")
        x_in = sem("x_in")
        w_cleared = sem("w_cleared")
        cleared = sem("cleared")
        id_ready = sem("id_ready")
        mask_ready = sem("mask_ready")
        mats = sem("mats")
        side_ready = sem("side_ready")
        setup_mm = sem("setup_mm")
        setup_out = sem("setup_out")
        derived = sem("derived")
        bn_ln = sem("bn_ln")
        bn_rs = sem("bn_rs")
        bn_ready = sem("bn_ready")
        s = {n: sem(n) for n in (
            "ac_mm", "a_out", "c_out", "mix_relu", "mix_mm", "mix_add", "uf_out", "fin_mm", "fin_add", "h1_out",
            "lnc_mm", "sq_out", "xc_out", "var_mm", "rs_ln", "rs_out", "xn_out",
            "proj_mm", "f_out", "i_out", "k_out", "q_out", "v_out", "o_out", "o1_out", "kz_out",
            "f_abs", "f_exp", "f_log", "lf_out", "li_a", "li_b", "li_out", "m_out", "t1_out", "lf2_out", "lg_out",
            "fs_out", "is_out", "nc_out", "nd_out", "ar_out", "et_out", "eu_out", "u_out", "lam_in", "lam_out",
            "ends_out", "ik_out", "nn_out", "nq_out", "den_mm", "den_out", "g_a", "g_b", "g_out",
            "at_mm", "at_out", "ut_mm", "ut_out", "av_mm", "tmp_out", "hr_a", "hr_out", "o_h",
            "sqo_out", "rms_mm", "rr_ln", "rr_out", "y_out", "h2_out",
            "l2c_mm", "sq2_out", "xc2_out", "var2_mm", "rs2_ln", "rs2_out", "xn2_out", "feat_out")}
        b = {n: sem("b_" + n) for n in (
            "lg_mm", "mx", "nmx", "ex", "rc", "wn", "wb", "w_mm", "w_out", "wt_mm", "wt_out", "bo_mm", "bo_out",
            "l1_mm", "h1", "l2_mm", "h2", "hw", "l3_mm", "res_a", "res", "tr_mm", "tr_out", "stored")}
        N_MIX, N_ATT, N_FFN, N_ROWS, N_BN = 6, 12, 11, 24, 10

        block = ctx.enter_context(nc.Block())

        @block.sync
        def _(sp):
            def load_x(g):
                return sp.dma_start(X[:, :].rearrange("d (b l) -> d b l", l=T),
                                    x[bass.ds(g * GB, GB)].rearrange("b d l -> d b l"))

            load_x(0).then_inc(x_in, 16)
            with nc.allow_non_contiguous_dma(reason="weights of 64 x 4"):
                sp.dma_start(wac[:, 0:D], tok_W1.rearrange("o d -> d o")).then_inc(mix_loaded, 16)
                sp.dma_start(wac[:, D:P], tok_W3.rearrange("o d -> d o")).then_inc(mix_loaded, 16)
            sp.wait_ge(w_cleared, 1)
            for h in range(2):
                sp.dma_start(w2_raw[half[h], D * h:D * h + D], tok_W2).then_inc(mix_loaded, 16)
                sp.dma_start(w4_raw[:, D * h:D * h + D], tok_W4).then_inc(mix_loaded, 16)
            for n, v in (("tok_b1", tok_b1), ("tok_b2", tok_b2), ("tok_b3", tok_b3), ("tok_b4", tok_b4), ("bq", bq),
                         ("bk", bk), ("bv", bv), ("bgi", bg[0:D]), ("bgf", bg[D:2 * D]), ("bgo", bg[2 * D:3 * D]),
                         ("input_bias", input_bias), ("norm_scale", norm_scale)):
                i = len(BN_ROWS) * EP + ROWS.index(n)
                for h in range(2):
                    sp.dma_start(rows[i:i + 1, D * h:D * h + D],
                                 v.rearrange("(a d) -> a d", a=1)).then_inc(rows_loaded, 16)

            with sp.Fori(1, G) as g:
                sp.wait_ge(s["ac_mm"], 4 * g)
                load_x(g).then_inc(x_in, 16)

            ov = out.rearrange("(g s f n) (p r) d -> g s f p n (r d)", g=G, s=2, f=2, n=2, r=2)
            with sp.Fori(0, G) as g:
                for f in range(2):
                    for k in range(2):
                        sp.wait_ge(b["tr_out"], 4 * g + 2 * f + k + 1)
                        sp.dma_start(ov[bass.ds(g, 1), k, f].rearrange("a p n c -> (a p) n c"),
                                     OUTT[f][:, k]).then_inc(b["stored"], 16)
            sp.wait_ge(b["stored"], 16 * 4 * G)

        @block.gpsimd
        def _(pool):
            nc.gpsimd.memset(w2_raw[:, :], 0.0).then_inc(w_cleared, 1)
            nc.gpsimd.memset(ident[:, :], 0.0).then_inc(id_ready, 1)
            pool.wait_ge(id_ready, 1)
            nc.gpsimd.affine_select(out=ident[:, :], in_=ident[:, :], compare_op=ALU.not_equal, fill=1.0, base=0,
                                    pattern=[[-1, P]], channel_multiplier=1).then_inc(id_ready, 1)
            nc.gpsimd.memset(wproj[:, :, :], 0.0).then_inc(w_cleared, 1)
            nc.gpsimd.memset(fw1[:, :, :, :], 0.0).then_inc(w_cleared, 1)
            nc.gpsimd.memset(fw2[:, :, :], 0.0).then_inc(w_cleared, 1)
            nc.gpsimd.memset(U3[:, :, 0:1], 0.0).then_inc(cleared, 1)
            nc.gpsimd.memset(UF[:, :], 0.0).then_inc(cleared, 1)
            nc.gpsimd.memset(M3[:, :, 0:1], 0.0).then_inc(cleared, 1)
            nc.gpsimd.memset(feat[:, :], 0.0).then_inc(cleared, 1)
            nc.gpsimd.memset(zeros[:, :], 0.0).then_inc(cleared, 1)
            nc.gpsimd.memset(ones_row[:, :], 1.0).then_inc(cleared, 1)
            nc.gpsimd.memset(ones[:, :], 1.0).then_inc(cleared, 1)
            nc.gpsimd.memset(causal[:, :], 1.0).then_inc(mask_ready, 1)
            pool.wait_ge(mask_ready, 1)
            for c in (0, 2):
                v = causal[:, C * c:C * c + C]
                nc.gpsimd.affine_select(out=v, in_=v, compare_op=ALU.is_ge, fill=0.0, base=0,
                                        pattern=[[1, C]], channel_multiplier=-1).then_inc(mask_ready, 1)
            pool.wait_ge(w_cleared, 4)
            for i, v in enumerate((b1, g1, be1, m1, v1, b2, g2, be2, m2, v2)):
                pool.dma_start(rows[i * EP:(i + 1) * EP, :],
                               v.rearrange("(p e) h -> p (e h)", e=2)).then_inc(bn_loaded, 16)
            w2v = W2.rearrange("(p two) h k -> two h p k", two=2)
            wov = Wo.rearrange("(p two) h d -> two h p d", two=2)
            for h in range(2):
                pool.dma_start(fw1[half[h], h, :, :].rearrange("d p (e h) -> d (p e) h", e=2),
                               W1.rearrange("e d h -> d e h")).then_inc(ffn_loaded, 16)
                pool.dma_start(fw2[half[h], :, D * h:D * h + D], w2v[h]).then_inc(ffn_loaded, 16)
                pool.dma_start(fwo[half[h], :, :], wov[h]).then_inc(ffn_loaded, 16)
                pool.dma_start(wr[half[h], :], Wr).then_inc(ffn_loaded, 16)
                pool.dma_start(bo_w[:, D * h:D * h + D], bo).then_inc(ffn_loaded, 16)
            pool.dma_start(br_row[:, :], br.rearrange("(a e) -> a e", a=1)).then_inc(ffn_loaded, 16)

            pool.wait_ge(cleared, 7)
            pool.wait_ge(side_ready, 4)

            def attention(a):
                pool.wait_ge(s["k_out"], 2 * a + 2)
                pool.wait_ge(s["at_mm"], GB * a)
                for k in range(2):
                    nc.gpsimd.tensor_tensor(KZ[:, k, :], K_NN[:, :], side[:, k:k + 1].to_broadcast([P, PC]), ALU.mult).then_inc(s["kz_out"], 1)
                pool.wait_ge(s["m_out"], SB * a + SB)
                nc.gpsimd.tensor_tensor(rowsof(LF[:, :]), rowsof(LF[:, :]), M3[:, :, 0:T], ALU.add)\
                    .then_inc(s["t1_out"], 1)
                nc.gpsimd.tensor_tensor(rowsof(LI[:, :]), rowsof(LI[:, :]), M3[:, :, 1:UW], ALU.subtract)\
                    .then_inc(s["lg_out"], 1)
                pool.wait_ge(s["t1_out"], a + 1)
                nc.gpsimd.tensor_tensor(rowsof(LF[:, :]), rowsof(LF[:, :]), M3[:, :, 1:UW], ALU.subtract)\
                    .then_inc(s["lf2_out"], 1)
                pool.wait_ge(s["o_out"], 2 * a + 2)
                nc.gpsimd.tensor_tensor(EO[:, :], EO[:, :], ones[:, :].to_broadcast([P, PC]), ALU.add).then_inc(s["o1_out"], 1)
                pool.wait_ge(s["is_out"], a + 1)
                nc.gpsimd.tensor_tensor(IS_HR[:, :], IS_HR[:, :], K_NN[:, :], ALU.mult).then_inc(s["ik_out"], 1)
                pool.wait_ge(s["nd_out"], a + 1)
                nc.gpsimd.tensor_tensor(LI[:, :], LI[:, :], ND[:, :], ALU.add).then_inc(s["ar_out"], 1)
                for h in range(2):
                    pool.wait_ge(s["eu_out"], a + 1)
                    pool.wait_ge(s["v_out"], 2 * a + h + 1)
                    nc.gpsimd.tensor_tensor(V[:, hs(h)], V[:, hs(h)], LI[:, hs(h)], ALU.mult)\
                        .then_inc(s["u_out"], 1)
                for h in range(2):
                    pool.wait_ge(s["nn_out"], SB * a + 2 * h + 2)
                    nc.gpsimd.tensor_tensor(K_NN[:, hs(h)], K_NN[:, hs(h)], Q[:, hs(h)], ALU.mult)\
                        .then_inc(s["nq_out"], 1)
                for h in range(2):
                    pool.wait_ge(s["rr_out"], 2 * a + h + 1)
                    nc.gpsimd.tensor_tensor(RS_FS[:, hs(h)], IS_HR[:, hs(h)], RS_FS[:, hs(h)], ALU.mult)\
                        .then_inc(s["y_out"], 1)
                for n in range(SB):
                    pool.wait_ge(s["xn2_out"], 2 * a + n // 2 + 1)
                    pool.wait_ge(s["feat_out"], SB * a + n)
                    nc.gpsimd.tensor_tensor(feat[:, :], feat[:, :], XN2[:, bass.ds(a * PC + T * n, T)], ALU.add)\
                        .then_inc(s["feat_out"], 1)

            attention(0)
            with pool.Fori(1, G) as a:
                attention(a)

            pool.wait_ge(b["bo_out"], 1)
            def residual(g):
                for f in range(2):
                    pool.wait_ge(b["res"], 2 * g)
                    nc.gpsimd.tensor_tensor(rowsof(R1[f]), rowsof(hh(g, f)),
                                            BOW.unsqueeze(1).to_broadcast([P, 2, T]), ALU.add).then_inc(b["res_a"], 1)

            residual(0)
            with pool.Fori(1, G) as g:
                residual(g)

        @block.scalar
        def _(act):
            act.wait_ge(w_cleared, 2)
            for i, w in enumerate((Wg[:, D:2 * D], Wg[:, 0:D], Wk, Wq, Wv, Wg[:, 2 * D:3 * D])):
                for h in range(2):
                    act.dma_start(wproj[half[h], i, D * h:D * h + D], w).then_inc(att_loaded, 16)
            act.wait_ge(setup_out, 3)
            for i, n in enumerate(("v1", "v2")):
                nc.scalar.activation(bn_s[:, i, :], bn_cols(n), ACT.Ln, bias=BN_EPS).then_inc(bn_ln, 1)
            act.wait_ge(bn_ln, 2)
            nc.scalar.activation(bn_s[:, :, :], bn_s[:, :, :], ACT.Exp, scale=-0.5).then_inc(bn_rs, 1)
            act.wait_ge(derived, 5)

            def relu(it, k, js):
                for i, j in enumerate(js):
                    act.wait_ge(s["mix_add"], 28 * it + 4 * k + i + 1)
                    nc.scalar.activation(U3[:, 2 * j:2 * j + 2, 1:UW], Z3[:, 2 * j:2 * j + 2, :], ACT.Relu)\
                        .then_inc(s["mix_relu"], 1)

            def turn(it, mix, att):
                a = it - 1
                if mix:
                    for j in range(4):
                        act.wait_ge(s["ac_mm"], 4 * it + j + 1)
                        nc.scalar.activation(A3[half[0], 2 * j:2 * j + 2, :], rowsof(TB[j][half[0], :]), ACT.Identity,
                                             bias=a_bias[half[0], :]).then_inc(s["a_out"], 1)
                        nc.scalar.activation(A3[half[1], 2 * j:2 * j + 2, ::-1], rowsof(TB[j][half[0], :]),
                                             ACT.Identity, bias=a_bias[half[0], :]).then_inc(s["a_out"], 1)
                    for j in range(4):
                        act.wait_ge(s["a_out"], 8 * it + 2 * j + 2)
                        nc.scalar.activation(U3[:, 2 * j:2 * j + 2, 1:UW], A3[:, 2 * j:2 * j + 2, :], ACT.Relu)\
                            .then_inc(s["mix_relu"], 1)
                if att:
                    for h in range(2):
                        act.wait_ge(s["lnc_mm"], 2 * a + h + 1)
                        nc.scalar.activation(SQ[:, hs(h)], QB[h][:, :], ACT.Square).then_inc(s["sq_out"], 1)
                if mix:
                    relu(it, 0, range(4))
                if att:
                    act.wait_ge(s["xn2_out"], 2 * a)
                    for h in range(2):
                        act.wait_ge(s["var_mm"], 2 * a + h + 1)
                        nc.scalar.activation(RS_FS[:, hs(h)], QB[2 + h][:, :], ACT.Ln, bias=TOK_EPS)\
                            .then_inc(s["rs_ln"], 1)
                    for h in range(2):
                        act.wait_ge(s["rs_ln"], 2 * a + h + 1)
                        nc.scalar.activation(RS_FS[:, hs(h)], RS_FS[:, hs(h)], ACT.Exp, scale=-0.5)\
                            .then_inc(s["rs_out"], 1)
                if mix:
                    relu(it, 1, range(4))
                if att:
                    for h in range(2):
                        act.wait_ge(s["proj_mm"], 12 * a + h + 1)
                        nc.scalar.activation(LF[:, hs(h)], QB[h][:, :], ACT.Identity, bias=neg_bf, scale=-1.0)\
                            .then_inc(s["f_out"], 1)
                    for h in range(2):
                        act.wait_ge(s["proj_mm"], 12 * a + 2 + h + 1)
                        nc.scalar.activation(LI[:, hs(h)], QB[2 + h][:, :], ACT.Exp, bias=bias_i, scale=0.2)\
                            .then_inc(s["i_out"], 1)
                    act.wait_ge(s["f_out"], 2 * a + 2)
                    nc.scalar.activation(SQ[:, :], LF[:, :], ACT.Abs).then_inc(s["f_abs"], 1)
                    act.wait_ge(s["f_abs"], a + 1)
                    nc.scalar.activation(SQ[:, :], SQ[:, :], ACT.Exp, scale=-1.0).then_inc(s["f_exp"], 1)
                    act.wait_ge(s["f_exp"], a + 1)
                    nc.scalar.activation(SQ[:, :], SQ[:, :], ACT.Ln, bias=1.0).then_inc(s["f_log"], 1)
                if mix:
                    relu(it, 2, range(4))
                if att:
                    for h in range(2):
                        act.wait_ge(s["proj_mm"], 12 * a + 8 + h + 1)
                        nc.scalar.activation(V[:, hs(h)], QB[h][:, :], ACT.Identity, bias=col("bv"))\
                            .then_inc(s["v_out"], 1)
                    for h in range(2):
                        act.wait_ge(s["proj_mm"], 12 * a + 10 + h + 1)
                        nc.scalar.activation(EO[:, hs(h)], QB[2 + h][:, :], ACT.Exp, bias=neg_bo, scale=-1.0)\
                            .then_inc(s["o_out"], 1)
                if mix:
                    relu(it, 3, range(4))
                if att:
                    act.wait_ge(s["lg_out"], a + 1)
                    nc.scalar.activation(IS_HR[:, :], LI[:, :], ACT.Exp).then_inc(s["is_out"], 1)
                    act.wait_ge(s["lf2_out"], a + 1)
                    nc.scalar.activation(RS_FS[:, :], LF[:, :], ACT.Exp).then_inc(s["fs_out"], 1)
                if mix:
                    relu(it, 4, range(4))
                if att:
                    act.wait_ge(s["ar_out"], a + 1)
                    nc.scalar.activation(LI[:, :], LI[:, :], ACT.Exp).then_inc(s["eu_out"], 1)
                    nc.scalar.activation(ND[:, :], ND[:, :], ACT.Exp, scale=-1.0).then_inc(s["et_out"], 1)
                    act.wait_ge(s["lam_in"], 2 * a + 2)
                    nc.scalar.activation(lam[:, :], lam[:, :], ACT.Exp).then_inc(s["lam_out"], 1)
                if mix:
                    relu(it, 5, range(4))
                if att:
                    for h in range(2):
                        act.wait_ge(s["ut_mm"], 2 * a + h + 1)
                        nc.scalar.activation(UT[:, hs(h)], QB[2 + h][:, :], ACT.Identity).then_inc(s["ut_out"], 1)
                    for h in range(2):
                        act.wait_ge(s["den_mm"], 2 * a + h + 1)
                        nc.scalar.activation(K_NN[:, hs(h)], QB[h][:, :], ACT.Abs).then_inc(s["den_out"], 1)
                if mix:
                    for i, j in enumerate((0, 2, 1, 3)):
                        act.wait_ge(s["mix_add"], 28 * it + 24 + i + 1)
                        nc.scalar.activation(UF3[half[0], 2 * j:2 * j + 2, 1:T], Z3[half[0], 2 * j:2 * j + 2, 0:T - 1],
                                             ACT.Relu).then_inc(s["uf_out"], 1)
                        nc.scalar.activation(UF3[half[1], 2 * j:2 * j + 2, 0:T - 1],
                                             Z3[half[1], 2 * j:2 * j + 2, T - 2::-1],
                                             ACT.Relu).then_inc(s["uf_out"], 1)
                if att:
                    act.wait_ge(s["lam_out"], a + 1)
                    for n in range(SB):
                        act.wait_ge(s["av_mm"], SB * a + n + 1)
                        nc.scalar.activation(SQ[:, C * n:C * n + C], QB[n][:, C:2 * C], ACT.Identity,
                                             scale=lam[:, 2 * n:2 * n + 1]).then_inc(s["tmp_out"], 1)
                if mix:
                    for h in range(2):
                        act.wait_ge(s["fin_add"], 2 * it + h + 1)
                        nc.scalar.activation(hh(it, h), Z[:, hs(h)], ACT.Relu, bias=c_bias).then_inc(s["h1_out"], 1)
                if att:
                    for h in range(2):
                        act.wait_ge(s["o_h"], 2 * a + h + 1)
                        nc.scalar.activation(SQ[:, hs(h)], IS_HR[:, hs(h)], ACT.Square).then_inc(s["sqo_out"], 1)
                    for h in range(2):
                        act.wait_ge(s["rms_mm"], 2 * a + h + 1)
                        nc.scalar.activation(RS_FS[:, hs(h)], QB[h][:, :], ACT.Ln, bias=RMS_EPS)\
                            .then_inc(s["rr_ln"], 1)
                    for h in range(2):
                        act.wait_ge(s["rr_ln"], 2 * a + h + 1)
                        nc.scalar.activation(RS_FS[:, hs(h)], RS_FS[:, hs(h)], ACT.Exp, scale=-0.5)\
                            .then_inc(s["rr_out"], 1)
                    for h in range(2):
                        act.wait_ge(s["l2c_mm"], 2 * a + h + 1)
                        nc.scalar.activation(SQ[:, hs(h)], QB[2 + h][:, :], ACT.Square).then_inc(s["sq2_out"], 1)
                    for h in range(2):
                        act.wait_ge(s["var2_mm"], 2 * a + h + 1)
                        nc.scalar.activation(RS_FS[:, hs(h)], QB[h][:, :], ACT.Ln, bias=TOK_EPS)\
                            .then_inc(s["rs2_ln"], 1)
                    for h in range(2):
                        act.wait_ge(s["rs2_ln"], 2 * a + h + 1)
                        nc.scalar.activation(RS_FS[:, hs(h)], RS_FS[:, hs(h)], ACT.Exp, scale=-0.5)\
                            .then_inc(s["rs2_out"], 1)

            turn(0, True, False)
            turn(1, True, True)
            with act.Fori(2, G) as it:
                turn(it, True, True)
            turn(G, False, True)

            for t in range(2):
                act.wait_ge(b["nmx"], 1)
                nc.scalar.activation(wx[:, t, :], QB[t][:, 0:E], ACT.Exp, bias=wmx[:, t:t + 1],
                                     accum_out=wsm[:, t:t + 1]).then_inc(b["ex"], 1)
            act.wait_ge(bn_ready, 7)

            def h1(g, t):
                for k in range(2):
                    act.wait_ge(b["l1_mm"], 16 * g + 2 * t + k + 1)
                    nc.scalar.activation(H1[t % 2][:, k, :], TB[k][:, :], ACT.Relu, bias=bn_t[:, 0, t % EP:t % EP + 1],
                                         scale=bn_s[:, 0, t % EP:t % EP + 1]).then_inc(b["h1"], 1)

            def h2(g, t):
                for k in range(2):
                    act.wait_ge(b["l2_mm"], 16 * g + 2 * t + k + 1)
                    nc.scalar.activation(H2[t % 2][:, k, :], TB[2 + k][:, :], ACT.Relu,
                                         bias=bn_t[:, 1, t % EP:t % EP + 1],
                                         scale=bn_s[:, 1, t % EP:t % EP + 1]).then_inc(b["h2"], 1)

            def experts(g):
                for t in range(2 * EP + 1):
                    if t < 2 * EP:
                        h1(g, t)
                    if t >= 1:
                        h2(g, t - 1)

            experts(0)
            with act.Fori(1, G) as g:
                experts(g)

        @block.tensor
        def _(pe):
            pe.wait_ge(id_ready, 2)
            pe.wait_ge(mix_loaded, 16 * N_MIX)
            pe.transpose(TB[0][:, 0:P], w2_raw[:, :], ident[:, :]).then_inc(setup_mm, 1)
            pe.transpose(TB[1][:, 0:D], w4_raw[:, :], ident[0:D, 0:D]).then_inc(setup_mm, 1)
            pe.wait_ge(rows_loaded, 16 * N_ROWS)
            pe.wait_ge(bn_loaded, 16 * N_BN)
            pe.transpose(TB[2][:, 0:NR], rows[:, :], ident[0:NR, 0:NR]).then_inc(setup_mm, 1)
            pe.wait_ge(setup_out, 3)
            pe.wait_ge(cleared, 7)
            pe.wait_ge(mats, 9)
            pe.wait_ge(att_loaded, 16 * N_ATT)

            def layer(it, k, js):
                for i, j in enumerate(js):
                    pe.wait_ge(s["mix_relu"], 28 * it + 4 * k + j + 1)
                    if k == 0:
                        pe.wait_ge(s["c_out"], 4 * it + j + 1)
                    pe.matmul(TB[j][:, :], w2T[:, :], U3[:, 2 * j:2 * j + 2, 0:T], start=True, stop=True)\
                        .then_inc(s["mix_mm"], 1)

            def project(a, p):
                freed = ("xc_out", "rs_ln", "f_out", "i_out", "k_out", "q_out")[p]
                for h in range(2):
                    if p == 0:
                        pe.wait_ge(s["xn_out"], 2 * a + h + 1)
                    pe.wait_ge(s[freed], 2 * a + h + 1)
                    pe.matmul(QB[(2 * p + h) % 4][:, :], wproj[:, p, :], XC[:, hs(h)], start=True, stop=True)\
                        .then_inc(s["proj_mm"], 1)

            def scores(a, bs):
                for bb in bs:
                    k, n = bb // SB, bb % SB
                    if bb == 0:
                        pe.wait_ge(s["kz_out"], 2 * a + 2)
                        pe.wait_ge(s["q_out"], 2 * a + 2)
                    if bb < 2:
                        pe.wait_ge(s["v_out"], 2 * a + bb + 1)
                    elif bb < 4:
                        pe.wait_ge(s["o_out"], 2 * a + bb - 1)
                    else:
                        pe.wait_ge(s["at_out"], GB * a + bb - 3)
                    pe.matmul(QB[bb % 4][:, 0:T], KZ[:, k, T * n:T * n + C], Q[:, T * n:T * n + T],
                              start=True, stop=True)
                    pe.matmul(QB[bb % 4][:, T:T + C], KZ[:, k, T * n + C:T * n + T], Q[:, T * n + C:T * n + T],
                              start=True, stop=True).then_inc(s["at_mm"], 1)

            def turn(it, mix, att):
                a = it - 1
                if mix:
                    pe.wait_ge(x_in, 16 * it + 16)
                    pe.wait_ge(s["fin_add"], 2 * it)
                    pe.wait_ge(s["mix_add"], 28 * it)
                    for j in range(4):
                        pe.matmul(TB[j][:, :], wac[:, :], X[:, tc(j)], start=True, stop=True)\
                            .then_inc(s["ac_mm"], 1)
                if att:
                    pe.wait_ge(s["rs2_ln"], 2 * a)
                    for h in range(2):
                        pe.wait_ge(s["h1_out"], 2 * a + h + 1)
                        pe.matmul(QB[h][:, :], center_mat[:, :], hh(a, h), start=True, stop=True)\
                            .then_inc(s["lnc_mm"], 1)
                if mix:
                    layer(it, 0, range(4))
                if att:
                    pe.wait_ge(s["xc2_out"], 2 * a)
                    for h in range(2):
                        pe.wait_ge(s["sq_out"], 2 * a + h + 1)
                        pe.matmul(QB[2 + h][:, :], mean_mat[:, :], SQ[:, hs(h)], start=True, stop=True)\
                            .then_inc(s["var_mm"], 1)
                if mix:
                    layer(it, 1, range(4))
                if att:
                    for p in range(4):
                        project(a, p)
                if mix:
                    layer(it, 2, range(4))
                if att:
                    for p in range(4, 6):
                        project(a, p)
                    scores(a, range(0, 4))
                if mix:
                    layer(it, 3, range(4))
                if att:
                    scores(a, range(4, 8))
                if mix:
                    layer(it, 4, range(4))
                    layer(it, 5, range(4))
                if att:
                    for h in range(2):
                        pe.wait_ge(s["u_out"], 2 * a + h + 1)
                        pe.wait_ge(s["at_out"], GB * a + 6 + h + 1)
                        for c in range(4):
                            mm = pe.transpose(QB[2 + h][:, C * c:C * c + C], V[:, HC * h + C * c:HC * h + C * c + C],
                                              ident[:, :])
                        mm.then_inc(s["ut_mm"], 1)
                    for h in range(2):
                        pe.wait_ge(s["nq_out"], 2 * a + h + 1)
                        pe.wait_ge(s["at_out"], GB * a + 4 + h + 1)
                        pe.matmul(QB[h][:, :], sum_mat[:, :], K_NN[:, hs(h)], start=True, stop=True)\
                            .then_inc(s["den_mm"], 1)
                if mix:
                    layer(it, 6, (0, 2, 1, 3))
                if att:
                    pe.wait_ge(s["at_out"], GB * a + GB)
                    for n in range(SB):
                        pe.wait_ge(s["ut_out"], 2 * a + n // 2 + 1)
                        if n < 2:
                            pe.wait_ge(s["den_out"], 2 * a + n + 1)
                        else:
                            pe.wait_ge(s["ut_out"], 2 * a + n - 1)
                        for c, w in ((0, T), (1, C)):
                            for k in range(2):
                                mm = pe.matmul(QB[n][half[k], T * c:T * c + w],
                                               UT[:, C * (2 * n + c) + D * k:C * (2 * n + c) + D * k + D],
                                               AT[:, SB * k + n, T * c:T * c + w], start=True, stop=True)
                        mm.then_inc(s["av_mm"], 1)
                if mix:
                    for h in range(2):
                        pe.wait_ge(s["uf_out"], 8 * it + 4 * h + 4)
                        for k in range(2):
                            n = SB * k + 2 * h
                            mm = pe.matmul(TB[h][half[k], :], w4T[:, :], UF3[:, n:n + 2, 0:T], start=True, stop=True)
                        mm.then_inc(s["fin_mm"], 1)
                if att:
                    pe.wait_ge(s["hr_out"], SB * a + SB)
                    for h in range(2):
                        pe.wait_ge(s["sqo_out"], 2 * a + h + 1)
                        pe.matmul(QB[h][:, :], mean_mat[:, :], SQ[:, hs(h)], start=True, stop=True)\
                            .then_inc(s["rms_mm"], 1)
                    for h in range(2):
                        pe.wait_ge(s["h2_out"], 2 * a + h + 1)
                        pe.matmul(QB[2 + h][:, :], center_mat[:, :], hh(a, h), start=True, stop=True)\
                            .then_inc(s["l2c_mm"], 1)
                    for h in range(2):
                        pe.wait_ge(s["sq2_out"], 2 * a + h + 1)
                        pe.wait_ge(s["rr_ln"], 2 * a + h + 1)
                        pe.matmul(QB[h][:, :], mean_mat[:, :], SQ[:, hs(h)], start=True, stop=True)\
                            .then_inc(s["var2_mm"], 1)

            turn(0, True, False)
            turn(1, True, True)
            with pe.Fori(2, G) as it:
                turn(it, True, True)
            turn(G, False, True)

            pe.wait_ge(ffn_loaded, 16 * N_FFN)
            pe.wait_ge(s["feat_out"], SB * G)
            pe.wait_ge(bn_ready, 8)
            pe.wait_ge(s["rs2_ln"], 2 * G)
            for t in range(2):
                pe.matmul(QB[t][:, 0:E], feat[:, P * t:P * t + P], wr[:, :], start=True, stop=False)
                pe.matmul(QB[t][:, 0:E], ones_row[:, :], br_row[:, :], start=False, stop=True)\
                    .then_inc(b["lg_mm"], 1)
            for t in range(2):
                pe.wait_ge(b["wb"], t + 1)
                for p in range(EP):
                    mm = pe.matmul(TB[p][:, P * t:P * t + P], wb[:, t, P * p:P * p + P], ident[:, :],
                                   start=True, stop=True)
            mm.then_inc(b["w_mm"], 1)
            for t in range(2):
                mm = pe.transpose(QB[2][0:E, P * t:P * t + P], wn[:, t, :], ident[:, :])
            mm.then_inc(b["wt_mm"], 1)
            pe.wait_ge(b["wt_out"], 1)
            pe.matmul(QB[3][:, 0:T], bo_w[:, :], wt, start=True, stop=True).then_inc(b["bo_mm"], 1)
            pe.wait_ge(b["w_out"], EP)
            pe.wait_ge(b["bo_out"], 1)

            def l1(g, t):
                for k in range(2):
                    pe.wait_ge(b["h1"], 16 * g + 2 * t)
                    pe.matmul(TB[k][:, :], fw1[:, k, t % EP, :], xn2(g, t // EP), start=True, stop=True)\
                        .then_inc(b["l1_mm"], 1)

            def l2(g, t):
                for k in range(2):
                    pe.wait_ge(b["h1"], 16 * g + 2 * t + k + 1)
                    pe.wait_ge(b["h2"], 16 * g + 2 * t)
                    pe.matmul(TB[2 + k][:, :], fw2[:, t % EP, :], H1[t % 2][:, k, :], start=True, stop=True)\
                        .then_inc(b["l2_mm"], 1)

            def l3(g, t):
                f, p = t // EP, t % EP
                pe.wait_ge(b["res"], 2 * g)
                pe.wait_ge(b["hw"], 16 * g + 2 * t + 2)
                for k in range(2):
                    mm = pe.matmul(QB[f][half[k], :], fwo[:, p, :], H2[t % 2][:, k, :],
                                   start=(p == 0), stop=(p == EP - 1))
                if p == EP - 1:
                    mm.then_inc(b["l3_mm"], 1)

            def turn_out(g, f):
                pe.wait_ge(b["res"], 2 * g + f + 1)
                pe.wait_ge(b["tr_out"], 4 * g)
                for n in range(2):
                    for r in range(2):
                        mm = pe.transpose(QB[2 + f][:, P * (2 * n + r):P * (2 * n + r) + P],
                                          RES[f][:, T * n + r:T * n + T:2], ident[:, :])
                mm.then_inc(b["tr_mm"], 1)

            def experts(g):
                for t in range(2 * EP + 2):
                    if t < 2 * EP:
                        l1(g, t)
                    if 1 <= t <= 2 * EP:
                        l2(g, t - 1)
                    if t >= 2:
                        l3(g, t - 2)
                    if t == EP + 3:
                        turn_out(g, 0)
                turn_out(g, 1)

            experts(0)
            with pe.Fori(1, G) as g:
                experts(g)

        @block.vector
        def _(dve):
            for k in range(2):
                for h in range(2):
                    nc.vector.memset(side[half[h], k:k + 1], float(h == k)).then_inc(side_ready, 1)
            for m, v in ((mean_mat, 1.0 / D), (sum_mat, 1.0)):
                for h in range(2):
                    nc.vector.memset(m[half[h], D * h:D * h + D], v).then_inc(mats, 1)
                    nc.vector.memset(m[half[h], D * (1 - h):D * (1 - h) + D], 0.0).then_inc(mats, 1)
            dve.wait_ge(mats, 8)
            dve.wait_ge(id_ready, 2)
            nc.vector.tensor_tensor(center_mat[:, :], ident[:, :], mean_mat[:, :], ALU.subtract).then_inc(mats, 1)
            for i, (dst, src) in enumerate(((w2T[:, :], TB[0][:, 0:P]), (w4T[:, :], TB[1][:, 0:D]),
                                            (cols[:, :], TB[2][:, 0:NR]))):
                dve.wait_ge(setup_mm, i + 1)
                nc.vector.tensor_copy(dst, src).then_inc(setup_out, 1)
            dve.wait_ge(setup_out, 3)
            nc.vector.tensor_scalar(neg_bf, col("bgf"), -1.0, None, ALU.mult).then_inc(derived, 1)
            nc.vector.tensor_scalar(bias_i, col("bgi"), col("input_bias"), 0.2, ALU.add, ALU.mult).then_inc(derived, 1)
            nc.vector.tensor_scalar(neg_bo, col("bgo"), -1.0, None, ALU.mult).then_inc(derived, 1)
            nc.vector.tensor_tensor(a_bias, col("tok_b1"), col("tok_b2"), ALU.add).then_inc(derived, 1)
            nc.vector.scalar_tensor_tensor(out=c_bias, in0=col("tok_b4"), scalar=2.0, in1=col("tok_b3"),
                                           op0=ALU.mult, op1=ALU.add).then_inc(derived, 1)
            dve.wait_ge(bn_rs, 1)
            for i, (gn, bn, mn) in enumerate((("g1", "b1", "m1"), ("g2", "b2", "m2"))):
                nc.vector.tensor_tensor(bn_s[:, i, :], bn_s[:, i, :], bn_cols(gn), ALU.mult).then_inc(bn_ready, 1)
                nc.vector.tensor_tensor(bn_t[:, i, :], bn_cols(bn), bn_cols(mn), ALU.subtract).then_inc(bn_ready, 1)
            dve.wait_ge(bn_ready, 4)
            nc.vector.tensor_tensor(bn_t[:, :, :], bn_t[:, :, :], bn_s[:, :, :], ALU.mult).then_inc(bn_ready, 1)
            dve.wait_ge(bn_ready, 5)
            for i, ben in enumerate(("be1", "be2")):
                nc.vector.tensor_tensor(bn_t[:, i, :], bn_t[:, i, :], bn_cols(ben), ALU.add).then_inc(bn_ready, 1)
            dve.wait_ge(ffn_loaded, 16 * N_FFN)
            nc.vector.tensor_scalar(wr[:, :], wr[:, :], 1.0 / NB, None, ALU.mult).then_inc(bn_ready, 1)
            dve.wait_ge(cleared, 7)
            dve.wait_ge(mask_ready, 3)

            def add(it, k, js):
                for i, j in enumerate(js):
                    dve.wait_ge(s["mix_mm"], 28 * it + 4 * k + i + 1)
                    nc.vector.tensor_tensor(Z[:, tc(j)], TB[j][:, :], A[:, tc(j)], ALU.add).then_inc(s["mix_add"], 1)

            def scores(a, bs):
                for bb in bs:
                    dve.wait_ge(s["at_mm"], GB * a + bb + 1)
                    nc.vector.tensor_tensor(AT[:, bb, :], QB[bb % 4][:, 0:3 * C], causal[:, :], ALU.mult)\
                        .then_inc(s["at_out"], 1)

            def turn(it, mix, att):
                a = it - 1
                if mix:
                    dve.wait_ge(s["fin_add"], 2 * it)
                    for j in range(4):
                        dve.wait_ge(s["ac_mm"], 4 * it + j + 1)
                        nc.vector.tensor_copy(CT[half[j // 2], 512 * (j % 2):512 * (j % 2) + 512], TB[j][half[1], :])\
                            .then_inc(s["c_out"], 1)
                if att:
                    dve.wait_ge(s["xn2_out"], 2 * a)
                    for h in range(2):
                        dve.wait_ge(s["sq_out"], 2 * a + h + 1)
                        nc.vector.tensor_copy(XC[:, hs(h)], QB[h][:, :]).then_inc(s["xc_out"], 1)
                if mix:
                    add(it, 0, range(4))
                if att:
                    for h in range(2):
                        dve.wait_ge(s["xc_out"], 2 * a + h + 1)
                        dve.wait_ge(s["rs_out"], 2 * a + h + 1)
                        nc.vector.tensor_tensor(XC[:, hs(h)], XC[:, hs(h)], RS_FS[:, hs(h)], ALU.mult)\
                            .then_inc(s["xn_out"], 1)
                if mix:
                    add(it, 1, range(4))
                if att:
                    for h in range(2):
                        dve.wait_ge(s["proj_mm"], 12 * a + 4 + h + 1)
                        nc.vector.tensor_scalar(K_NN[:, hs(h)], QB[h][:, :], col("bk"), 1.0 / 8.0, ALU.add, ALU.mult)\
                            .then_inc(s["k_out"], 1)
                    for h in range(2):
                        dve.wait_ge(s["proj_mm"], 12 * a + 6 + h + 1)
                        nc.vector.tensor_scalar(Q[:, hs(h)], QB[2 + h][:, :], col("bq"), None, ALU.add)\
                            .then_inc(s["q_out"], 1)
                if mix:
                    add(it, 2, range(4))
                if att:
                    dve.wait_ge(s["i_out"], 2 * a + 2)
                    nc.vector.tensor_scalar(LI[:, :], LI[:, :], 1.0, None, ALU.add).then_inc(s["li_a"], 1)
                    dve.wait_ge(s["li_a"], a + 1)
                    nc.vector.reciprocal(LI[:, :], LI[:, :]).then_inc(s["li_b"], 1)
                    dve.wait_ge(s["f_log"], a + 1)
                    nc.vector.scalar_tensor_tensor(out=LF[:, :], in0=LF[:, :], scalar=0.0, in1=SQ[:, :],
                                                   op0=ALU.min, op1=ALU.subtract).then_inc(s["lf_out"], 1)
                    dve.wait_ge(s["li_b"], a + 1)
                    nc.vector.tensor_scalar(LI[:, :], LI[:, :], -20.0, 10.0, ALU.mult, ALU.add)\
                        .then_inc(s["li_out"], 1)
                    dve.wait_ge(s["lf_out"], a + 1)
                    dve.wait_ge(s["li_out"], a + 1)
                    for n in range(SB):
                        nc.vector.tensor_tensor_scan(M3[:, n, 1:UW], LF[:, T * n:T * n + T], LI[:, T * n:T * n + T],
                                                     0.0, ALU.add, ALU.max).then_inc(s["m_out"], 1)
                if mix:
                    add(it, 3, range(4))
                if att:
                    scores(a, range(0, 4))
                    dve.wait_ge(s["lf2_out"], a + 1)
                    for n in ("nd_out", "ends_out", "g_out"):
                        dve.wait_ge(s[n], a)
                    dve.wait_ge(s["lam_in"], 2 * a)
                    for c in range(GB):
                        nc.vector.tensor_tensor_scan(NC_[:, C * c:C * c + C], LF[:, C * c:C * c + C], zeros[:, :],
                                                     0.0, ALU.add, ALU.min).then_inc(s["nc_out"], 1)
                    dve.wait_ge(s["nc_out"], GB * a + GB)
                    nc.vector.scalar_tensor_tensor(out=ND3, in0=NC3[:, :, C - 1:C].to_broadcast([P, GB, C]), scalar=REF,
                                                   in1=NC3, op0=ALU.mult, op1=ALU.subtract).then_inc(s["nd_out"], 1)
                    nc.vector.tensor_scalar(lam[:, 0:GB:2].unsqueeze(2), NC3[:, 0:GB:2, C - 1:C], 1.0 - REF, None,
                                            ALU.mult).then_inc(s["lam_in"], 1)
                    nc.vector.tensor_scalar(lam[:, 1:GB:2].unsqueeze(2), NC3[:, 1:GB:2, C - 1:C], REF, None,
                                            ALU.mult).then_inc(s["lam_in"], 1)
                    nc.vector.tensor_copy(decay_ends[:, bass.ds(a * GB, GB)].unsqueeze(2), NC3[:, :, C - 1:C])\
                        .then_inc(s["ends_out"], 1)
                if mix:
                    add(it, 4, range(4))
                if att:
                    scores(a, range(4, 8))
                    dve.wait_ge(s["fs_out"], a + 1)
                    dve.wait_ge(s["ik_out"], a + 1)
                    dve.wait_ge(s["kz_out"], 2 * a + 2)
                    for n in range(SB):
                        r = slice(T * n, T * n + T)
                        nc.vector.tensor_tensor_scan(K_NN[:, r], RS_FS[:, r], IS_HR[:, r], 0.0, ALU.mult, ALU.add)\
                            .then_inc(s["nn_out"], 1)
                if mix:
                    add(it, 5, range(4))
                if att:
                    dve.wait_ge(s["den_out"], 2 * a + 2)
                    dve.wait_ge(s["o1_out"], a + 1)
                    nc.vector.scalar_tensor_tensor(out=EO[:, :], in0=K_NN[:, :], scalar=1e-6, in1=EO[:, :],
                                                   op0=ALU.max, op1=ALU.mult).then_inc(s["g_a"], 1)
                if mix:
                    add(it, 6, (0, 2, 1, 3))
                if att:
                    dve.wait_ge(s["g_a"], a + 1)
                    nc.vector.reciprocal(EO[:, :], EO[:, :]).then_inc(s["g_b"], 1)
                    dve.wait_ge(s["g_b"], a + 1)
                    dve.wait_ge(s["et_out"], a + 1)
                    nc.vector.tensor_tensor(EO[:, :], EO[:, :], ND[:, :], ALU.mult).then_inc(s["g_out"], 1)
                    dve.wait_ge(s["nn_out"], SB * a + SB)
                    for n in range(SB):
                        dve.wait_ge(s["tmp_out"], SB * a + n + 1)
                        nc.vector.scalar_tensor_tensor(out=HR3[:, n, C:T], in0=SQ[:, C * n:C * n + C],
                                                       scalar=lam[:, 2 * n + 1:2 * n + 2], in1=QB[n][:, T:T + C],
                                                       op0=ALU.mult, op1=ALU.add)\
                            .then_inc(s["hr_a"], 1)
                        nc.vector.tensor_copy(HR3[:, n, 0:C], QB[n][:, 0:C]).then_inc(s["hr_out"], 1)
                    dve.wait_ge(s["g_out"], a + 1)
                    for h in range(2):
                        dve.wait_ge(s["hr_out"], SB * a + 2 * h + 2)
                        dve.wait_ge(s["hr_a"], SB * a + 2 * h + 2)
                        nc.vector.tensor_tensor(IS_HR[:, hs(h)], IS_HR[:, hs(h)], EO[:, hs(h)], ALU.mult)\
                            .then_inc(s["o_h"], 1)
                if mix:
                    for h in range(2):
                        dve.wait_ge(s["fin_mm"], 2 * it + h + 1)
                        nc.vector.tensor_tensor(Z[:, hs(h)], TB[h][:, :], CT[:, hs(h)], ALU.add)\
                            .then_inc(s["fin_add"], 1)
                if att:
                    for h in range(2):
                        dve.wait_ge(s["y_out"], 2 * a + h + 1)
                        nc.vector.scalar_tensor_tensor(out=hh(a, h), in0=RS_FS[:, hs(h)], scalar=col("norm_scale"),
                                                       in1=hh(a, h), op0=ALU.mult, op1=ALU.add)\
                            .then_inc(s["h2_out"], 1)
                    for h in range(2):
                        dve.wait_ge(s["sq2_out"], 2 * a + h + 1)
                        nc.vector.tensor_copy(XC[:, hs(h)], QB[2 + h][:, :]).then_inc(s["xc2_out"], 1)
                    for h in range(2):
                        dve.wait_ge(s["xc2_out"], 2 * a + h + 1)
                        dve.wait_ge(s["rs2_out"], 2 * a + h + 1)
                        nc.vector.tensor_tensor(xn2(a, h), XC[:, hs(h)], RS_FS[:, hs(h)], ALU.mult)\
                            .then_inc(s["xn2_out"], 1)

            turn(0, True, False)
            turn(1, True, True)
            with dve.Fori(2, G) as it:
                turn(it, True, True)
            turn(G, False, True)

            for t in range(2):
                dve.wait_ge(b["lg_mm"], t + 1)
                nc.vector.tensor_reduce(wmx[:, t:t + 1], QB[t][:, 0:E], AX_X, ALU.max).then_inc(b["mx"], 1)
            dve.wait_ge(b["mx"], 2)
            nc.vector.tensor_scalar(wmx, wmx, -1.0, None, ALU.mult).then_inc(b["nmx"], 1)
            dve.wait_ge(b["ex"], 2)
            nc.vector.reciprocal(wrc, wsm).then_inc(b["rc"], 1)
            dve.wait_ge(b["rc"], 1)
            for t in range(2):
                nc.vector.tensor_scalar(wn[:, t, :], wx[:, t, :], wrc[:, t:t + 1], None, ALU.mult)\
                    .then_inc(b["wn"], 1)
            for t in range(2):
                dve.wait_ge(b["wn"], t + 1)
                nc.vector.tensor_copy(wb[:, t, :].rearrange("p (e c) -> p e c", c=D),
                                      wn[:, t, :].unsqueeze(2).to_broadcast([P, E, D])).then_inc(b["wb"], 1)
            dve.wait_ge(b["w_mm"], 1)
            for p in range(EP):
                nc.vector.tensor_copy(WM[:, p, :], TB[p][:, 0:T]).then_inc(b["w_out"], 1)
            dve.wait_ge(b["wt_mm"], 1)
            nc.vector.tensor_copy(wt, QB[2][0:E, 0:T]).then_inc(b["wt_out"], 1)
            dve.wait_ge(b["bo_mm"], 1)
            nc.vector.tensor_copy(BOW, QB[3][:, 0:T]).then_inc(b["bo_out"], 1)

            def weigh(g, t):
                for k in range(2):
                    dve.wait_ge(b["h2"], 16 * g + 2 * t + k + 1)
                    v = rowsof(H2[t % 2][:, k, :])
                    nc.vector.tensor_tensor(v, v, WM[:, t % EP, :].unsqueeze(1).to_broadcast([P, 2, T]), ALU.mult)\
                        .then_inc(b["hw"], 1)

            def finish(g, f):
                dve.wait_ge(b["l3_mm"], 2 * g + f + 1)
                dve.wait_ge(b["res_a"], 2 * g + f + 1)
                dve.wait_ge(b["tr_mm"], 2 * g)
                nc.vector.tensor_tensor(RES[f], QB[f][:, :], R1[f], ALU.add).then_inc(b["res"], 1)

            def token_major(g, f):
                dve.wait_ge(b["tr_mm"], 2 * g + f + 1)
                dve.wait_ge(b["stored"], 64 * g)
                for k in range(2):
                    nc.vector.tensor_copy(OUTT[f][:, k].rearrange("p n (r d) -> p (n r) d", r=2),
                                          QB[2 + f][:, :].rearrange("p (m k d) -> p m k d", k=2, d=D)[:, :, k, :])\
                        .then_inc(b["tr_out"], 1)

            def experts(g):
                for t in range(2 * EP):
                    weigh(g, t)
                    if t == EP:
                        finish(g, 0)
                    if t == EP + 2:
                        token_major(g, 0)
                finish(g, 1)
                token_major(g, 1)

            experts(0)
            with dve.Fori(1, G) as g:
                experts(g)


_INS = ["x", "tok_W1", "tok_b1", "tok_W2", "tok_b2", "tok_W3", "tok_b3", "tok_W4", "tok_b4",
        "attn_Wq", "attn_bq", "attn_Wk", "attn_bk", "attn_Wv", "attn_bv", "attn_Wg", "attn_bg",
        "attn_input_bias", "attn_norm_scale", "ffn_Wr", "ffn_br", "ffn_W1", "ffn_b1", "ffn_g1", "ffn_be1",
        "ffn_m1", "ffn_v1", "ffn_W2", "ffn_b2", "ffn_g2", "ffn_be2", "ffn_m2", "ffn_v2", "ffn_Wo", "ffn_bo"]


def kernel(**inputs):
    import numpy as np
    import concourse.bacc as bacc
    from concourse.bass_utils import run_bass_kernel_spmd as run

    nc = bacc.Bacc("TRN2", target_bir_lowering=False, num_devices=1)
    arrays, args = {}, []
    for name in _INS:
        a = np.ascontiguousarray(inputs[name if name == "x" else "L0_" + name])
        arrays["in_" + name] = a
        args.append(nc.dram_tensor("in_" + name, a.shape, mybir.dt.from_np(a.dtype), kind="ExternalInput").ap())
    result = nc.dram_tensor("result", (NB, T, D), F32, kind="ExternalOutput").ap()
    build(nc, *args, result)
    r = run(nc, [arrays], core_ids=[0])
    return r.results[0]["result"]
```

```python
from contextlib import ExitStack

import concourse.bass as bass
from concourse import mybir

F32 = mybir.dt.float32
ALU = mybir.AluOpType
ACT = mybir.ActivationFunctionType
AX_X = mybir.AxisListType.X

P = 128
D = 64
T = 256
NB = 64
GB = 8
SB = GB // 2
G = NB // GB
PC = SB * T
HC = PC // 2
C = 128
REF = 0.45
E = 8
LN_EXP, LN, EXP_TANH = "natural_log_exp_and_others", "natural_log", "exp_and_others"
EP = E // 2
UW = T + 1
FC = 512
NFC = NB // 2 * T // FC
TOK_EPS, RMS_EPS, BN_EPS = 1e-5, 1e-8, 1e-3
ROWS = ["tok_b1", "tok_b2", "tok_b3", "tok_b4", "bq", "bk", "bv", "bgi", "bgf", "bgo", "input_bias", "norm_scale"]
BN_ROWS = ["b1", "g1", "be1", "m1", "v1", "b2", "g2", "be2", "m2", "v2"]
NV, NBN = len(ROWS), len(BN_ROWS) * EP
SCORE_BANK = (0, 1, 2, 3, 0, 1, 0, 1)
JS = (2, 3, 0, 1)
JS_LAST = (0, 2, 1, 3)
RMS_SCALE = 2.0 ** 40


def build(nc, x, tok_W1, tok_b1, tok_W2, tok_b2, tok_W3, tok_b3, tok_W4, tok_b4, Wq, bq, Wk, bk, Wv, bv,
          Wg, bg, input_bias, norm_scale, Wr, br, W1, b1, g1, be1, m1, v1, W2, b2, g2, be2, m2, v2, Wo, bo, out):
    with ExitStack() as ctx:
        def sb(name, shape):
            return ctx.enter_context(nc.sbuf_tensor(name, shape, F32))

        def sem(name):
            return ctx.enter_context(nc.semaphore(name))

        ident = sb("ident", [P, P])
        mean_mat = sb("mean_mat", [P, P])
        center_mat = sb("center_mat", [P, P])
        sum_mat = sb("sum_mat", [P, P])
        causal = sb("causal", [P, 3 * C])
        cols = sb("cols", [P, NV + NBN])
        wac = sb("wac", [4, P])
        w2T = sb("w2T", [P, P])
        w4T = sb("w4T", [P, D])
        wproj = sb("wproj", [P, 6, P])
        fw1 = sb("fw1", [P, 2, EP, P])
        fw2 = sb("fw2", [P, EP, P])
        fwo = sb("fwo", [P, EP, D])
        wr = sb("wr", [P, E])
        br_row = sb("br_row", [1, E])
        ones_row = sb("ones_row", [1, P])
        bo_w = sb("bo_w", [E, P])
        col2 = sb("col2", [P, 8])
        bn_s = sb("bn_s", [P, 2, EP])
        bn_t = sb("bn_t", [P, 2, EP])

        HH = sb("HH", [P, NB // 2 * T])
        XN2 = sb("XN2", [P, NB // 2 * T])
        feat = sb("feat", [P, T])
        decay_ends = sb("decay_ends", [P, G * GB])

        X = sb("X", [4, GB * T])
        A = sb("A", [P, GB * T])
        CT = sb("CT", [P, PC])
        Z = sb("Z", [P, GB * T])
        U = sb("U", [P, GB * UW])
        UF = sb("UF", [P, GB * UW])

        SQ = sb("SQ", [P, PC])
        XC_IS = sb("XC_IS", [P, PC])
        RS_FS = sb("RS_FS", [P, PC])
        LF_UT = sb("LF_UT", [P, PC])
        LI = sb("LI", [P, PC])
        K_NN = sb("K_NN", [P, PC])
        KZ = sb("KZ", [P, 2, PC])
        Q = sb("Q", [P, PC])
        V = sb("V", [P, PC])
        EO = sb("EO", [P, PC])
        M = sb("M", [P, SB * UW])
        NC_ = sb("NC_", [P, PC])
        HR = sb("HR", [P, PC])
        AT = sb("AT", [P, GB, 3 * C])
        ends = sb("ends", [P, GB])
        lam = sb("lam", [P, GB])
        SQL = sb("SQL", [P, PC])
        RSL = sb("RSL", [P, PC])
        zeros = sb("zeros", [P, C])
        side = sb("side", [P, 2])

        rows = SQL[0:NV, 0:P]
        bn_rows = SQL[0:NBN, P:2 * P]
        w2_raw = RSL[:, 0:P]
        w4_raw = RSL[0:D, P:2 * P]

        H1 = [A[:, 0:1024].rearrange("p (s c) -> p s c", s=2), A[:, 1024:2048].rearrange("p (s c) -> p s c", s=2)]
        H2 = [Z[:, 0:1024].rearrange("p (s c) -> p s c", s=2), Z[:, 1024:2048].rearrange("p (s c) -> p s c", s=2)]
        WM = AT[:, 0:4, 0:T]
        BOW = LF_UT[:, 0:T]
        wb = K_NN[:, :].rearrange("p (t c) -> p t c", t=2)
        wn = M[:, 0:16].rearrange("p (t e) -> p t e", t=2)
        wx = M[:, 16:32].rearrange("p (t e) -> p t e", t=2)
        wmx, wsm, wrc = M[:, 32:34], M[:, 34:36], M[:, 36:38]
        wt = Q[0:E, 0:T]
        R1 = [SQ[:, 0:512], SQ[:, 512:1024]]
        RES = [XC_IS[:, 0:512], XC_IS[:, 512:1024]]
        OUTT = [V[:, 512 * f:512 * f + 512].rearrange("p (s n c) -> p s n c", s=2, n=2) for f in range(2)]

        TB = [ctx.enter_context(nc.psum_tensor(f"TB{j}", [P, 512], F32)) for j in range(4)]
        QB = [ctx.enter_context(nc.psum_tensor(f"QB{j}", [P, 512], F32)) for j in range(4)]

        U3 = U[:, :].rearrange("p (n c) -> p n c", c=UW)
        UF3 = UF[:, :].rearrange("p (n c) -> p n c", c=UW)
        A3 = A[:, :].rearrange("p (n c) -> p n c", c=T)
        Z3 = Z[:, :].rearrange("p (n c) -> p n c", c=T)
        M3 = M[:, :].rearrange("p (n c) -> p n c", c=UW)
        NC3 = NC_[:, :].rearrange("p (n c) -> p n c", c=C)
        HR3 = HR[:, :].rearrange("p (n c) -> p n c", c=T)
        half = [slice(0, D), slice(D, P)]

        def hs(h):
            return slice(HC * h, HC * h + HC)

        def tc(j):
            return slice(512 * j, 512 * j + 512)

        def rowsof(ap, c=T):
            return ap.rearrange("p (n c) -> p n c", c=c)

        def hh(a, h):
            return HH[:, bass.ds(a * PC + HC * h, HC)]

        def xn2(a, h):
            return XN2[:, bass.ds(a * PC + HC * h, HC)]

        def col(name):
            i = ROWS.index(name)
            return cols[:, i:i + 1]

        def bn_cols(name):
            i = NV + BN_ROWS.index(name) * EP
            return cols[:, i:i + EP]

        neg_bf, bias_i, neg_bo, a_bias, c_bias, out_scale = (col2[:, i:i + 1] for i in range(6))

        mix_loaded = sem("mix_loaded")
        rows_loaded = sem("rows_loaded")
        bn_loaded = sem("bn_loaded")
        att_loaded = sem("att_loaded")
        ffn_loaded = sem("ffn_loaded")
        x_in = sem("x_in")
        w_cleared = sem("w_cleared")
        cleared = sem("cleared")
        id_ready = sem("id_ready")
        mask_ready = sem("mask_ready")
        mats = sem("mats")
        side_ready = sem("side_ready")
        setup_mm = sem("setup_mm")
        setup_out = sem("setup_out")
        derived = sem("derived")
        bn_ln = sem("bn_ln")
        bn_rs = sem("bn_rs")
        bn_ready = sem("bn_ready")
        s = {n: sem(n) for n in (
            "ac_mm", "a_out", "c_out", "u0_out", "mix_relu", "mix_mm", "mix_add", "uf_out", "fin_mm", "fin_add", "h1_out",
            "lnc_mm", "sq_out", "xc_out", "var_mm", "rs_ln", "rs_out", "xn_out",
            "proj_mm", "f_out", "i_out", "k_out", "q_out", "v_out", "o_out", "kz_out",
            "f_abs", "f_exp", "f_log", "lf_out", "li_out", "m_out", "t1_out", "lf2_out", "lg_out",
            "o_abs", "o_exp", "o_log", "sp_out", "ee_out", "et_out",
            "fs_out", "is_out", "nc_out", "ends_out", "nd_out", "ar_out", "eu_out", "u_out", "lam_in", "lam_out",
            "ends_kept", "ik_out", "nn_out", "nq_out", "den_mm", "den_sq", "den_out",
            "at_mm", "at_out", "ut_mm", "ut_out", "av_mm", "tmp_out", "hr_a", "hr_out", "o_h",
            "sqo_out", "rms_mm", "rms_add", "rr_ln", "rr_out", "y_out", "h2_out",
            "l2c_mm", "sq2_out", "xc2_out", "var2_mm", "rs2_ln", "rs2_out", "xn2_out", "feat_out")}
        b = {n: sem("b_" + n) for n in (
            "lg_mm", "mx", "nmx", "ex", "rc", "wn", "wb", "w_mm", "w_out", "wt_mm", "wt_out", "bo_mm", "bo_out",
            "l1_mm", "h1", "l2_mm", "h2", "hw", "l3_mm", "res_a", "res", "tr_mm", "tr_out")}
        stored = [sem("b_stored0"), sem("b_stored1")]

        def after(engine, semaphore, count):
            if not isinstance(count, int) or count > 0:
                engine.wait_ge(semaphore, count)

        N_MIX, N_ATT, N_FFN, N_BN = 6, 12, 11, len(BN_ROWS)

        block = ctx.enter_context(nc.Block())

        @block.sync
        def _(sp):
            def load_x(g):
                return sp.dma_start(X[:, :].rearrange("d (b l) -> d b l", l=T),
                                    x[bass.ds(g * GB, GB)].rearrange("b d l -> d b l"))

            load_x(0).then_inc(x_in, 16)
            with nc.allow_non_contiguous_dma(reason="weights of 64 x 4"):
                sp.dma_start(wac[:, 0:D], tok_W1.rearrange("o d -> d o")).then_inc(mix_loaded, 16)
                sp.dma_start(wac[:, D:P], tok_W3.rearrange("o d -> d o")).then_inc(mix_loaded, 16)
            sp.wait_ge(w_cleared, 1)
            for h in range(2):
                sp.dma_start(w2_raw[half[h], D * h:D * h + D], tok_W2).then_inc(mix_loaded, 16)
                sp.dma_start(w4_raw[:, D * h:D * h + D], tok_W4).then_inc(mix_loaded, 16)
            for n, v in (("tok_b1", tok_b1), ("tok_b2", tok_b2), ("tok_b3", tok_b3), ("tok_b4", tok_b4), ("bq", bq),
                         ("bk", bk), ("bv", bv), ("bgi", bg[0:D]), ("bgf", bg[D:2 * D]), ("bgo", bg[2 * D:3 * D]),
                         ("input_bias", input_bias), ("norm_scale", norm_scale)):
                i = ROWS.index(n)
                sp.dma_start(rows[i:i + 1, :].rearrange("a (t d) -> a t d", t=2),
                             v.rearrange("(a t d) -> a t d", a=1, t=1).to_broadcast([1, 2, D]))\
                    .then_inc(rows_loaded, 16)

            with sp.Fori(1, G) as g:
                sp.wait_ge(s["ac_mm"], 4 * g)
                load_x(g).then_inc(x_in, 16)

            ov = out.rearrange("(g s f n) (p r) d -> g s f p n (r d)", g=G, s=2, f=2, n=2, r=2)
            with sp.Fori(0, G) as g:
                for f in range(2):
                    for k in range(2):
                        sp.wait_ge(b["tr_out"], 4 * g + 2 * f + k + 1)
                        sp.dma_start(ov[bass.ds(g, 1), k, f].rearrange("a p n c -> (a p) n c"),
                                     OUTT[f][:, k]).then_inc(stored[f], 16)
            for f in range(2):
                sp.wait_ge(stored[f], 16 * 2 * G)

        @block.gpsimd
        def _(pool):
            nc.gpsimd.memset(w2_raw[:, :], 0.0).then_inc(w_cleared, 1)
            nc.gpsimd.memset(ident[:, :], 0.0).then_inc(id_ready, 1)
            pool.wait_ge(id_ready, 1)
            nc.gpsimd.affine_select(out=ident[:, :], in_=ident[:, :], compare_op=ALU.not_equal, fill=1.0, base=0,
                                    pattern=[[-1, P]], channel_multiplier=1).then_inc(id_ready, 1)
            nc.gpsimd.memset(wproj[:, :, :], 0.0).then_inc(w_cleared, 1)
            nc.gpsimd.memset(fw1[:, :, :, :], 0.0).then_inc(w_cleared, 1)
            nc.gpsimd.memset(fw2[:, :, :], 0.0).then_inc(w_cleared, 1)
            nc.gpsimd.memset(U3[:, :, 0:1], 0.0).then_inc(cleared, 1)
            nc.gpsimd.memset(UF[:, :], 0.0).then_inc(cleared, 1)
            nc.gpsimd.memset(M3[:, :, 0:1], 0.0).then_inc(cleared, 1)
            nc.gpsimd.memset(feat[:, :], 0.0).then_inc(cleared, 1)
            nc.gpsimd.memset(zeros[:, :], 0.0).then_inc(cleared, 1)
            nc.gpsimd.memset(ones_row[:, :], 1.0).then_inc(cleared, 1)
            nc.gpsimd.memset(causal[:, :], 1.0).then_inc(mask_ready, 1)
            pool.wait_ge(mask_ready, 1)
            for c in (0, 2):
                v = causal[:, C * c:C * c + C]
                nc.gpsimd.affine_select(out=v, in_=v, compare_op=ALU.is_ge, fill=0.0, base=0,
                                        pattern=[[1, C]], channel_multiplier=-1).then_inc(mask_ready, 1)
            pool.wait_ge(w_cleared, 4)
            for i, v in enumerate((b1, g1, be1, m1, v1, b2, g2, be2, m2, v2)):
                pool.dma_start(bn_rows[i * EP:(i + 1) * EP, :],
                               v.rearrange("(p e) h -> p (e h)", e=2)).then_inc(bn_loaded, 16)
            w2v = W2.rearrange("(p two) h k -> two h p k", two=2)
            wov = Wo.rearrange("(p two) h d -> two h p d", two=2)
            for h in range(2):
                pool.dma_start(fw1[half[h], h, :, :].rearrange("d p (e h) -> d (p e) h", e=2),
                               W1.rearrange("e d h -> d e h")).then_inc(ffn_loaded, 16)
                pool.dma_start(fw2[half[h], :, D * h:D * h + D], w2v[h]).then_inc(ffn_loaded, 16)
                pool.dma_start(fwo[half[h], :, :], wov[h]).then_inc(ffn_loaded, 16)
                pool.dma_start(wr[half[h], :], Wr).then_inc(ffn_loaded, 16)
                pool.dma_start(bo_w[:, D * h:D * h + D], bo).then_inc(ffn_loaded, 16)
            pool.dma_start(br_row[:, :], br.rearrange("(a e) -> a e", a=1)).then_inc(ffn_loaded, 16)

            pool.wait_ge(cleared, 6)
            pool.wait_ge(side_ready, 4)

            def turn(it, att, late):
                a, l = it - 1, it - 2
                if att:
                    pool.wait_ge(s["k_out"], 2 * a + 2)
                    pool.wait_ge(s["at_mm"], GB * a)
                    for k in range(2):
                        nc.gpsimd.tensor_tensor(KZ[:, k, :], K_NN[:, :], side[:, k:k + 1].to_broadcast([P, PC]),
                                                ALU.mult).then_inc(s["kz_out"], 1)
                if late:
                    for h in range(2):
                        pool.wait_ge(s["rr_out"], 2 * l + h + 1)
                        nc.gpsimd.tensor_tensor(RSL[:, hs(h)], HR[:, hs(h)], RSL[:, hs(h)], ALU.mult)\
                            .then_inc(s["y_out"], 1)
                if att:
                    pool.wait_ge(s["m_out"], SB * a + SB)
                    nc.gpsimd.tensor_tensor(rowsof(LF_UT[:, :]), rowsof(LF_UT[:, :]), M3[:, :, 0:T], ALU.add)\
                        .then_inc(s["t1_out"], 1)
                    pool.wait_ge(s["t1_out"], a + 1)
                    nc.gpsimd.tensor_tensor(rowsof(LF_UT[:, :]), rowsof(LF_UT[:, :]), M3[:, :, 1:UW], ALU.subtract)\
                        .then_inc(s["lf2_out"], 1)
                    nc.gpsimd.tensor_tensor(rowsof(LI[:, :]), rowsof(LI[:, :]), M3[:, :, 1:UW], ALU.subtract)\
                        .then_inc(s["lg_out"], 1)
                    pool.wait_ge(s["is_out"], a + 1)
                    pool.wait_ge(s["nd_out"], a + 1)
                    nc.gpsimd.tensor_tensor(LI[:, :], LI[:, :], NC_[:, :], ALU.add).then_inc(s["ar_out"], 1)
                    nc.gpsimd.tensor_tensor(XC_IS[:, :], XC_IS[:, :], K_NN[:, :], ALU.mult).then_inc(s["ik_out"], 1)
                    for h in range(2):
                        pool.wait_ge(s["eu_out"], a + 1)
                        pool.wait_ge(s["v_out"], 2 * a + h + 1)
                        nc.gpsimd.tensor_tensor(V[:, hs(h)], V[:, hs(h)], LI[:, hs(h)], ALU.mult)\
                            .then_inc(s["u_out"], 1)
                    for h in range(2):
                        pool.wait_ge(s["nn_out"], SB * a + 2 * h + 2)
                        nc.gpsimd.tensor_tensor(K_NN[:, hs(h)], K_NN[:, hs(h)], Q[:, hs(h)], ALU.mult)\
                            .then_inc(s["nq_out"], 1)
                    pool.wait_ge(s["sp_out"], a + 1)
                    nc.gpsimd.tensor_tensor(EO[:, :], EO[:, :], NC_[:, :], ALU.add).then_inc(s["ee_out"], 1)
                if late:
                    for n in range(SB):
                        pool.wait_ge(s["xn2_out"], 2 * l + n // 2 + 1)
                        pool.wait_ge(s["feat_out"], SB * l + n)
                        nc.gpsimd.tensor_tensor(feat[:, :], feat[:, :], XN2[:, bass.ds(l * PC + T * n, T)], ALU.add)\
                            .then_inc(s["feat_out"], 1)

            turn(1, True, False)
            turn(2, True, True)
            with pool.Fori(3, G + 1) as it:
                turn(it, True, True)
            turn(G + 1, False, True)

            pool.wait_ge(b["bo_out"], 1)
            def residual(g):
                for f in range(2):
                    after(pool, b["res"], 2 * g - 1 + f)
                    nc.gpsimd.tensor_tensor(rowsof(R1[f]), rowsof(hh(g, f)),
                                            BOW.unsqueeze(1).to_broadcast([P, 2, T]), ALU.add).then_inc(b["res_a"], 1)

            residual(0)
            with pool.Fori(1, G) as g:
                residual(g)

        @block.scalar
        def _(act):
            act.wait_ge(w_cleared, 2)
            for i, w in enumerate((Wg[:, D:2 * D], Wg[:, 0:D], Wk, Wq, Wv, Wg[:, 2 * D:3 * D])):
                for h in range(2):
                    act.dma_start(wproj[half[h], i, D * h:D * h + D], w).then_inc(att_loaded, 16)
            nc.scalar.preload_act_table_set(LN_EXP)
            act.wait_ge(derived, 6)

            def inputs(it, js):
                for i in js:
                    j = JS[i]
                    act.wait_ge(s["ac_mm"], 4 * it + i + 1)
                    nc.scalar.activation(A3[half[0], 2 * j:2 * j + 2, :], rowsof(TB[j][half[0], :]), ACT.Identity,
                                         bias=a_bias[half[0], :]).then_inc(s["a_out"], 1)
                    nc.scalar.activation(A3[half[1], 2 * j:2 * j + 2, ::-1], rowsof(TB[j][half[0], :]), ACT.Identity,
                                         bias=a_bias[half[0], :]).then_inc(s["a_out"], 1)

            def relu(it, k, js):
                for i in js:
                    j = JS[i]
                    act.wait_ge(s["mix_add"], 28 * it + 4 * k + i + 1)
                    nc.scalar.activation(U3[:, 2 * j:2 * j + 2, 1:UW], Z3[:, 2 * j:2 * j + 2, :], ACT.Relu)\
                        .then_inc(s["mix_relu"], 1)

            def turn(it, mix, att, late):
                a, l = it - 1, it - 2
                if mix:
                    inputs(it, (0, 1))
                if att:
                    for h in range(2):
                        act.wait_ge(s["lnc_mm"], 2 * a + h + 1)
                        nc.scalar.activation(SQ[:, hs(h)], QB[h][:, :], ACT.Square).then_inc(s["sq_out"], 1)
                if mix:
                    inputs(it, (2, 3))
                if late:
                    for h in range(2):
                        act.wait_ge(s["o_h"], 2 * l + h + 1)
                        nc.scalar.activation(SQL[:, hs(h)], HR[:, hs(h)], ACT.Square).then_inc(s["sqo_out"], 1)
                if mix:
                    relu(it, 0, (0, 1))
                if att:
                    for h in range(2):
                        act.wait_ge(s["var_mm"], 2 * a + h + 1)
                        nc.scalar.activation(RS_FS[:, hs(h)], QB[h][:, :], ACT.Ln, bias=TOK_EPS)\
                            .then_inc(s["rs_ln"], 1)
                    for h in range(2):
                        act.wait_ge(s["rs_ln"], 2 * a + h + 1)
                        nc.scalar.activation(RS_FS[:, hs(h)], RS_FS[:, hs(h)], ACT.Exp, scale=-0.5)\
                            .then_inc(s["rs_out"], 1)
                if mix:
                    relu(it, 0, (2, 3))
                if att:
                    nc.scalar.preload_act_table_set(EXP_TANH)
                if mix:
                    relu(it, 1, (0, 1))
                if att:
                    for h in range(2):
                        act.wait_ge(s["proj_mm"], 12 * a + h + 1)
                        nc.scalar.activation(LF_UT[:, hs(h)], QB[2 + h][:, :], ACT.Identity, bias=neg_bf, scale=-1.0)\
                            .then_inc(s["f_out"], 1)
                if mix:
                    relu(it, 1, (2, 3))
                if att:
                    for h in range(2):
                        act.wait_ge(s["proj_mm"], 12 * a + 2 + h + 1)
                        nc.scalar.activation(LI[:, hs(h)], QB[h][:, :], ACT.Tanh, bias=bias_i, scale=0.1)\
                            .then_inc(s["i_out"], 1)
                    act.wait_ge(s["f_out"], 2 * a + 2)
                    nc.scalar.activation(SQ[:, :], LF_UT[:, :], ACT.Abs).then_inc(s["f_abs"], 1)
                    act.wait_ge(s["f_abs"], a + 1)
                    nc.scalar.activation(SQ[:, :], SQ[:, :], ACT.Exp, scale=-1.0).then_inc(s["f_exp"], 1)
                nc.scalar.preload_act_table_set(LN)
                if att:
                    act.wait_ge(s["f_exp"], a + 1)
                    nc.scalar.activation(SQ[:, :], SQ[:, :], ACT.Ln, bias=1.0).then_inc(s["f_log"], 1)
                if late:
                    for h in range(2):
                        act.wait_ge(s["rms_add"], 2 * l + h + 1)
                        nc.scalar.activation(RSL[:, hs(h)], RSL[:, hs(h)], ACT.Ln, scale=RMS_SCALE)\
                            .then_inc(s["rr_ln"], 1)
                nc.scalar.preload_act_table_set(LN_EXP)
                if late:
                    for h in range(2):
                        act.wait_ge(s["rr_ln"], 2 * l + h + 1)
                        nc.scalar.activation(RSL[:, hs(h)], RSL[:, hs(h)], ACT.Exp, scale=-0.5)\
                            .then_inc(s["rr_out"], 1)
                if mix:
                    relu(it, 2, range(4))
                if att:
                    for h in range(2):
                        act.wait_ge(s["proj_mm"], 12 * a + 8 + h + 1)
                        nc.scalar.activation(V[:, hs(h)], QB[2 + h][:, :], ACT.Identity, bias=col("bv"))\
                            .then_inc(s["v_out"], 1)
                    for h in range(2):
                        act.wait_ge(s["proj_mm"], 12 * a + 10 + h + 1)
                        nc.scalar.activation(EO[:, hs(h)], QB[h][:, :], ACT.Identity, bias=neg_bo, scale=-1.0)\
                            .then_inc(s["o_out"], 1)
                if mix:
                    relu(it, 3, range(4))
                if att:
                    act.wait_ge(s["lf2_out"], a + 1)
                    nc.scalar.activation(RS_FS[:, :], LF_UT[:, :], ACT.Exp).then_inc(s["fs_out"], 1)
                    act.wait_ge(s["lg_out"], a + 1)
                    nc.scalar.activation(XC_IS[:, :], LI[:, :], ACT.Exp).then_inc(s["is_out"], 1)
                if mix:
                    relu(it, 4, range(4))
                if late:
                    for h in range(2):
                        act.wait_ge(s["l2c_mm"], 2 * l + h + 1)
                        nc.scalar.activation(SQL[:, hs(h)], QB[2 + h][:, :], ACT.Square).then_inc(s["sq2_out"], 1)
                if att:
                    act.wait_ge(s["ar_out"], a + 1)
                    nc.scalar.activation(LI[:, :], LI[:, :], ACT.Exp).then_inc(s["eu_out"], 1)
                    act.wait_ge(s["lam_in"], 2 * a + 2)
                    nc.scalar.activation(lam[:, :], lam[:, :], ACT.Exp).then_inc(s["lam_out"], 1)
                    act.wait_ge(s["lf_out"], a + 1)
                    act.wait_ge(s["o_out"], 2 * a + 2)
                    nc.scalar.activation(SQ[:, :], EO[:, :], ACT.Abs).then_inc(s["o_abs"], 1)
                    act.wait_ge(s["o_abs"], a + 1)
                    nc.scalar.activation(SQ[:, :], SQ[:, :], ACT.Exp, scale=-1.0).then_inc(s["o_exp"], 1)
                    act.wait_ge(s["o_exp"], a + 1)
                    nc.scalar.activation(SQ[:, :], SQ[:, :], ACT.Ln, bias=1.0).then_inc(s["o_log"], 1)
                if mix:
                    relu(it, 5, range(4))
                if late:
                    for h in range(2):
                        act.wait_ge(s["var2_mm"], 2 * l + h + 1)
                        nc.scalar.activation(RSL[:, hs(h)], QB[2 + h][:, :], ACT.Ln, bias=TOK_EPS)\
                            .then_inc(s["rs2_ln"], 1)
                    for h in range(2):
                        act.wait_ge(s["rs2_ln"], 2 * l + h + 1)
                        nc.scalar.activation(RSL[:, hs(h)], RSL[:, hs(h)], ACT.Exp, scale=-0.5)\
                            .then_inc(s["rs2_out"], 1)
                if mix:
                    for i, j in enumerate(JS_LAST):
                        act.wait_ge(s["mix_add"], 28 * it + 24 + i + 1)
                        nc.scalar.activation(UF3[half[0], 2 * j:2 * j + 2, 1:T], Z3[half[0], 2 * j:2 * j + 2, 0:T - 1],
                                             ACT.Relu).then_inc(s["uf_out"], 1)
                        nc.scalar.activation(UF3[half[1], 2 * j:2 * j + 2, 0:T - 1],
                                             Z3[half[1], 2 * j:2 * j + 2, T - 2::-1],
                                             ACT.Relu).then_inc(s["uf_out"], 1)
                if att:
                    for h in range(2):
                        act.wait_ge(s["ut_mm"], 2 * a + h + 1)
                        nc.scalar.activation(LF_UT[:, hs(h)], QB[h][:, :], ACT.Identity).then_inc(s["ut_out"], 1)
                    for h in range(2):
                        act.wait_ge(s["den_mm"], 2 * a + h + 1)
                        nc.scalar.activation(K_NN[:, hs(h)], QB[2 + h][:, :], ACT.Square).then_inc(s["den_sq"], 1)
                    act.wait_ge(s["ee_out"], a + 1)
                    nc.scalar.activation(EO[:, :], EO[:, :], ACT.Exp, scale=-1.0).then_inc(s["et_out"], 1)
                    act.wait_ge(s["lam_out"], a + 1)
                    for n in range(SB):
                        act.wait_ge(s["av_mm"], SB * a + n + 1)
                        nc.scalar.activation(SQ[:, C * n:C * n + C], QB[n][:, C:2 * C], ACT.Identity,
                                             scale=lam[:, 2 * n:2 * n + 1]).then_inc(s["tmp_out"], 1)
                if mix:
                    for h in range(2):
                        act.wait_ge(s["fin_add"], 2 * it + h + 1)
                        nc.scalar.activation(hh(it, h), Z[:, hs(h)], ACT.Relu, bias=c_bias).then_inc(s["h1_out"], 1)

            turn(0, True, False, False)
            turn(1, True, True, False)
            turn(2, True, True, True)
            with act.Fori(3, G) as it:
                turn(it, True, True, True)
            turn(G, False, True, True)
            turn(G + 1, False, False, True)

            act.wait_ge(setup_out, 4)
            for i, n in enumerate(("v1", "v2")):
                nc.scalar.activation(bn_s[:, i, :], bn_cols(n), ACT.Ln, bias=BN_EPS).then_inc(bn_ln, 1)
            act.wait_ge(bn_ln, 2)
            nc.scalar.activation(bn_s[:, :, :], bn_s[:, :, :], ACT.Exp, scale=-0.5).then_inc(bn_rs, 1)

            for t in range(2):
                act.wait_ge(b["nmx"], 1)
                nc.scalar.activation(wx[:, t, :], QB[t][:, 0:E], ACT.Exp, bias=wmx[:, t:t + 1],
                                     accum_out=wsm[:, t:t + 1]).then_inc(b["ex"], 1)
            act.wait_ge(bn_ready, 7)

            def h1(g, t):
                for k in range(2):
                    act.wait_ge(b["l1_mm"], 16 * g + 2 * t + k + 1)
                    nc.scalar.activation(H1[t % 2][:, k, :], TB[k][:, :], ACT.Relu, bias=bn_t[:, 0, t % EP:t % EP + 1],
                                         scale=bn_s[:, 0, t % EP:t % EP + 1]).then_inc(b["h1"], 1)

            def h2(g, t):
                for k in range(2):
                    act.wait_ge(b["l2_mm"], 16 * g + 2 * t + k + 1)
                    nc.scalar.activation(H2[t % 2][:, k, :], TB[2 + k][:, :], ACT.Relu,
                                         bias=bn_t[:, 1, t % EP:t % EP + 1],
                                         scale=bn_s[:, 1, t % EP:t % EP + 1]).then_inc(b["h2"], 1)

            def experts(g, first=False):
                for t in range(2 * EP):
                    h1(g, t)
                    if not (first and t == 0):
                        h2(g, t - 1)

            experts(0, True)
            with act.Fori(1, G) as g:
                experts(g)
            h2(G - 1, 2 * EP - 1)

        @block.tensor
        def _(pe):
            pe.wait_ge(id_ready, 2)
            pe.wait_ge(mix_loaded, 16 * N_MIX)
            pe.transpose(TB[0][:, 0:P], w2_raw, ident[:, :]).then_inc(setup_mm, 1)
            pe.transpose(TB[1][:, 0:D], w4_raw, ident[0:D, 0:D]).then_inc(setup_mm, 1)
            pe.wait_ge(rows_loaded, 16 * NV)
            pe.transpose(TB[2][:, 0:NV], rows, ident[0:NV, 0:NV]).then_inc(setup_mm, 1)
            pe.wait_ge(bn_loaded, 16 * N_BN)
            pe.transpose(TB[3][:, 0:NBN], bn_rows, ident[0:NBN, 0:NBN]).then_inc(setup_mm, 1)
            pe.wait_ge(setup_out, 4)
            pe.wait_ge(cleared, 6)

            def inputs(it, js):
                for j in js:
                    pe.matmul(TB[j][:, :], wac[:, :], X[:, tc(j)], start=True, stop=True).then_inc(s["ac_mm"], 1)

            def layer(it, k, js):
                for j in js:
                    if k == 0:
                        pe.wait_ge(s["u0_out"], 4 * it + JS.index(j) + 1)
                    else:
                        pe.wait_ge(s["mix_relu"], 24 * it + 4 * (k - 1) + JS.index(j) + 1)
                    pe.matmul(TB[j][:, :], w2T[:, :], U3[:, 2 * j:2 * j + 2, 0:T], start=True, stop=True)\
                        .then_inc(s["mix_mm"], 1)

            def project(a, l, p, late):
                freed = (None, "rs_ln", "f_out", "i_out", "k_out", "q_out")[p]
                for h in range(2):
                    if p == 0:
                        pe.wait_ge(s["xn_out"], 2 * a + h + 1)
                        if late:
                            pe.wait_ge(s["rms_add"], 2 * l + h + 1)
                    else:
                        pe.wait_ge(s[freed], 2 * a + h + 1)
                    pe.matmul(QB[2 - 2 * (p % 2) + h][:, :], wproj[:, p, :], XC_IS[:, hs(h)], start=True, stop=True)\
                        .then_inc(s["proj_mm"], 1)

            def scores(a, bs):
                for bb in bs:
                    k, n = bb // SB, bb % SB
                    bank = QB[SCORE_BANK[bb]]
                    if bb < 2:
                        pe.wait_ge(s["o_out"], 2 * a + bb + 1)
                    elif bb < 4:
                        pe.wait_ge(s["v_out"], 2 * a + bb - 1)
                    elif bb < 6:
                        pe.wait_ge(s["at_out"], GB * a + bb - 3)
                    else:
                        pe.wait_ge(s["at_out"], GB * a + bb - 1)
                    pe.matmul(bank[:, 0:T], KZ[:, k, T * n:T * n + C], Q[:, T * n:T * n + T], start=True, stop=True)
                    pe.matmul(bank[:, T:T + C], KZ[:, k, T * n + C:T * n + T], Q[:, T * n + C:T * n + T],
                              start=True, stop=True).then_inc(s["at_mm"], 1)

            def turn(it, mix, att, late):
                a, l = it - 1, it - 2
                if mix:
                    pe.wait_ge(x_in, 16 * it + 16)
                    after(pe, s["mix_add"], 28 * it)
                    inputs(it, JS[0:2])
                if att:
                    pe.wait_ge(s["hr_out"], SB * a)
                    for h in range(2):
                        pe.wait_ge(s["h1_out"], 2 * a + h + 1)
                        pe.matmul(QB[h][:, :], center_mat[:, :], hh(a, h), start=True, stop=True)\
                            .then_inc(s["lnc_mm"], 1)
                if mix:
                    after(pe, s["fin_add"], 2 * it)
                    inputs(it, JS[2:4])
                    layer(it, 0, JS[0:2])
                if att:
                    for h in range(2):
                        pe.wait_ge(s["xc_out"], 2 * a + h + 1)
                        pe.wait_ge(s["sq_out"], 2 * a + h + 1)
                        pe.matmul(QB[h][:, :], mean_mat[:, :], SQ[:, hs(h)], start=True, stop=True)\
                            .then_inc(s["var_mm"], 1)
                if mix:
                    layer(it, 0, JS[2:4])
                if late:
                    for h in range(2):
                        pe.wait_ge(s["sqo_out"], 2 * l + h + 1)
                        pe.matmul(QB[2 + h][:, :], mean_mat[:, :], SQL[:, hs(h)], start=True, stop=True)\
                            .then_inc(s["rms_mm"], 1)
                if mix:
                    layer(it, 1, JS)
                if att:
                    for p in range(4):
                        project(a, l, p, late)
                if mix:
                    layer(it, 2, JS)
                if att:
                    for p in range(4, 6):
                        project(a, l, p, late)
                if mix:
                    layer(it, 3, JS)
                if att:
                    pe.wait_ge(s["kz_out"], 2 * a + 2)
                    pe.wait_ge(s["q_out"], 2 * a + 2)
                    scores(a, range(0, 4))
                if mix:
                    layer(it, 4, JS)
                if late:
                    for h in range(2):
                        if att:
                            pe.wait_ge(s["at_out"], GB * a + 3 + h)
                        else:
                            pe.wait_ge(s["rms_add"], 2 * l + h + 1)
                        pe.wait_ge(s["h2_out"], 2 * l + h + 1)
                        pe.matmul(QB[2 + h][:, :], center_mat[:, :], hh(l, h), start=True, stop=True)\
                            .then_inc(s["l2c_mm"], 1)
                if att:
                    scores(a, range(4, 6))
                if mix:
                    layer(it, 5, JS)
                if att:
                    scores(a, range(6, 8))
                if late:
                    for h in range(2):
                        pe.wait_ge(s["sq2_out"], 2 * l + h + 1)
                        pe.wait_ge(s["xc2_out"], 2 * l + h + 1)
                        pe.matmul(QB[2 + h][:, :], mean_mat[:, :], SQL[:, hs(h)], start=True, stop=True)\
                            .then_inc(s["var2_mm"], 1)
                if mix:
                    layer(it, 6, JS_LAST)
                if att:
                    for h in range(2):
                        pe.wait_ge(s["u_out"], 2 * a + h + 1)
                        pe.wait_ge(s["at_out"], GB * a + 6 + h + 1)
                        for c in range(4):
                            mm = pe.transpose(QB[h][:, C * c:C * c + C], V[:, HC * h + C * c:HC * h + C * c + C],
                                              ident[:, :])
                        mm.then_inc(s["ut_mm"], 1)
                    for h in range(2):
                        pe.wait_ge(s["nq_out"], 2 * a + h + 1)
                        if late:
                            pe.wait_ge(s["rs2_ln"], 2 * l + h + 1)
                        pe.matmul(QB[2 + h][:, :], sum_mat[:, :], K_NN[:, hs(h)], start=True, stop=True)\
                            .then_inc(s["den_mm"], 1)
                if att:
                    pe.wait_ge(s["at_out"], GB * a + GB)
                    for n in range(SB):
                        pe.wait_ge(s["ut_out"], 2 * a + n // 2 + 1)
                        if n < 2:
                            pe.wait_ge(s["ut_out"], 2 * a + n + 1)
                        else:
                            pe.wait_ge(s["den_sq"], 2 * a + n - 1)
                        for c, w in ((0, T), (1, C)):
                            for k in range(2):
                                mm = pe.matmul(QB[n][half[k], T * c:T * c + w],
                                               LF_UT[:, C * (2 * n + c) + D * k:C * (2 * n + c) + D * k + D],
                                               AT[:, SB * k + n, T * c:T * c + w], start=True, stop=True)
                        mm.then_inc(s["av_mm"], 1)
                if mix:
                    for h in range(2):
                        pe.wait_ge(s["uf_out"], 8 * it + 4 * h + 4)
                        for k in range(2):
                            n = SB * k + 2 * h
                            mm = pe.matmul(TB[h][half[k], :], w4T[:, :], UF3[:, n:n + 2, 0:T], start=True, stop=True)
                        mm.then_inc(s["fin_mm"], 1)

            turn(0, True, False, False)
            pe.wait_ge(mats, 9)
            pe.wait_ge(att_loaded, 16 * N_ATT)
            turn(1, True, True, False)
            turn(2, True, True, True)
            with pe.Fori(3, G) as it:
                turn(it, True, True, True)
            turn(G, False, True, True)
            turn(G + 1, False, False, True)

            pe.wait_ge(ffn_loaded, 16 * N_FFN)
            pe.wait_ge(s["feat_out"], SB * G)
            pe.wait_ge(bn_ready, 8)
            for t in range(2):
                pe.matmul(QB[t][:, 0:E], feat[:, P * t:P * t + P], wr[:, :], start=True, stop=False)
                pe.matmul(QB[t][:, 0:E], ones_row[:, :], br_row[:, :], start=False, stop=True)\
                    .then_inc(b["lg_mm"], 1)
            for t in range(2):
                pe.wait_ge(b["wb"], t + 1)
                for p in range(EP):
                    mm = pe.matmul(TB[p][:, P * t:P * t + P], wb[:, t, P * p:P * p + P], ident[:, :],
                                   start=True, stop=True)
            mm.then_inc(b["w_mm"], 1)
            for t in range(2):
                mm = pe.transpose(QB[2][0:E, P * t:P * t + P], wn[:, t, :], ident[:, :])
            mm.then_inc(b["wt_mm"], 1)
            pe.wait_ge(b["wt_out"], 1)
            pe.matmul(QB[3][:, 0:T], bo_w[:, :], wt, start=True, stop=True).then_inc(b["bo_mm"], 1)
            pe.wait_ge(b["w_out"], EP)
            pe.wait_ge(b["bo_out"], 1)

            def l1(g, t):
                for k in range(2):
                    pe.wait_ge(b["h1"], 16 * g + 2 * t)
                    pe.matmul(TB[k][:, :], fw1[:, k, t % EP, :], xn2(g, t // EP), start=True, stop=True)\
                        .then_inc(b["l1_mm"], 1)

            def l2(g, t):
                for k in range(2):
                    pe.wait_ge(b["h1"], 16 * g + 2 * t + k + 1)
                    pe.wait_ge(b["h2"], 16 * g + 2 * t)
                    pe.matmul(TB[2 + k][:, :], fw2[:, t % EP, :], H1[t % 2][:, k, :], start=True, stop=True)\
                        .then_inc(b["l2_mm"], 1)

            def l3(g, t):
                f, p = t // EP % 2, t % EP
                if p == 0:
                    after(pe, b["res"], 2 * g - 1 + f)
                pe.wait_ge(b["hw"], 16 * g + 2 * t + 2)
                for k in range(2):
                    mm = pe.matmul(QB[f][half[k], :], fwo[:, p, :], H2[t % 2][:, k, :],
                                   start=(p == 0), stop=(p == EP - 1))
                if p == EP - 1:
                    mm.then_inc(b["l3_mm"], 1)

            def turn_out(g, f):
                pe.wait_ge(b["res"], 2 * g + f + 1)
                after(pe, b["tr_out"], 4 * g - 2 + 2 * f)
                for n in range(2):
                    for r in range(2):
                        mm = pe.transpose(QB[2 + f][:, P * (2 * n + r):P * (2 * n + r) + P],
                                          RES[f][:, T * n + r:T * n + T:2], ident[:, :])
                mm.then_inc(b["tr_mm"], 1)

            def experts(g, first=False):
                for t in range(2 * EP):
                    l1(g, t)
                    if not (first and t < 1):
                        l2(g, t - 1)
                    if not (first and t < 2):
                        l3(g, t - 2)
                    if t == 3 and not first:
                        turn_out(g - 1, 1)
                    if t == EP + 3:
                        turn_out(g, 0)

            experts(0, True)
            with pe.Fori(1, G) as g:
                experts(g)
            l2(G - 1, 2 * EP - 1)
            l3(G - 1, 2 * EP - 2)
            l3(G - 1, 2 * EP - 1)
            turn_out(G - 1, 1)

        @block.vector
        def _(dve):
            for k in range(2):
                for h in range(2):
                    nc.vector.memset(side[half[h], k:k + 1], float(h == k)).then_inc(side_ready, 1)
            for m, v in ((mean_mat, 1.0 / D), (sum_mat, 1.0)):
                for h in range(2):
                    nc.vector.memset(m[half[h], D * h:D * h + D], v).then_inc(mats, 1)
                    nc.vector.memset(m[half[h], D * (1 - h):D * (1 - h) + D], 0.0).then_inc(mats, 1)
            dve.wait_ge(mats, 8)
            dve.wait_ge(id_ready, 2)
            nc.vector.tensor_tensor(center_mat[:, :], ident[:, :], mean_mat[:, :], ALU.subtract).then_inc(mats, 1)
            for i, (dst, src) in enumerate(((w2T[:, :], TB[0][:, 0:P]), (w4T[:, :], TB[1][:, 0:D]),
                                            (cols[:, 0:NV], TB[2][:, 0:NV]), (cols[:, NV:NV + NBN], TB[3][:, 0:NBN]))):
                dve.wait_ge(setup_mm, i + 1)
                nc.vector.tensor_copy(dst, src).then_inc(setup_out, 1)
            dve.wait_ge(setup_out, 4)
            nc.vector.tensor_scalar(neg_bf, col("bgf"), -1.0, None, ALU.mult).then_inc(derived, 1)
            nc.vector.tensor_scalar(bias_i, col("bgi"), col("input_bias"), 0.1, ALU.add, ALU.mult).then_inc(derived, 1)
            nc.vector.tensor_scalar(neg_bo, col("bgo"), -1.0, None, ALU.mult).then_inc(derived, 1)
            nc.vector.tensor_tensor(a_bias, col("tok_b1"), col("tok_b2"), ALU.add).then_inc(derived, 1)
            nc.vector.scalar_tensor_tensor(out=c_bias, in0=col("tok_b4"), scalar=2.0, in1=col("tok_b3"),
                                           op0=ALU.mult, op1=ALU.add).then_inc(derived, 1)
            nc.vector.tensor_scalar(out_scale, col("norm_scale"), RMS_SCALE ** 0.5, None, ALU.mult)\
                .then_inc(derived, 1)
            dve.wait_ge(cleared, 6)
            dve.wait_ge(mask_ready, 3)

            def add(it, k, js):
                for i, j in enumerate(js):
                    dve.wait_ge(s["mix_mm"], 28 * it + 4 * k + i + 1)
                    nc.vector.tensor_tensor(Z[:, tc(j)], TB[j][:, :], A[:, tc(j)], ALU.add).then_inc(s["mix_add"], 1)

            def start(it, js):
                for i in js:
                    j = JS[i]
                    dve.wait_ge(s["ac_mm"], 4 * it + i + 1)
                    nc.vector.tensor_copy(CT[half[j // 2], 512 * (j % 2):512 * (j % 2) + 512], TB[j][half[1], :])\
                        .then_inc(s["c_out"], 1)
                    dve.wait_ge(s["a_out"], 8 * it + 2 * i + 2)
                    nc.vector.tensor_scalar(U3[:, 2 * j:2 * j + 2, 1:UW], A3[:, 2 * j:2 * j + 2, :], 0.0, None,
                                            ALU.max).then_inc(s["u0_out"], 1)

            def scores(a, bs):
                for bb in bs:
                    dve.wait_ge(s["at_mm"], GB * a + bb + 1)
                    nc.vector.tensor_tensor(AT[:, bb, :], QB[SCORE_BANK[bb]][:, 0:3 * C], causal[:, :], ALU.mult)\
                        .then_inc(s["at_out"], 1)

            def turn(it, mix, att, late):
                a, l = it - 1, it - 2
                if mix:
                    dve.wait_ge(s["fin_add"], 2 * it)
                    start(it, (0, 1))
                if att:
                    dve.wait_ge(s["nn_out"], SB * a)
                    for h in range(2):
                        dve.wait_ge(s["sq_out"], 2 * a + h + 1)
                        nc.vector.tensor_copy(XC_IS[:, hs(h)], QB[h][:, :]).then_inc(s["xc_out"], 1)
                if mix:
                    start(it, (2, 3))
                    add(it, 0, JS)
                if att:
                    for h in range(2):
                        dve.wait_ge(s["xc_out"], 2 * a + h + 1)
                        dve.wait_ge(s["rs_out"], 2 * a + h + 1)
                        nc.vector.tensor_tensor(XC_IS[:, hs(h)], XC_IS[:, hs(h)], RS_FS[:, hs(h)], ALU.mult)\
                            .then_inc(s["xn_out"], 1)
                if late:
                    dve.wait_ge(s["xn2_out"], 2 * l)
                    for h in range(2):
                        dve.wait_ge(s["den_out"], l + 1)
                        dve.wait_ge(s["rms_mm"], 2 * l + h + 1)
                        nc.vector.tensor_tensor(RSL[:, hs(h)], QB[2 + h][:, :], K_NN[:, hs(h)], ALU.add)\
                            .then_inc(s["rms_add"], 1)
                if mix:
                    add(it, 1, JS)
                if att:
                    if late:
                        dve.wait_ge(s["rms_add"], 2 * l + 2)
                    for h in range(2):
                        dve.wait_ge(s["proj_mm"], 12 * a + 4 + h + 1)
                        nc.vector.tensor_scalar(K_NN[:, hs(h)], QB[2 + h][:, :], col("bk"), 1.0 / 8.0, ALU.add,
                                                ALU.mult).then_inc(s["k_out"], 1)
                    for h in range(2):
                        dve.wait_ge(s["proj_mm"], 12 * a + 6 + h + 1)
                        nc.vector.tensor_scalar(Q[:, hs(h)], QB[h][:, :], col("bq"), None, ALU.add)\
                            .then_inc(s["q_out"], 1)
                    dve.wait_ge(s["i_out"], 2 * a + 2)
                    nc.vector.tensor_scalar(LI[:, :], LI[:, :], 10.0, None, ALU.mult).then_inc(s["li_out"], 1)
                    dve.wait_ge(s["f_log"], a + 1)
                    nc.vector.scalar_tensor_tensor(out=LF_UT[:, :], in0=LF_UT[:, :], scalar=0.0, in1=SQ[:, :],
                                                   op0=ALU.min, op1=ALU.subtract).then_inc(s["lf_out"], 1)
                    dve.wait_ge(s["lf_out"], a + 1)
                    dve.wait_ge(s["li_out"], a + 1)
                    for n in range(SB):
                        nc.vector.tensor_tensor_scan(M3[:, n, 1:UW], LF_UT[:, T * n:T * n + T], LI[:, T * n:T * n + T],
                                                     0.0, ALU.add, ALU.max).then_inc(s["m_out"], 1)
                if mix:
                    add(it, 2, JS)
                if late:
                    for h in range(2):
                        dve.wait_ge(s["y_out"], 2 * l + h + 1)
                        nc.vector.scalar_tensor_tensor(out=hh(l, h), in0=RSL[:, hs(h)], scalar=out_scale,
                                                       in1=hh(l, h), op0=ALU.mult, op1=ALU.add)\
                            .then_inc(s["h2_out"], 1)
                if mix:
                    add(it, 3, JS)
                if att:
                    scores(a, range(0, 4))
                    dve.wait_ge(s["lf2_out"], a + 1)
                    for c in range(GB):
                        nc.vector.tensor_tensor_scan(NC_[:, C * c:C * c + C], LF_UT[:, C * c:C * c + C], zeros[:, :],
                                                     0.0, ALU.add, ALU.min).then_inc(s["nc_out"], 1)
                    dve.wait_ge(s["nc_out"], GB * a + GB)
                    dve.wait_ge(s["nd_out"], a)
                    dve.wait_ge(s["ends_kept"], a)
                    dve.wait_ge(s["lam_in"], 2 * a)
                    nc.vector.tensor_copy(ends[:, :].unsqueeze(2), NC3[:, :, C - 1:C]).then_inc(s["ends_out"], 1)
                    dve.wait_ge(s["ends_out"], a + 1)
                    nc.vector.scalar_tensor_tensor(out=NC3, in0=ends[:, :].unsqueeze(2).to_broadcast([P, GB, C]),
                                                   scalar=REF, in1=NC3, op0=ALU.mult, op1=ALU.subtract)\
                        .then_inc(s["nd_out"], 1)
                    nc.vector.tensor_scalar(lam[:, 0:GB:2], ends[:, 0:GB:2], 1.0 - REF, None, ALU.mult)\
                        .then_inc(s["lam_in"], 1)
                    nc.vector.tensor_scalar(lam[:, 1:GB:2], ends[:, 1:GB:2], REF, None, ALU.mult)\
                        .then_inc(s["lam_in"], 1)
                    nc.vector.tensor_copy(decay_ends[:, bass.ds(a * GB, GB)], ends[:, :]).then_inc(s["ends_kept"], 1)
                if mix:
                    add(it, 4, JS)
                if late:
                    for h in range(2):
                        dve.wait_ge(s["sq2_out"], 2 * l + h + 1)
                        nc.vector.tensor_copy(xn2(l, h), QB[2 + h][:, :]).then_inc(s["xc2_out"], 1)
                if att:
                    scores(a, range(4, 6))
                if mix:
                    add(it, 5, JS)
                if att:
                    dve.wait_ge(s["o_log"], a + 1)
                    nc.vector.scalar_tensor_tensor(out=EO[:, :], in0=EO[:, :], scalar=0.0, in1=SQ[:, :],
                                                   op0=ALU.max, op1=ALU.add).then_inc(s["sp_out"], 1)
                    dve.wait_ge(s["fs_out"], a + 1)
                    dve.wait_ge(s["ik_out"], a + 1)
                    dve.wait_ge(s["kz_out"], 2 * a + 2)
                    for n in range(SB):
                        r = slice(T * n, T * n + T)
                        nc.vector.tensor_tensor_scan(K_NN[:, r], RS_FS[:, r], XC_IS[:, r], 0.0, ALU.mult, ALU.add)\
                            .then_inc(s["nn_out"], 1)
                if att:
                    scores(a, range(6, 8))
                if mix:
                    add(it, 6, JS_LAST)
                if late:
                    for h in range(2):
                        dve.wait_ge(s["xc2_out"], 2 * l + h + 1)
                        dve.wait_ge(s["rs2_out"], 2 * l + h + 1)
                        nc.vector.tensor_tensor(xn2(l, h), xn2(l, h), RSL[:, hs(h)], ALU.mult)\
                            .then_inc(s["xn2_out"], 1)
                if att:
                    dve.wait_ge(s["den_sq"], 2 * a + 2)
                    nc.vector.tensor_scalar(K_NN[:, :], K_NN[:, :], 1e-12, RMS_EPS, ALU.max, ALU.mult)\
                        .then_inc(s["den_out"], 1)
                if att:
                    if late:
                        dve.wait_ge(s["y_out"], 2 * l + 2)
                    for n in range(SB):
                        dve.wait_ge(s["tmp_out"], SB * a + n + 1)
                        nc.vector.scalar_tensor_tensor(out=HR3[:, n, C:T], in0=SQ[:, C * n:C * n + C],
                                                       scalar=lam[:, 2 * n + 1:2 * n + 2], in1=QB[n][:, T:T + C],
                                                       op0=ALU.mult, op1=ALU.add).then_inc(s["hr_a"], 1)
                        nc.vector.tensor_copy(HR3[:, n, 0:C], QB[n][:, 0:C]).then_inc(s["hr_out"], 1)
                if mix:
                    for h in range(2):
                        dve.wait_ge(s["fin_mm"], 2 * it + h + 1)
                        nc.vector.tensor_tensor(Z[:, hs(h)], TB[h][:, :], CT[:, hs(h)], ALU.add)\
                            .then_inc(s["fin_add"], 1)
                if att:
                    dve.wait_ge(s["et_out"], a + 1)
                    for h in range(2):
                        dve.wait_ge(s["hr_out"], SB * a + 2 * h + 2)
                        dve.wait_ge(s["hr_a"], SB * a + 2 * h + 2)
                        nc.vector.tensor_tensor(HR[:, hs(h)], HR[:, hs(h)], EO[:, hs(h)], ALU.mult)\
                            .then_inc(s["o_h"], 1)

            turn(0, True, False, False)
            turn(1, True, True, False)
            turn(2, True, True, True)
            with dve.Fori(3, G) as it:
                turn(it, True, True, True)
            turn(G, False, True, True)
            turn(G + 1, False, False, True)

            dve.wait_ge(bn_rs, 1)
            for i, (gn, bn, mn) in enumerate((("g1", "b1", "m1"), ("g2", "b2", "m2"))):
                nc.vector.tensor_tensor(bn_s[:, i, :], bn_s[:, i, :], bn_cols(gn), ALU.mult).then_inc(bn_ready, 1)
                nc.vector.tensor_tensor(bn_t[:, i, :], bn_cols(bn), bn_cols(mn), ALU.subtract).then_inc(bn_ready, 1)
            dve.wait_ge(bn_ready, 4)
            nc.vector.tensor_tensor(bn_t[:, :, :], bn_t[:, :, :], bn_s[:, :, :], ALU.mult).then_inc(bn_ready, 1)
            dve.wait_ge(bn_ready, 5)
            for i, ben in enumerate(("be1", "be2")):
                nc.vector.tensor_tensor(bn_t[:, i, :], bn_t[:, i, :], bn_cols(ben), ALU.add).then_inc(bn_ready, 1)
            dve.wait_ge(ffn_loaded, 16 * N_FFN)
            nc.vector.tensor_scalar(wr[:, :], wr[:, :], 1.0 / NB, None, ALU.mult).then_inc(bn_ready, 1)

            for t in range(2):
                dve.wait_ge(b["lg_mm"], t + 1)
                nc.vector.tensor_reduce(wmx[:, t:t + 1], QB[t][:, 0:E], AX_X, ALU.max).then_inc(b["mx"], 1)
            dve.wait_ge(b["mx"], 2)
            nc.vector.tensor_scalar(wmx, wmx, -1.0, None, ALU.mult).then_inc(b["nmx"], 1)
            dve.wait_ge(b["ex"], 2)
            nc.vector.reciprocal(wrc, wsm).then_inc(b["rc"], 1)
            dve.wait_ge(b["rc"], 1)
            for t in range(2):
                nc.vector.tensor_scalar(wn[:, t, :], wx[:, t, :], wrc[:, t:t + 1], None, ALU.mult)\
                    .then_inc(b["wn"], 1)
            for t in range(2):
                dve.wait_ge(b["wn"], t + 1)
                nc.vector.tensor_copy(wb[:, t, :].rearrange("p (e c) -> p e c", c=D),
                                      wn[:, t, :].unsqueeze(2).to_broadcast([P, E, D])).then_inc(b["wb"], 1)
            dve.wait_ge(b["w_mm"], 1)
            for p in range(EP):
                nc.vector.tensor_copy(WM[:, p, :], TB[p][:, 0:T]).then_inc(b["w_out"], 1)
            dve.wait_ge(b["wt_mm"], 1)
            nc.vector.tensor_copy(wt, QB[2][0:E, 0:T]).then_inc(b["wt_out"], 1)
            dve.wait_ge(b["bo_mm"], 1)
            nc.vector.tensor_copy(BOW, QB[3][:, 0:T]).then_inc(b["bo_out"], 1)

            def weigh(g, t):
                for k in range(2):
                    dve.wait_ge(b["h2"], 16 * g + 2 * t + k + 1)
                    v = rowsof(H2[t % 2][:, k, :])
                    nc.vector.tensor_tensor(v, v, WM[:, t % EP, :].unsqueeze(1).to_broadcast([P, 2, T]), ALU.mult)\
                        .then_inc(b["hw"], 1)

            def finish(g, f):
                dve.wait_ge(b["l3_mm"], 2 * g + f + 1)
                dve.wait_ge(b["res_a"], 2 * g + f + 1)
                after(dve, b["tr_mm"], 2 * g - 1 + f)
                nc.vector.tensor_tensor(RES[f], QB[f][:, :], R1[f], ALU.add).then_inc(b["res"], 1)

            def token_major(g, f):
                dve.wait_ge(b["tr_mm"], 2 * g + f + 1)
                dve.wait_ge(stored[f], 32 * g)
                for k in range(2):
                    nc.vector.tensor_copy(OUTT[f][:, k].rearrange("p n (r d) -> p (n r) d", r=2),
                                          QB[2 + f][:, :].rearrange("p (m k d) -> p m k d", k=2, d=D)[:, :, k, :])\
                        .then_inc(b["tr_out"], 1)

            def experts(g, first=False):
                for t in range(2 * EP):
                    weigh(g, t)
                    if t == 1 and not first:
                        finish(g - 1, 1)
                    if t == 3 and not first:
                        token_major(g - 1, 1)
                    if t == EP + 1:
                        finish(g, 0)
                    if t == EP + 3:
                        token_major(g, 0)

            experts(0, True)
            with dve.Fori(1, G) as g:
                experts(g)
            finish(G - 1, 1)
            token_major(G - 1, 1)


_INS = ["x", "tok_W1", "tok_b1", "tok_W2", "tok_b2", "tok_W3", "tok_b3", "tok_W4", "tok_b4",
        "attn_Wq", "attn_bq", "attn_Wk", "attn_bk", "attn_Wv", "attn_bv", "attn_Wg", "attn_bg",
        "attn_input_bias", "attn_norm_scale", "ffn_Wr", "ffn_br", "ffn_W1", "ffn_b1", "ffn_g1", "ffn_be1",
        "ffn_m1", "ffn_v1", "ffn_W2", "ffn_b2", "ffn_g2", "ffn_be2", "ffn_m2", "ffn_v2", "ffn_Wo", "ffn_bo"]


def kernel(**inputs):
    import numpy as np
    import concourse.bacc as bacc
    from concourse.bass_utils import run_bass_kernel_spmd as run

    nc = bacc.Bacc("TRN2", target_bir_lowering=False, num_devices=1)
    arrays, args = {}, []
    for name in _INS:
        a = np.ascontiguousarray(inputs[name if name == "x" else "L0_" + name])
        arrays["in_" + name] = a
        args.append(nc.dram_tensor("in_" + name, a.shape, mybir.dt.from_np(a.dtype), kind="ExternalInput").ap())
    result = nc.dram_tensor("result", (NB, T, D), F32, kind="ExternalOutput").ap()
    build(nc, *args, result)
    r = run(nc, [arrays], core_ids=[0])
    return r.results[0]["result"]
```

```python
from contextlib import ExitStack

import concourse.bass as bass
from concourse import mybir

F32 = mybir.dt.float32
ALU = mybir.AluOpType
ACT = mybir.ActivationFunctionType
AX_X = mybir.AxisListType.X

P = 128
D = 64
T = 256
NB = 64
GB = 8
SB = GB // 2
G = NB // GB
PC = SB * T
HC = PC // 2
C = 128
REF = 0.45
E = 8
LN_EXP, LN, EXP_TANH = "natural_log_exp_and_others", "natural_log", "exp_and_others"
EP = E // 2
UW = T + 1
FC = 512
NFC = NB // 2 * T // FC
TOK_EPS, RMS_EPS, BN_EPS = 1e-5, 1e-8, 1e-3
ROWS = ["tok_b1", "tok_b2", "tok_b3", "tok_b4", "bq", "bk", "bv", "bgi", "bgf", "bgo", "input_bias", "norm_scale"]
BN_ROWS = ["b1", "g1", "be1", "m1", "v1", "b2", "g2", "be2", "m2", "v2"]
NM, NV, NBN = 4, len(ROWS), len(BN_ROWS) * EP
SCORE_BANK = (0, 1, 2, 3, 0, 1, 0, 1)
JS = (2, 3, 0, 1)
JS_LAST = (2, 0, 3, 1)
WIDEST = -140.0
N_WARM = 14
RMS_SCALE = 2.0 ** 40


def build(nc, x, tok_W1, tok_b1, tok_W2, tok_b2, tok_W3, tok_b3, tok_W4, tok_b4, Wq, bq, Wk, bk, Wv, bv,
          Wg, bg, input_bias, norm_scale, Wr, br, W1, b1, g1, be1, m1, v1, W2, b2, g2, be2, m2, v2, Wo, bo, out):
    with ExitStack() as ctx:
        def sb(name, shape):
            return ctx.enter_context(nc.sbuf_tensor(name, shape, F32))

        def sem(name):
            return ctx.enter_context(nc.semaphore(name))

        ident = sb("ident", [P, P])
        mean_mat = sb("mean_mat", [P, P])
        center_mat = sb("center_mat", [P, P])
        sum_mat = sb("sum_mat", [P, P])
        causal = sb("causal", [P, 3 * C])
        cols = sb("cols", [P, NV + NBN])
        wac = sb("wac", [4, P])
        w2T = sb("w2T", [P, P])
        w4T = sb("w4T", [P, D])
        wproj = sb("wproj", [P, 6, P])
        fw1 = sb("fw1", [P, 2, EP, P])
        fw2 = sb("fw2", [P, EP, P])
        fwo = sb("fwo", [P, EP, D])
        wr = sb("wr", [P, E])
        br_row = sb("br_row", [1, E])
        ones_row = sb("ones_row", [1, P])
        bo_w = sb("bo_w", [E, P])
        col2 = sb("col2", [P, 8])
        bn_s = sb("bn_s", [P, 2, EP])
        bn_t = sb("bn_t", [P, 2, EP])

        HH = sb("HH", [P, NB // 2 * T])
        XN2 = sb("XN2", [P, NB // 2 * T])
        feat = sb("feat", [P, T])
        decay_ends = sb("decay_ends", [P, G * GB])

        X = sb("X", [4, GB * T])
        A = sb("A", [P, GB * T])
        CT = sb("CT", [P, PC])
        Z = sb("Z", [P, GB * T])
        U = sb("U", [P, GB * UW])
        UF = sb("UF", [P, GB * UW])

        SQ = sb("SQ", [P, PC])
        XC_IS = sb("XC_IS", [P, PC])
        RS_FS = sb("RS_FS", [P, PC])
        LF_UT = sb("LF_UT", [P, PC])
        LI = sb("LI", [P, PC])
        K_NN = sb("K_NN", [P, PC])
        KZ = sb("KZ", [P, 2, PC])
        Q = sb("Q", [P, PC])
        V = sb("V", [P, PC])
        EO = sb("EO", [P, PC])
        M = sb("M", [P, SB * UW])
        NC_ = sb("NC_", [P, PC])
        HR = sb("HR", [P, PC])
        AT = sb("AT", [P, GB, 3 * C])
        ends = sb("ends", [P, GB])
        lam = sb("lam", [P, GB])
        SQL = sb("SQL", [P, PC])
        RSL = sb("RSL", [P, PC])
        zeros = sb("zeros", [P, C])
        side = sb("side", [P, 2])

        wide_f = sb("wide_f", [P, 2])
        wide_i = ctx.enter_context(nc.sbuf_tensor("wide_i", [1, 1], mybir.dt.int32))

        sel = RSL[:, HC:HC + P]
        vk, m_row, mq = SQL[:, 0:HC], SQL[:, HC:PC], RSL[:, 0:HC]

        mix_rows = SQL[0:NM, 0:P]
        att_rows = SQL[0:NV - NM, 2 * P:3 * P]
        bn_rows = SQL[0:NBN, P:2 * P]
        w2_raw = RSL[:, 0:P]
        w4_raw = RSL[0:D, P:2 * P]

        H1 = [A[:, 0:1024].rearrange("p (s c) -> p s c", s=2), A[:, 1024:2048].rearrange("p (s c) -> p s c", s=2)]
        H2 = [Z[:, 0:1024].rearrange("p (s c) -> p s c", s=2), Z[:, 1024:2048].rearrange("p (s c) -> p s c", s=2)]
        H2_AHEAD = [CT[:, :], Z[:, 1024:2048], U[:, 0:1024], KZ[:, 0, :], KZ[:, 1, :], RS_FS[:, :], Z[:, 0:1024]]
        H2_AHEAD = [v.rearrange("p (s c) -> p s c", s=2) for v in H2_AHEAD]
        WM = AT[:, 0:4, 0:T]
        BOW = LF_UT[:, 0:T]
        wb = K_NN[:, :].rearrange("p (t c) -> p t c", t=2)
        wn = M[:, 0:16].rearrange("p (t e) -> p t e", t=2)
        wx = M[:, 16:32].rearrange("p (t e) -> p t e", t=2)
        wmx, wsm, wrc = M[:, 32:34], M[:, 34:36], M[:, 36:38]
        wt = Q[0:E, 0:T]
        R1 = [SQ[:, 0:512], SQ[:, 512:1024]]
        RES = [XC_IS[:, 0:512], XC_IS[:, 512:1024]]
        OUTT = [V[:, 512 * f:512 * f + 512].rearrange("p (s n c) -> p s n c", s=2, n=2) for f in range(2)]

        TB = [ctx.enter_context(nc.psum_tensor(f"TB{j}", [P, 512], F32)) for j in range(4)]
        QB = [ctx.enter_context(nc.psum_tensor(f"QB{j}", [P, 512], F32)) for j in range(4)]

        U3 = U[:, :].rearrange("p (n c) -> p n c", c=UW)
        UF3 = UF[:, :].rearrange("p (n c) -> p n c", c=UW)
        A3 = A[:, :].rearrange("p (n c) -> p n c", c=T)
        Z3 = Z[:, :].rearrange("p (n c) -> p n c", c=T)
        M3 = M[:, :].rearrange("p (n c) -> p n c", c=UW)
        NC3 = NC_[:, :].rearrange("p (n c) -> p n c", c=C)
        HR3 = HR[:, :].rearrange("p (n c) -> p n c", c=T)
        half = [slice(0, D), slice(D, P)]

        def hs(h):
            return slice(HC * h, HC * h + HC)

        def tc(j):
            return slice(512 * j, 512 * j + 512)

        def rowsof(ap, c=T):
            return ap.rearrange("p (n c) -> p n c", c=c)

        def hh(a, h):
            return HH[:, bass.ds(a * PC + HC * h, HC)]

        def xn2(a, h):
            return XN2[:, bass.ds(a * PC + HC * h, HC)]

        def col(name):
            i = ROWS.index(name)
            return cols[:, i:i + 1]

        def bn_cols(name):
            i = NV + BN_ROWS.index(name) * EP
            return cols[:, i:i + EP]

        neg_bf, bias_i, neg_bo, a_bias, c_bias, out_scale = (col2[:, i:i + 1] for i in range(6))

        mix_loaded = sem("mix_loaded")
        bn_loaded = sem("bn_loaded")
        att_loaded = sem("att_loaded")
        ffn_loaded = sem("ffn_loaded")
        x_in = sem("x_in")
        w_cleared = sem("w_cleared")
        cleared = sem("cleared")
        id_ready = sem("id_ready")
        mask_ready = sem("mask_ready")
        mats = sem("mats")
        side_ready = sem("side_ready")
        setup_mm = sem("setup_mm")
        setup_out = sem("setup_out")
        derived = sem("derived")
        bn_ln = sem("bn_ln")
        bn_rs = sem("bn_rs")
        bn_ready = sem("bn_ready")
        s = {n: sem(n) for n in (
            "ac_mm", "a_out", "c_out", "u0_out", "mix_relu", "mix_mm", "mix_add", "uf_out", "fin_mm", "fin_add", "h1_out",
            "lnc_mm", "sq_out", "xc_out", "var_mm", "rs_ln", "rs_out", "xn_out",
            "proj_mm", "f_out", "i_out", "k_out", "q_out", "v_out", "o_out", "kz_out",
            "f_abs", "f_exp", "f_log", "lf_out", "li_out", "m_out", "t1_out", "lf2_out", "lg_out",
            "o_abs", "o_exp", "o_log", "sp_out", "ee_out", "et_out",
            "fs_out", "is_out", "nc_out", "ends_out", "nd_out", "ar_out", "eu_out", "u_out", "lam_in", "lam_out",
            "ends_kept", "ik_out", "nn_out", "nq_out", "den_mm", "den_sq", "den_out",
            "at_mm", "at_out", "ut_mm", "ut_out", "av_mm", "tmp_out", "hr_a", "hr_out", "o_h",
            "sqo_out", "rms_mm", "rms_add", "rr_ln", "rr_out", "y_out", "h2_out",
            "l2c_mm", "sq2_out", "xc2_out", "var2_mm", "rs2_ln", "rs2_out", "xn2_out", "feat_out")}
        b = {n: sem("b_" + n) for n in (
            "lg_mm", "mx", "nmx", "ex", "rc", "wn", "wb", "w_mm", "w_out", "wt_mm", "wt_out", "bo_mm", "bo_out",
            "l1_mm", "h1", "l2_mm", "h2", "hw", "l3_mm", "res_a", "res", "tr_mm", "tr_out")}
        stored = [sem("b_stored0"), sem("b_stored1")]

        def after(engine, semaphore, count):
            if not isinstance(count, int) or count > 0:
                engine.wait_ge(semaphore, count)

        range_min, range_mm, range_all, wide_ready = (sem(n) for n in ("range_min", "range_mm", "range_all", "wide_ready"))
        feat_cleared, hr_cleared = sem("feat_cleared"), sem("hr_cleared")
        rec, bcast_mm = sem("rec"), sem("bcast_mm")
        REC = 7

        ahead = {n: sem("ahead_" + n) for n in ("l1_mm", "h1", "l2_mm", "h2")}

        def settle(engine, it, mix, att, late):
            if mix:
                engine.wait_ge(s["feat_out"], SB * it)
            if att:
                engine.wait_ge(s["h1_out"], 2 * it)
            if late:
                engine.wait_ge(s["o_h"], 2 * it - 2)

        def plain_pass(engine, turn, prepare=None, again=None):
            engine.wait_ge(wide_ready, 1)
            wide = engine.value_load(wide_i[:, :], min_val=0, max_val=1)
            with engine.If(wide != 0):
                if prepare:
                    prepare()
                with engine.Fori(0, G) as g:
                    turn(g + G, True, False, False, True)
                    turn(g + (G + 1), False, True, False, True)
                    turn(g + (G + 2), False, False, True, True)
                engine.wait_ge(s["feat_out"], 2 * SB * G)
                if again:
                    for i in range(N_AHEAD + 1):
                        again(i, N_AHEAD)

        N_AHEAD = 2 * EP - 1
        N_MIX, N_ATT, N_FFN, N_BN = NM + 5, 18, 11, len(BN_ROWS)

        def load_rows(engine, name, v):
            i, n = ROWS.index(name), 3 if v is bg else 1
            dst, loaded = (mix_rows[i:i + n, :], mix_loaded) if i < NM else (att_rows[i - NM:i - NM + n, :], att_loaded)
            engine.dma_start(dst.rearrange("a (t d) -> a t d", t=2),
                             v.rearrange("(a t d) -> a t d", a=n, t=1).to_broadcast([n, 2, D]))\
                .then_inc(loaded, 16)

        block = ctx.enter_context(nc.Block())

        @block.sync
        def _(sp):
            def load_x(g):
                return sp.dma_start(X[:, :].rearrange("d (b l) -> d b l", l=T),
                                    x[bass.ds(g * GB, GB)].rearrange("b d l -> d b l"))

            with nc.allow_non_contiguous_dma(reason="weights of 64 x 4"):
                sp.dma_start(wac[:, 0:D], tok_W1.rearrange("o d -> d o")).then_inc(mix_loaded, 16)
                sp.dma_start(wac[:, D:P], tok_W3.rearrange("o d -> d o")).then_inc(mix_loaded, 16)
            for n, v in (("tok_b1", tok_b1), ("tok_b2", tok_b2), ("tok_b3", tok_b3), ("tok_b4", tok_b4)):
                load_rows(sp, n, v)
            load_x(0).then_inc(x_in, 16)
            sp.wait_ge(mix_loaded, 16 * N_MIX)
            sp.wait_ge(w_cleared, 2)
            for i, w in enumerate((Wg[:, D:2 * D], Wg[:, 0:D], Wk, Wq, Wv, Wg[:, 2 * D:3 * D])):
                for h in range(2):
                    sp.dma_start(wproj[half[h], i, D * h:D * h + D], w).then_inc(att_loaded, 16)

            for n, v in (("bq", bq), ("bk", bk), ("bv", bv), ("bgi", bg), ("input_bias", input_bias),
                         ("norm_scale", norm_scale)):
                load_rows(sp, n, v)

            with sp.Fori(1, G) as g:
                sp.wait_ge(s["ac_mm"], 4 * g)
                load_x(g).then_inc(x_in, 16)

            sp.wait_ge(wide_ready, 1)
            wide = sp.value_load(wide_i[:, :], min_val=0, max_val=1)
            with sp.If(wide != 0):
                with sp.Fori(0, G) as g:
                    sp.wait_ge(s["ac_mm"], 4 * (g + G))
                    load_x(g).then_inc(x_in, 16)

            ov = out.rearrange("(g s f n) (p r) d -> g s f p n (r d)", g=G, s=2, f=2, n=2, r=2)
            with sp.Fori(0, G) as g:
                for f in range(2):
                    for k in range(2):
                        sp.wait_ge(b["tr_out"], 4 * g + 2 * f + k + 1)
                        sp.dma_start(ov[bass.ds(g, 1), k, f].rearrange("a p n c -> (a p) n c"),
                                     OUTT[f][:, k]).then_inc(stored[f], 16)
            for f in range(2):
                sp.wait_ge(stored[f], 16 * 2 * G)

        @block.gpsimd
        def _(pool):
            nc.gpsimd.memset(w2_raw[:, :], 0.0).then_inc(w_cleared, 1)
            nc.gpsimd.memset(ident[:, :], 0.0).then_inc(id_ready, 1)
            pool.wait_ge(id_ready, 1)
            nc.gpsimd.affine_select(out=ident[:, :], in_=ident[:, :], compare_op=ALU.not_equal, fill=1.0, base=0,
                                    pattern=[[-1, P]], channel_multiplier=1).then_inc(id_ready, 1)
            nc.gpsimd.memset(wproj[:, :, :], 0.0).then_inc(w_cleared, 1)
            nc.gpsimd.memset(fw1[:, :, :, :], 0.0).then_inc(w_cleared, 1)
            nc.gpsimd.memset(fw2[:, :, :], 0.0).then_inc(w_cleared, 1)
            nc.gpsimd.memset(U3[:, :, 0:1], 0.0).then_inc(cleared, 1)
            nc.gpsimd.memset(UF[:, :], 0.0).then_inc(cleared, 1)
            nc.gpsimd.memset(M3[:, :, 0:1], 0.0).then_inc(cleared, 1)
            nc.gpsimd.memset(feat[:, :], 0.0).then_inc(cleared, 1)
            nc.gpsimd.memset(zeros[:, :], 0.0).then_inc(cleared, 1)
            nc.gpsimd.memset(ones_row[:, :], 1.0).then_inc(cleared, 1)
            nc.gpsimd.memset(causal[:, :], 1.0).then_inc(mask_ready, 1)
            pool.wait_ge(mask_ready, 1)
            for c in (0, 2):
                v = causal[:, C * c:C * c + C]
                nc.gpsimd.affine_select(out=v, in_=v, compare_op=ALU.is_ge, fill=0.0, base=0,
                                        pattern=[[1, C]], channel_multiplier=-1).then_inc(mask_ready, 1)
            pool.wait_ge(w_cleared, 4)
            for i, v in enumerate((b1, g1, be1, m1, v1, b2, g2, be2, m2, v2)):
                pool.dma_start(bn_rows[i * EP:(i + 1) * EP, :],
                               v.rearrange("(p e) h -> p (e h)", e=2)).then_inc(bn_loaded, 16)
            w2v = W2.rearrange("(p two) h k -> two h p k", two=2)
            wov = Wo.rearrange("(p two) h d -> two h p d", two=2)
            for h in range(2):
                pool.dma_start(fw1[half[h], h, :, :].rearrange("d p (e h) -> d (p e) h", e=2),
                               W1.rearrange("e d h -> d e h")).then_inc(ffn_loaded, 16)
                pool.dma_start(fw2[half[h], :, D * h:D * h + D], w2v[h]).then_inc(ffn_loaded, 16)
                pool.dma_start(fwo[half[h], :, :], wov[h]).then_inc(ffn_loaded, 16)
                pool.dma_start(wr[half[h], :], Wr).then_inc(ffn_loaded, 16)
                pool.dma_start(bo_w[:, D * h:D * h + D], bo).then_inc(ffn_loaded, 16)
            pool.dma_start(br_row[:, :], br.rearrange("(a e) -> a e", a=1)).then_inc(ffn_loaded, 16)

            pool.wait_ge(cleared, 6)
            pool.wait_ge(side_ready, 4)

            def turn(it, att, late, plain=False):
                a, l = it - 1, it - 2
                gl = l - G if plain else l
                if plain:
                    settle(pool, it, False, att, late)
                if att:
                    pool.wait_ge(s["k_out"], 2 * a + 2)
                    if not plain:
                        pool.wait_ge(s["at_mm"], GB * a)
                    for k in range(2):
                        nc.gpsimd.tensor_tensor(KZ[:, k, :], K_NN[:, :], side[:, k:k + 1].to_broadcast([P, PC]),
                                                ALU.mult).then_inc(s["kz_out"], 1)
                if late:
                    for h in range(2):
                        pool.wait_ge(s["rr_out"], 2 * l + h + 1)
                        nc.gpsimd.tensor_tensor(RSL[:, hs(h)], HR[:, hs(h)], RSL[:, hs(h)], ALU.mult)\
                            .then_inc(s["y_out"], 1)
                if att:
                    pool.wait_ge(s["m_out"], SB * a + SB)
                    nc.gpsimd.tensor_tensor(rowsof(LF_UT[:, :]), rowsof(LF_UT[:, :]), M3[:, :, 0:T], ALU.add)\
                        .then_inc(s["t1_out"], 1)
                    pool.wait_ge(s["t1_out"], a + 1)
                    nc.gpsimd.tensor_tensor(rowsof(LF_UT[:, :]), rowsof(LF_UT[:, :]), M3[:, :, 1:UW], ALU.subtract)\
                        .then_inc(s["lf2_out"], 1)
                    nc.gpsimd.tensor_tensor(rowsof(LI[:, :]), rowsof(LI[:, :]), M3[:, :, 1:UW], ALU.subtract)\
                        .then_inc(s["lg_out"], 1)
                    pool.wait_ge(s["is_out"], a + 1)
                    pool.wait_ge(s["nd_out"], a + 1)
                    nc.gpsimd.tensor_tensor(LI[:, :], LI[:, :], NC_[:, :], ALU.add).then_inc(s["ar_out"], 1)
                    nc.gpsimd.tensor_tensor(XC_IS[:, :], XC_IS[:, :], K_NN[:, :], ALU.mult).then_inc(s["ik_out"], 1)
                    for h in range(2):
                        pool.wait_ge(s["eu_out"], a + 1)
                        pool.wait_ge(s["v_out"], 2 * a + h + 1)
                        nc.gpsimd.tensor_tensor(V[:, hs(h)], V[:, hs(h)], LI[:, hs(h)], ALU.mult)\
                            .then_inc(s["u_out"], 1)
                    for h in range(2):
                        pool.wait_ge(s["nn_out"], SB * a + 2 * h + 2)
                        nc.gpsimd.tensor_tensor(K_NN[:, hs(h)], K_NN[:, hs(h)], Q[:, hs(h)], ALU.mult)\
                            .then_inc(s["nq_out"], 1)
                    pool.wait_ge(s["sp_out"], a + 1)
                    nc.gpsimd.tensor_tensor(EO[:, :], EO[:, :], NC_[:, :], ALU.add).then_inc(s["ee_out"], 1)
                if late:
                    for n in range(SB):
                        pool.wait_ge(s["xn2_out"], 2 * l + n // 2 + 1)
                        pool.wait_ge(s["feat_out"], SB * l + n)
                        nc.gpsimd.tensor_tensor(feat[:, :], feat[:, :], XN2[:, bass.ds(gl * PC + T * n, T)], ALU.add)\
                            .then_inc(s["feat_out"], 1)

            turn(1, True, False)
            turn(2, True, True)
            with pool.Fori(3, G + 1) as it:
                turn(it, True, True)
            turn(G + 1, False, True)

            def plain_turn(it, mix, att, late, plain):
                if att or late:
                    turn(it, att, late, plain)

            def clear_feat():
                pool.wait_ge(s["feat_out"], SB * G)
                pool.wait_ge(ahead["h2"], 2 * N_AHEAD)
                nc.gpsimd.memset(feat[:, :], 0.0).then_inc(feat_cleared, 1)
                nc.gpsimd.memset(U3[:, :, 0:1], 0.0).then_inc(feat_cleared, 1)
                pool.wait_ge(feat_cleared, 2)

            plain_pass(pool, plain_turn, clear_feat)

            pool.wait_ge(b["bo_out"], 1)
            def residual(g):
                for f in range(2):
                    after(pool, b["res"], 2 * g - 1 + f)
                    nc.gpsimd.tensor_tensor(rowsof(R1[f]), rowsof(hh(g, f)),
                                            BOW.unsqueeze(1).to_broadcast([P, 2, T]), ALU.add).then_inc(b["res_a"], 1)

            residual(0)
            with pool.Fori(1, G) as g:
                residual(g)

        @block.scalar
        def _(act):
            act.wait_ge(w_cleared, 1)
            for h in range(2):
                act.dma_start(w2_raw[half[h], D * h:D * h + D], tok_W2).then_inc(mix_loaded, 16)
            act.dma_start(w4_raw.rearrange("o (t d) -> o t d", t=2),
                          tok_W4.rearrange("o (t d) -> o t d", t=1).to_broadcast([D, 2, D])).then_inc(mix_loaded, 16)
            nc.scalar.preload_act_table_set(LN_EXP)
            act.wait_ge(derived, 2)

            def inputs(it, js):
                for i in js:
                    j = JS[i]
                    act.wait_ge(s["ac_mm"], 4 * it + i + 1)
                    nc.scalar.activation(A3[half[0], 2 * j:2 * j + 2, :], rowsof(TB[j][half[0], :]), ACT.Identity,
                                         bias=a_bias[half[0], :]).then_inc(s["a_out"], 1)
                    nc.scalar.activation(A3[half[1], 2 * j:2 * j + 2, ::-1], rowsof(TB[j][half[0], :]), ACT.Identity,
                                         bias=a_bias[half[0], :]).then_inc(s["a_out"], 1)

            def relu(it, k, js):
                for i in js:
                    j = JS[i]
                    act.wait_ge(s["mix_add"], 28 * it + 4 * k + i + 1)
                    nc.scalar.activation(U3[:, 2 * j:2 * j + 2, 1:UW], Z3[:, 2 * j:2 * j + 2, :], ACT.Relu)\
                        .then_inc(s["mix_relu"], 1)

            def last_relu(it, js):
                for i in js:
                    j = JS_LAST[i]
                    act.wait_ge(s["mix_add"], 28 * it + 24 + i + 1)
                    nc.scalar.activation(UF3[half[0], 2 * j:2 * j + 2, 1:T], Z3[half[0], 2 * j:2 * j + 2, 0:T - 1],
                                         ACT.Relu).then_inc(s["uf_out"], 1)
                    nc.scalar.activation(UF3[half[1], 2 * j:2 * j + 2, 0:T - 1],
                                         Z3[half[1], 2 * j:2 * j + 2, T - 2::-1], ACT.Relu).then_inc(s["uf_out"], 1)

            def ahead_step(i, done=0):
                if i < N_AHEAD:
                    for k in range(2):
                        act.wait_ge(ahead["l1_mm"], 2 * (done + i) + k + 1)
                        nc.scalar.activation(H1[i % 2][:, k, :], TB[k][:, :], ACT.Relu,
                                             bias=bn_t[:, 0, i % EP:i % EP + 1],
                                             scale=bn_s[:, 0, i % EP:i % EP + 1]).then_inc(ahead["h1"], 1)
                if i > 0:
                    j = i - 1
                    for k in range(2):
                        act.wait_ge(ahead["l2_mm"], 2 * (done + j) + k + 1)
                        nc.scalar.activation(H2_AHEAD[j][:, k, :], TB[2 + k][:, :], ACT.Relu,
                                             bias=bn_t[:, 1, j % EP:j % EP + 1],
                                             scale=bn_s[:, 1, j % EP:j % EP + 1]).then_inc(ahead["h2"], 1)

            def turn(it, mix, att, late, plain=False):
                a, l = it - 1, it - 2
                gm, ga, gl = (it - G, a - G, l - G) if plain else (it, a, l)
                last = isinstance(it, int) and it == G
                last_late = isinstance(it, int) and it == G + 1
                if plain:
                    settle(act, it, mix, att, late)
                if mix:
                    inputs(it, (0, 1))
                if att:
                    for h in range(2):
                        act.wait_ge(s["lnc_mm"], 2 * a + h + 1)
                        nc.scalar.activation(SQ[:, hs(h)], QB[h][:, :], ACT.Square).then_inc(s["sq_out"], 1)
                if last:
                    ahead_step(0)
                if mix:
                    inputs(it, (2, 3))
                if late:
                    for h in range(2):
                        act.wait_ge(s["o_h"], 2 * l + h + 1)
                        nc.scalar.activation(SQL[:, hs(h)], HR[:, hs(h)], ACT.Square).then_inc(s["sqo_out"], 1)
                if last_late:
                    ahead_step(5)
                if mix:
                    relu(it, 0, (0, 1))
                if att:
                    for h in range(2):
                        act.wait_ge(s["var_mm"], 2 * a + h + 1)
                        nc.scalar.activation(RS_FS[:, hs(h)], QB[h][:, :], ACT.Ln, bias=TOK_EPS)\
                            .then_inc(s["rs_ln"], 1)
                    for h in range(2):
                        act.wait_ge(s["rs_ln"], 2 * a + h + 1)
                        nc.scalar.activation(RS_FS[:, hs(h)], RS_FS[:, hs(h)], ACT.Exp, scale=-0.5)\
                            .then_inc(s["rs_out"], 1)
                if last:
                    ahead_step(1)
                if mix:
                    relu(it, 0, (2, 3))
                if att:
                    nc.scalar.preload_act_table_set(EXP_TANH)
                if mix:
                    relu(it, 1, (0, 1))
                if att:
                    for h in range(2):
                        act.wait_ge(s["proj_mm"], 12 * a + h + 1)
                        nc.scalar.activation(LF_UT[:, hs(h)], QB[2 + h][:, :], ACT.Identity, bias=neg_bf, scale=-1.0)\
                            .then_inc(s["f_out"], 1)
                if mix:
                    relu(it, 1, (2, 3))
                if att:
                    for h in range(2):
                        act.wait_ge(s["proj_mm"], 12 * a + 2 + h + 1)
                        nc.scalar.activation(LI[:, hs(h)], QB[h][:, :], ACT.Tanh, bias=bias_i, scale=0.1)\
                            .then_inc(s["i_out"], 1)
                    act.wait_ge(s["f_out"], 2 * a + 2)
                    nc.scalar.activation(SQ[:, :], LF_UT[:, :], ACT.Abs).then_inc(s["f_abs"], 1)
                    act.wait_ge(s["f_abs"], a + 1)
                    nc.scalar.activation(SQ[:, :], SQ[:, :], ACT.Exp, scale=-1.0).then_inc(s["f_exp"], 1)
                nc.scalar.preload_act_table_set(LN)
                if att:
                    act.wait_ge(s["f_exp"], a + 1)
                    nc.scalar.activation(SQ[:, :], SQ[:, :], ACT.Ln, bias=1.0).then_inc(s["f_log"], 1)
                if late:
                    for h in range(2):
                        act.wait_ge(s["rms_add"], 2 * l + h + 1)
                        nc.scalar.activation(RSL[:, hs(h)], RSL[:, hs(h)], ACT.Ln, scale=RMS_SCALE)\
                            .then_inc(s["rr_ln"], 1)
                nc.scalar.preload_act_table_set(LN_EXP)
                if late:
                    for h in range(2):
                        act.wait_ge(s["rr_ln"], 2 * l + h + 1)
                        nc.scalar.activation(RSL[:, hs(h)], RSL[:, hs(h)], ACT.Exp, scale=-0.5)\
                            .then_inc(s["rr_out"], 1)
                if mix:
                    relu(it, 2, range(4))
                if att:
                    for h in range(2):
                        act.wait_ge(s["proj_mm"], 12 * a + 8 + h + 1)
                        nc.scalar.activation(V[:, hs(h)], QB[2 + h][:, :], ACT.Identity, bias=col("bv"))\
                            .then_inc(s["v_out"], 1)
                    for h in range(2):
                        act.wait_ge(s["proj_mm"], 12 * a + 10 + h + 1)
                        nc.scalar.activation(EO[:, hs(h)], QB[h][:, :], ACT.Identity, bias=neg_bo, scale=-1.0)\
                            .then_inc(s["o_out"], 1)
                if last:
                    ahead_step(2)
                if mix:
                    relu(it, 3, range(4))
                if att:
                    act.wait_ge(s["lf2_out"], a + 1)
                    nc.scalar.activation(RS_FS[:, :], LF_UT[:, :], ACT.Exp).then_inc(s["fs_out"], 1)
                    act.wait_ge(s["lg_out"], a + 1)
                    nc.scalar.activation(XC_IS[:, :], LI[:, :], ACT.Exp).then_inc(s["is_out"], 1)
                if mix:
                    relu(it, 4, range(4))
                if late:
                    for h in range(2):
                        act.wait_ge(s["l2c_mm"], 2 * l + h + 1)
                        nc.scalar.activation(SQL[:, hs(h)], QB[2 + h][:, :], ACT.Square).then_inc(s["sq2_out"], 1)
                if last_late:
                    ahead_step(6)
                if att:
                    act.wait_ge(s["ar_out"], a + 1)
                    nc.scalar.activation(LI[:, :], LI[:, :], ACT.Exp).then_inc(s["eu_out"], 1)
                if att and not plain:
                    act.wait_ge(s["lam_in"], 2 * a + 2)
                    nc.scalar.activation(lam[:, :], lam[:, :], ACT.Exp).then_inc(s["lam_out"], 1)
                if att:
                    act.wait_ge(s["lf_out"], a + 1)
                    act.wait_ge(s["o_out"], 2 * a + 2)
                    nc.scalar.activation(SQ[:, :], EO[:, :], ACT.Abs).then_inc(s["o_abs"], 1)
                    act.wait_ge(s["o_abs"], a + 1)
                    nc.scalar.activation(SQ[:, :], SQ[:, :], ACT.Exp, scale=-1.0).then_inc(s["o_exp"], 1)
                    act.wait_ge(s["o_exp"], a + 1)
                    nc.scalar.activation(SQ[:, :], SQ[:, :], ACT.Ln, bias=1.0).then_inc(s["o_log"], 1)
                if last:
                    ahead_step(3)
                if mix:
                    relu(it, 5, range(4))
                if late:
                    for h in range(2):
                        act.wait_ge(s["var2_mm"], 2 * l + h + 1)
                        nc.scalar.activation(RSL[:, hs(h)], QB[2 + h][:, :], ACT.Ln, bias=TOK_EPS)\
                            .then_inc(s["rs2_ln"], 1)
                    for h in range(2):
                        act.wait_ge(s["rs2_ln"], 2 * l + h + 1)
                        nc.scalar.activation(RSL[:, hs(h)], RSL[:, hs(h)], ACT.Exp, scale=-0.5)\
                            .then_inc(s["rs2_out"], 1)
                if last:
                    ahead_step(4)
                if mix:
                    last_relu(it, (0, 1))
                if att and not plain:
                    for h in range(2):
                        act.wait_ge(s["ut_mm"], 2 * a + h + 1)
                        nc.scalar.activation(LF_UT[:, hs(h)], QB[h][:, :], ACT.Identity).then_inc(s["ut_out"], 1)
                if mix:
                    last_relu(it, (2, 3))
                if att:
                    for h in range(2):
                        act.wait_ge(s["den_mm"], 2 * a + h + 1)
                        nc.scalar.activation(K_NN[:, hs(h)], QB[2 + h][:, :], ACT.Square).then_inc(s["den_sq"], 1)
                if att and not plain:
                    act.wait_ge(s["lam_out"], a + 1)
                    for n in range(SB):
                        act.wait_ge(s["av_mm"], SB * a + n + 1)
                        nc.scalar.activation(SQ[:, C * n:C * n + C], QB[n][:, C:2 * C], ACT.Identity,
                                             scale=lam[:, 2 * n:2 * n + 1]).then_inc(s["tmp_out"], 1)
                if att:
                    act.wait_ge(s["ee_out"], a + 1)
                    nc.scalar.activation(EO[:, :], EO[:, :], ACT.Exp, scale=-1.0).then_inc(s["et_out"], 1)
                if mix:
                    for h in range(2):
                        act.wait_ge(s["fin_add"], 2 * it + h + 1)
                        nc.scalar.activation(hh(gm, h), Z[:, hs(h)], ACT.Relu, bias=c_bias).then_inc(s["h1_out"], 1)

            turn(0, True, False, False)
            act.wait_ge(derived, 6)
            turn(1, True, True, False)
            act.wait_ge(setup_out, 5)
            for i, n in enumerate(("v1", "v2")):
                nc.scalar.activation(bn_s[:, i, :], bn_cols(n), ACT.Ln, bias=BN_EPS).then_inc(bn_ln, 1)
            act.wait_ge(bn_ln, 2)
            nc.scalar.activation(bn_s[:, :, :], bn_s[:, :, :], ACT.Exp, scale=-0.5).then_inc(bn_rs, 1)
            turn(2, True, True, True)
            with act.Fori(3, G) as it:
                turn(it, True, True, True)
            act.wait_ge(bn_ready, 7)
            turn(G, False, True, True)
            turn(G + 1, False, False, True)
            ahead_step(7)
            plain_pass(act, turn, again=ahead_step)

            for t in range(2):
                act.wait_ge(b["nmx"], 1)
                nc.scalar.activation(wx[:, t, :], QB[t][:, 0:E], ACT.Exp, bias=wmx[:, t:t + 1],
                                     accum_out=wsm[:, t:t + 1]).then_inc(b["ex"], 1)

            def h1(g, t):
                for k in range(2):
                    act.wait_ge(b["l1_mm"], 16 * g + 2 * t + k + 1)
                    count = 1 + 2 * N_AHEAD if isinstance(g, int) and k == 0 else 1
                    nc.scalar.activation(H1[t % 2][:, k, :], TB[k][:, :], ACT.Relu, bias=bn_t[:, 0, t % EP:t % EP + 1],
                                         scale=bn_s[:, 0, t % EP:t % EP + 1]).then_inc(b["h1"], count)

            def h2(g, t):
                for k in range(2):
                    act.wait_ge(b["l2_mm"], 16 * g + 2 * t + k + 1)
                    nc.scalar.activation(H2[t % 2][:, k, :], TB[2 + k][:, :], ACT.Relu,
                                         bias=bn_t[:, 1, t % EP:t % EP + 1],
                                         scale=bn_s[:, 1, t % EP:t % EP + 1]).then_inc(b["h2"], 1)

            def experts(g):
                for t in range(2 * EP):
                    h1(g, t)
                    h2(g, t - 1)

            h1(0, N_AHEAD)
            with act.Fori(1, G) as g:
                experts(g)
            h2(G - 1, 2 * EP - 1)

        @block.tensor
        def _(pe):
            pe.wait_ge(id_ready, 2)
            for _ in range(N_WARM):
                pe.matmul(QB[0][:, 0:P], ident[:, :], ident[:, :], start=True, stop=True)
            pe.wait_ge(mix_loaded, 16 * N_MIX)
            pe.transpose(TB[0][:, 0:P], w2_raw, ident[:, :]).then_inc(setup_mm, 1)
            pe.transpose(TB[1][:, 0:D], w4_raw, ident[0:D, 0:D]).then_inc(setup_mm, 1)
            pe.transpose(TB[2][:, 0:NM], mix_rows, ident[0:NM, 0:NM]).then_inc(setup_mm, 1)
            pe.wait_ge(setup_out, 3)
            pe.wait_ge(cleared, 6)

            def inputs(it, js):
                for j in js:
                    pe.matmul(TB[j][:, :], wac[:, :], X[:, tc(j)], start=True, stop=True).then_inc(s["ac_mm"], 1)

            def layer(it, k, js):
                for j in js:
                    if k == 0:
                        pe.wait_ge(s["u0_out"], 4 * it + JS.index(j) + 1)
                    else:
                        pe.wait_ge(s["mix_relu"], 24 * it + 4 * (k - 1) + JS.index(j) + 1)
                    pe.matmul(TB[j][:, :], w2T[:, :], U3[:, 2 * j:2 * j + 2, 0:T], start=True, stop=True)\
                        .then_inc(s["mix_mm"], 1)

            def project(a, l, p, late):
                freed = (None, "rs_ln", "f_out", "i_out", "k_out", "q_out")[p]
                for h in range(2):
                    if p == 0:
                        pe.wait_ge(s["xn_out"], 2 * a + h + 1)
                        if late:
                            pe.wait_ge(s["rms_add"], 2 * l + h + 1)
                    else:
                        pe.wait_ge(s[freed], 2 * a + h + 1)
                    pe.matmul(QB[2 - 2 * (p % 2) + h][:, :], wproj[:, p, :], XC_IS[:, hs(h)], start=True, stop=True)\
                        .then_inc(s["proj_mm"], 1)

            def scores(a, bs):
                for bb in bs:
                    k, n = bb // SB, bb % SB
                    bank = QB[SCORE_BANK[bb]]
                    if bb < 2:
                        pe.wait_ge(s["o_out"], 2 * a + bb + 1)
                    elif bb < 4:
                        pe.wait_ge(s["v_out"], 2 * a + bb - 1)
                    elif bb < 6:
                        pe.wait_ge(s["at_out"], GB * a + bb - 3)
                    else:
                        pe.wait_ge(s["at_out"], GB * a + bb - 1)
                    pe.matmul(bank[:, 0:T], KZ[:, k, T * n:T * n + C], Q[:, T * n:T * n + T], start=True, stop=True)
                    pe.matmul(bank[:, T:T + C], KZ[:, k, T * n + C:T * n + T], Q[:, T * n + C:T * n + T],
                              start=True, stop=True).then_inc(s["at_mm"], 1)

            def values(a, n):
                pe.wait_ge(s["at_out"], GB * a + GB)
                pe.wait_ge(s["ut_out"], 2 * a + min(n + 1, 2))
                if n >= 2:
                    pe.wait_ge(s["den_sq"], 2 * a + n - 1)
                for c, w in ((0, T), (1, C)):
                    for k in range(2):
                        mm = pe.matmul(QB[n][half[k], T * c:T * c + w],
                                       LF_UT[:, C * (2 * n + c) + D * k:C * (2 * n + c) + D * k + D],
                                       AT[:, SB * k + n, T * c:T * c + w], start=True, stop=True)
                mm.then_inc(s["av_mm"], 1)

            def final(it, h):
                pe.wait_ge(s["uf_out"], 8 * it + 4 * h + 4)
                for k in range(2):
                    n = SB * k + 2 * h
                    mm = pe.matmul(TB[h][half[k], :], w4T[:, :], UF3[:, n:n + 2, 0:T], start=True, stop=True)
                mm.then_inc(s["fin_mm"], 1)

            def ahead_step(i, done=0):
                for k in range(2):
                    if i < N_AHEAD:
                        if done + i > 0:
                            pe.wait_ge(ahead["h1"], 2 * (done + i))
                        pe.matmul(TB[k][:, :], fw1[:, k, i % EP, :], xn2(0, i // EP), start=True, stop=True)\
                            .then_inc(ahead["l1_mm"], 1)
                for k in range(2):
                    if i > 0:
                        j = i - 1
                        pe.wait_ge(ahead["h1"], 2 * (done + j) + k + 1)
                        if done + j > 0:
                            pe.wait_ge(ahead["h2"], 2 * (done + j))
                        pe.matmul(TB[2 + k][:, :], fw2[:, j % EP, :], H1[j % 2][:, k, :], start=True, stop=True)\
                            .then_inc(ahead["l2_mm"], 1)

            def turn(it, mix, att, late, plain=False):
                a, l = it - 1, it - 2
                gm, ga, gl = (it - G, a - G, l - G) if plain else (it, a, l)
                last = isinstance(it, int) and it == G
                last_late = isinstance(it, int) and it == G + 1
                if plain:
                    settle(pe, it, mix, att, late)
                if mix:
                    pe.wait_ge(x_in, 16 * it + 16)
                    after(pe, s["mix_add"], 28 * it)
                    inputs(it, JS[0:2])
                if att:
                    for h in range(2):
                        if not plain:
                            after(pe, s["hr_out"], SB * a - SB + h + 1)
                        pe.wait_ge(s["h1_out"], 2 * a + h + 1)
                        pe.matmul(QB[h][:, :], center_mat[:, :], hh(ga, h), start=True, stop=True)\
                            .then_inc(s["lnc_mm"], 1)
                if last:
                    ahead_step(0)
                if mix:
                    after(pe, s["fin_add"], 2 * it)
                    inputs(it, JS[2:4])
                    layer(it, 0, JS[0:2])
                if att:
                    for h in range(2):
                        pe.wait_ge(s["xc_out"], 2 * a + h + 1)
                        pe.wait_ge(s["sq_out"], 2 * a + h + 1)
                        pe.matmul(QB[h][:, :], mean_mat[:, :], SQ[:, hs(h)], start=True, stop=True)\
                            .then_inc(s["var_mm"], 1)
                if last_late:
                    ahead_step(5)
                if mix:
                    layer(it, 0, JS[2:4])
                if late:
                    for h in range(2):
                        pe.wait_ge(s["sqo_out"], 2 * l + h + 1)
                        pe.matmul(QB[2 + h][:, :], mean_mat[:, :], SQL[:, hs(h)], start=True, stop=True)\
                            .then_inc(s["rms_mm"], 1)
                if last:
                    ahead_step(1)
                if mix:
                    layer(it, 1, JS)
                if att:
                    for p in range(4):
                        project(a, l, p, late)
                if mix:
                    layer(it, 2, JS)
                if att:
                    for p in range(4, 6):
                        project(a, l, p, late)
                if last:
                    ahead_step(2)
                if mix:
                    layer(it, 3, JS)
                if att and not plain:
                    pe.wait_ge(s["kz_out"], 2 * a + 2)
                    pe.wait_ge(s["q_out"], 2 * a + 2)
                    scores(a, range(0, 4))
                if last_late:
                    ahead_step(6)
                if mix:
                    layer(it, 4, JS)
                if late:
                    for h in range(2):
                        if att:
                            pe.wait_ge(s["at_out"], GB * a + 3 + h)
                        else:
                            pe.wait_ge(s["rms_add"], 2 * l + h + 1)
                        pe.wait_ge(s["h2_out"], 2 * l + h + 1)
                        pe.matmul(QB[2 + h][:, :], center_mat[:, :], hh(gl, h), start=True, stop=True)\
                            .then_inc(s["l2c_mm"], 1)
                if att and not plain:
                    scores(a, range(4, 6))
                if last:
                    ahead_step(3)
                if mix:
                    layer(it, 5, JS)
                if att and not plain:
                    scores(a, range(6, 8))
                if late:
                    for h in range(2):
                        pe.wait_ge(s["sq2_out"], 2 * l + h + 1)
                        pe.wait_ge(s["xc2_out"], 2 * l + h + 1)
                        pe.matmul(QB[2 + h][:, :], mean_mat[:, :], SQL[:, hs(h)], start=True, stop=True)\
                            .then_inc(s["var2_mm"], 1)
                if last:
                    ahead_step(4)
                if mix:
                    layer(it, 6, JS_LAST)
                if att and not plain:
                    for h in range(2):
                        pe.wait_ge(s["u_out"], 2 * a + h + 1)
                        pe.wait_ge(s["at_out"], GB * a + 6 + h + 1)
                        for c in range(4):
                            mm = pe.transpose(QB[h][:, C * c:C * c + C], V[:, HC * h + C * c:HC * h + C * c + C],
                                              ident[:, :])
                        mm.then_inc(s["ut_mm"], 1)
                if att:
                    for h in range(2):
                        pe.wait_ge(s["nq_out"], 2 * a + h + 1)
                        if late:
                            pe.wait_ge(s["rs2_ln"], 2 * l + h + 1)
                        if plain:
                            pe.wait_ge(s["v_out"], 2 * a + h + 1)
                        pe.matmul(QB[2 + h][:, :], sum_mat[:, :], K_NN[:, hs(h)], start=True, stop=True)\
                            .then_inc(s["den_mm"], 1)
                if att and plain:
                    for h in range(2):
                        with pe.Fori(0, D) as j:
                            J = (ga * 2 + h) * D + j
                            pe.wait_ge(s["kz_out"], 2 * a + 2)
                            pe.wait_ge(s["o_out"], 2 * a + 2)
                            pe.wait_ge(rec, J * REC + 2)
                            for k in range(2):
                                pe.matmul(QB[0][:, :], sel, KZ[:, k, hs(h)], start=(k == 0), stop=(k == 1))
                            pe.matmul(QB[1][:, :], sel, Q[:, hs(h)], start=True, stop=True).then_inc(bcast_mm, 1)
                for n in range(SB):
                    if att and not plain:
                        values(a, n)
                    if mix and n % 2 == 1:
                        final(it, n // 2)

            turn(0, True, False, False)
            pe.wait_ge(att_loaded, 16 * N_ATT)
            pe.transpose(QB[2][:, 0:NV - NM], att_rows, ident[0:NV - NM, 0:NV - NM]).then_inc(setup_mm, 1)
            pe.wait_ge(bn_loaded, 16 * N_BN)
            pe.transpose(QB[3][:, 0:NBN], bn_rows, ident[0:NBN, 0:NBN]).then_inc(setup_mm, 1)
            pe.wait_ge(setup_out, 5)
            pe.wait_ge(mats, 9)
            turn(1, True, True, False)
            turn(2, True, True, True)
            with pe.Fori(3, G) as it:
                turn(it, True, True, True)
            pe.wait_ge(ffn_loaded, 16 * N_FFN)
            turn(G, False, True, True)
            turn(G + 1, False, False, True)
            pe.wait_ge(range_min, 1)
            pe.transpose(QB[0][0:1, 0:P], wide_f[:, 0:1], ident[:, :]).then_inc(range_mm, 1)
            ahead_step(7)

            def wait_cleared():
                pe.wait_ge(feat_cleared, 2)

            plain_pass(pe, turn, wait_cleared, ahead_step)

            pe.wait_ge(s["feat_out"], SB * G)
            pe.wait_ge(bn_ready, 8)
            for t in range(2):
                pe.matmul(QB[t][:, 0:E], feat[:, P * t:P * t + P], wr[:, :], start=True, stop=False)
                pe.matmul(QB[t][:, 0:E], ones_row[:, :], br_row[:, :], start=False, stop=True)\
                    .then_inc(b["lg_mm"], 1)
            pe.wait_ge(ahead["h2"], 2 * N_AHEAD)
            for t in range(2):
                pe.wait_ge(b["wb"], t + 1)
                for p in range(EP):
                    mm = pe.matmul(TB[p][:, P * t:P * t + P], wb[:, t, P * p:P * p + P], ident[:, :],
                                   start=True, stop=True)
            mm.then_inc(b["w_mm"], 1)
            for t in range(2):
                mm = pe.transpose(QB[2][0:E, P * t:P * t + P], wn[:, t, :], ident[:, :])
            mm.then_inc(b["wt_mm"], 1)
            pe.wait_ge(b["wt_out"], 1)
            pe.matmul(QB[3][:, 0:T], bo_w[:, :], wt, start=True, stop=True).then_inc(b["bo_mm"], 1)
            pe.wait_ge(b["w_out"], EP)
            pe.wait_ge(b["bo_out"], 1)

            def l1(g, t):
                for k in range(2):
                    if not isinstance(g, int):
                        pe.wait_ge(b["h1"], 16 * g + 2 * t)
                    count = 1 + 2 * N_AHEAD if isinstance(g, int) and k == 0 else 1
                    pe.matmul(TB[k][:, :], fw1[:, k, t % EP, :], xn2(g, t // EP), start=True, stop=True)\
                        .then_inc(b["l1_mm"], count)

            def l2(g, t):
                for k in range(2):
                    pe.wait_ge(b["h1"], 16 * g + 2 * t + k + 1)
                    pe.wait_ge(b["h2"], 16 * g + 2 * t)
                    pe.matmul(TB[2 + k][:, :], fw2[:, t % EP, :], H1[t % 2][:, k, :], start=True, stop=True)\
                        .then_inc(b["l2_mm"], 1)

            def l3(g, t):
                f, p = t // EP % 2, t % EP
                if p == 0:
                    after(pe, b["res"], 2 * g - 1 + f)
                pe.wait_ge(b["hw"], 16 * g + 2 * t + 2)
                src = H2_AHEAD[t] if isinstance(g, int) and g == 0 and t < N_AHEAD else H2[t % 2]
                for k in range(2):
                    mm = pe.matmul(QB[f][half[k], :], fwo[:, p, :], src[:, k, :],
                                   start=(p == 0), stop=(p == EP - 1))
                if p == EP - 1:
                    mm.then_inc(b["l3_mm"], 1)
                return mm

            def turn_out(g, f):
                pe.wait_ge(b["res"], 2 * g + f + 1)
                after(pe, b["tr_out"], 4 * g - 2 + 2 * f)
                for n in range(2):
                    for r in range(2):
                        mm = pe.transpose(QB[2 + f][:, P * (2 * n + r):P * (2 * n + r) + P],
                                          RES[f][:, T * n + r:T * n + T:2], ident[:, :])
                mm.then_inc(b["tr_mm"], 1)

            def experts(g):
                for t in range(2 * EP):
                    l1(g, t)
                    l2(g, t - 1)
                    l3(g, t - 2)
                    if t == 3:
                        turn_out(g - 1, 1)
                    if t == EP + 3:
                        turn_out(g, 0)

            l1(0, N_AHEAD)
            l3(0, 0).then_inc(b["l2_mm"], 2 * N_AHEAD)
            l3(0, 1).then_inc(b["h2"], 2 * N_AHEAD)
            for t in range(2, 2 * EP - 2):
                l3(0, t)
            turn_out(0, 0)
            with pe.Fori(1, G) as g:
                experts(g)
            l2(G - 1, 2 * EP - 1)
            l3(G - 1, 2 * EP - 2)
            l3(G - 1, 2 * EP - 1)
            turn_out(G - 1, 1)

        @block.vector
        def _(dve):
            for k in range(2):
                for h in range(2):
                    nc.vector.memset(side[half[h], k:k + 1], float(h == k)).then_inc(side_ready, 1)
            for m, v in ((mean_mat, 1.0 / D), (sum_mat, 1.0)):
                for h in range(2):
                    nc.vector.memset(m[half[h], D * h:D * h + D], v).then_inc(mats, 1)
                    nc.vector.memset(m[half[h], D * (1 - h):D * (1 - h) + D], 0.0).then_inc(mats, 1)
            dve.wait_ge(mats, 8)
            dve.wait_ge(id_ready, 2)
            nc.vector.tensor_tensor(center_mat[:, :], ident[:, :], mean_mat[:, :], ALU.subtract).then_inc(mats, 1)
            for i, (dst, src) in enumerate(((w2T[:, :], TB[0][:, 0:P]), (w4T[:, :], TB[1][:, 0:D]),
                                            (cols[:, 0:NM], TB[2][:, 0:NM]))):
                dve.wait_ge(setup_mm, i + 1)
                nc.vector.tensor_copy(dst, src).then_inc(setup_out, 1)
            dve.wait_ge(setup_out, 3)
            nc.vector.tensor_tensor(a_bias, col("tok_b1"), col("tok_b2"), ALU.add).then_inc(derived, 1)
            nc.vector.scalar_tensor_tensor(out=c_bias, in0=col("tok_b4"), scalar=2.0, in1=col("tok_b3"),
                                           op0=ALU.mult, op1=ALU.add).then_inc(derived, 1)
            dve.wait_ge(cleared, 6)
            dve.wait_ge(mask_ready, 3)

            def add(it, k, js):
                for i, j in enumerate(js):
                    dve.wait_ge(s["mix_mm"], 28 * it + 4 * k + i + 1)
                    nc.vector.tensor_tensor(Z[:, tc(j)], TB[j][:, :], A[:, tc(j)], ALU.add).then_inc(s["mix_add"], 1)

            def start(it, js):
                for i in js:
                    j = JS[i]
                    dve.wait_ge(s["ac_mm"], 4 * it + i + 1)
                    nc.vector.tensor_copy(CT[half[j // 2], 512 * (j % 2):512 * (j % 2) + 512], TB[j][half[1], :])\
                        .then_inc(s["c_out"], 1)
                    dve.wait_ge(s["a_out"], 8 * it + 2 * i + 2)
                    nc.vector.tensor_scalar(U3[:, 2 * j:2 * j + 2, 1:UW], A3[:, 2 * j:2 * j + 2, :], 0.0, None,
                                            ALU.max).then_inc(s["u0_out"], 1)

            def scores(a, bs):
                for bb in bs:
                    dve.wait_ge(s["at_mm"], GB * a + bb + 1)
                    nc.vector.tensor_tensor(AT[:, bb, :], QB[SCORE_BANK[bb]][:, 0:3 * C], causal[:, :], ALU.mult)\
                        .then_inc(s["at_out"], 1)

            def turn(it, mix, att, late, plain=False):
                a, l = it - 1, it - 2
                gm, ga, gl = (it - G, a - G, l - G) if plain else (it, a, l)
                if plain:
                    settle(dve, it, mix, att, late)
                if mix:
                    dve.wait_ge(s["fin_add"], 2 * it)
                    start(it, (0, 1))
                if att:
                    dve.wait_ge(s["nn_out"], SB * a)
                    for h in range(2):
                        dve.wait_ge(s["sq_out"], 2 * a + h + 1)
                        nc.vector.tensor_copy(XC_IS[:, hs(h)], QB[h][:, :]).then_inc(s["xc_out"], 1)
                if mix:
                    start(it, (2, 3))
                    add(it, 0, JS)
                if att:
                    for h in range(2):
                        dve.wait_ge(s["xc_out"], 2 * a + h + 1)
                        dve.wait_ge(s["rs_out"], 2 * a + h + 1)
                        nc.vector.tensor_tensor(XC_IS[:, hs(h)], XC_IS[:, hs(h)], RS_FS[:, hs(h)], ALU.mult)\
                            .then_inc(s["xn_out"], 1)
                if late:
                    dve.wait_ge(s["xn2_out"], 2 * l)
                    for h in range(2):
                        dve.wait_ge(s["den_out"], l + 1)
                        dve.wait_ge(s["rms_mm"], 2 * l + h + 1)
                        nc.vector.tensor_tensor(RSL[:, hs(h)], QB[2 + h][:, :], K_NN[:, hs(h)], ALU.add)\
                            .then_inc(s["rms_add"], 1)
                if mix:
                    add(it, 1, JS)
                if att:
                    if late:
                        dve.wait_ge(s["rms_add"], 2 * l + 2)
                    for h in range(2):
                        dve.wait_ge(s["proj_mm"], 12 * a + 4 + h + 1)
                        nc.vector.tensor_scalar(K_NN[:, hs(h)], QB[2 + h][:, :], col("bk"), 1.0 / 8.0, ALU.add,
                                                ALU.mult).then_inc(s["k_out"], 1)
                    for h in range(2):
                        dve.wait_ge(s["proj_mm"], 12 * a + 6 + h + 1)
                        nc.vector.tensor_scalar(Q[:, hs(h)], QB[h][:, :], col("bq"), None, ALU.add)\
                            .then_inc(s["q_out"], 1)
                    dve.wait_ge(s["i_out"], 2 * a + 2)
                    nc.vector.tensor_scalar(LI[:, :], LI[:, :], 10.0, None, ALU.mult).then_inc(s["li_out"], 1)
                    dve.wait_ge(s["f_log"], a + 1)
                    nc.vector.scalar_tensor_tensor(out=LF_UT[:, :], in0=LF_UT[:, :], scalar=0.0, in1=SQ[:, :],
                                                   op0=ALU.min, op1=ALU.subtract).then_inc(s["lf_out"], 1)
                    dve.wait_ge(s["lf_out"], a + 1)
                    dve.wait_ge(s["li_out"], a + 1)
                    for n in range(SB):
                        nc.vector.tensor_tensor_scan(M3[:, n, 1:UW], LF_UT[:, T * n:T * n + T], LI[:, T * n:T * n + T],
                                                     0.0, ALU.add, ALU.max).then_inc(s["m_out"], 1)
                if mix:
                    add(it, 2, JS)
                if late:
                    for h in range(2):
                        dve.wait_ge(s["y_out"], 2 * l + h + 1)
                        nc.vector.scalar_tensor_tensor(out=hh(gl, h), in0=RSL[:, hs(h)], scalar=out_scale,
                                                       in1=hh(gl, h), op0=ALU.mult, op1=ALU.add)\
                            .then_inc(s["h2_out"], 1)
                if mix:
                    add(it, 3, JS)
                if att and not plain:
                    scores(a, range(0, 4))
                    dve.wait_ge(s["lf2_out"], a + 1)
                    for c in range(GB):
                        nc.vector.tensor_tensor_scan(NC_[:, C * c:C * c + C], LF_UT[:, C * c:C * c + C], zeros[:, :],
                                                     0.0, ALU.add, ALU.min).then_inc(s["nc_out"], 1)
                    dve.wait_ge(s["nc_out"], GB * a + GB)
                    dve.wait_ge(s["nd_out"], a)
                    dve.wait_ge(s["ends_kept"], a)
                    dve.wait_ge(s["lam_in"], 2 * a)
                    nc.vector.tensor_copy(ends[:, :].unsqueeze(2), NC3[:, :, C - 1:C]).then_inc(s["ends_out"], 1)
                    dve.wait_ge(s["ends_out"], a + 1)
                    nc.vector.scalar_tensor_tensor(out=NC3, in0=ends[:, :].unsqueeze(2).to_broadcast([P, GB, C]),
                                                   scalar=REF, in1=NC3, op0=ALU.mult, op1=ALU.subtract)\
                        .then_inc(s["nd_out"], 1)
                    nc.vector.tensor_scalar(lam[:, 0:GB:2], ends[:, 0:GB:2], 1.0 - REF, None, ALU.mult)\
                        .then_inc(s["lam_in"], 1)
                    nc.vector.tensor_scalar(lam[:, 1:GB:2], ends[:, 1:GB:2], REF, None, ALU.mult)\
                        .then_inc(s["lam_in"], 1)
                    nc.vector.tensor_copy(decay_ends[:, bass.ds(ga * GB, GB)], ends[:, :]).then_inc(s["ends_kept"], 1)
                if att and plain:
                    nc.vector.memset(NC_[:, :], 0.0).then_inc(s["nd_out"], 1)
                    nc.vector.memset(HR[:, :], 0.0).then_inc(hr_cleared, 1)
                if mix:
                    add(it, 4, JS)
                if late:
                    for h in range(2):
                        dve.wait_ge(s["sq2_out"], 2 * l + h + 1)
                        nc.vector.tensor_copy(xn2(gl, h), QB[2 + h][:, :]).then_inc(s["xc2_out"], 1)
                if att and not plain:
                    scores(a, range(4, 6))
                if mix:
                    add(it, 5, JS)
                if att:
                    dve.wait_ge(s["o_log"], a + 1)
                    nc.vector.scalar_tensor_tensor(out=EO[:, :], in0=EO[:, :], scalar=0.0, in1=SQ[:, :],
                                                   op0=ALU.max, op1=ALU.add).then_inc(s["sp_out"], 1)
                    dve.wait_ge(s["fs_out"], a + 1)
                    dve.wait_ge(s["ik_out"], a + 1)
                    dve.wait_ge(s["kz_out"], 2 * a + 2)
                    for n in range(SB):
                        r = slice(T * n, T * n + T)
                        nc.vector.tensor_tensor_scan(K_NN[:, r], RS_FS[:, r], XC_IS[:, r], 0.0, ALU.mult, ALU.add)\
                            .then_inc(s["nn_out"], 1)
                if att and not plain:
                    scores(a, range(6, 8))
                if mix:
                    add(it, 6, JS_LAST)
                if late:
                    for h in range(2):
                        dve.wait_ge(s["xc2_out"], 2 * l + h + 1)
                        dve.wait_ge(s["rs2_out"], 2 * l + h + 1)
                        nc.vector.tensor_tensor(xn2(gl, h), xn2(gl, h), RSL[:, hs(h)], ALU.mult)\
                            .then_inc(s["xn2_out"], 1)
                if att:
                    dve.wait_ge(s["den_sq"], 2 * a + 2)
                    nc.vector.tensor_scalar(K_NN[:, :], K_NN[:, :], 1e-12, RMS_EPS, ALU.max, ALU.mult)\
                        .then_inc(s["den_out"], 1)
                if att and plain:
                    for h in range(2):
                        with dve.Fori(0, D) as j:
                            J = (ga * 2 + h) * D + j
                            for k in range(2):
                                nc.vector.tensor_copy(sel[:, D * k:D * k + D],
                                                      ident[:, bass.ds(j + D * k, 1)].to_broadcast([P, D]))\
                                    .then_inc(rec, 1)
                            dve.wait_ge(hr_cleared, ga + 1)
                            dve.wait_ge(s["u_out"], 2 * a + h + 1)
                            dve.wait_ge(bcast_mm, J + 1)
                            nc.vector.tensor_tensor(vk, QB[0][:, :], V[:, hs(h)], ALU.mult).then_inc(rec, 1)
                            dve.wait_ge(rec, J * REC + 3)
                            for n in range(2):
                                q = slice(T * n, T * n + T)
                                nc.vector.tensor_tensor_scan(m_row[:, q], RS_FS[:, HC * h + T * n:HC * h + T * n + T],
                                                             vk[:, q], 0.0, ALU.mult, ALU.add).then_inc(rec, 1)
                            dve.wait_ge(rec, J * REC + 5)
                            nc.vector.tensor_tensor(mq, m_row, QB[1][:, :], ALU.mult).then_inc(rec, 1)
                            dve.wait_ge(rec, J * REC + 6)
                            nc.vector.tensor_tensor(HR[:, hs(h)], HR[:, hs(h)], mq, ALU.add).then_inc(rec, 1)
                    dve.wait_ge(rec, (ga + 1) * (2 * D * REC))
                if att and not plain:
                    if late:
                        dve.wait_ge(s["y_out"], 2 * l + 2)
                    for n in range(SB):
                        dve.wait_ge(s["tmp_out"], SB * a + n + 1)
                        nc.vector.scalar_tensor_tensor(out=HR3[:, n, C:T], in0=SQ[:, C * n:C * n + C],
                                                       scalar=lam[:, 2 * n + 1:2 * n + 2], in1=QB[n][:, T:T + C],
                                                       op0=ALU.mult, op1=ALU.add).then_inc(s["hr_a"], 1)
                        nc.vector.tensor_copy(HR3[:, n, 0:C], QB[n][:, 0:C]).then_inc(s["hr_out"], 1)
                if mix:
                    for h in range(2):
                        dve.wait_ge(s["fin_mm"], 2 * it + h + 1)
                        nc.vector.tensor_tensor(Z[:, hs(h)], TB[h][:, :], CT[:, hs(h)], ALU.add)\
                            .then_inc(s["fin_add"], 1)
                if att:
                    dve.wait_ge(s["et_out"], a + 1)
                    for h in range(2):
                        if not plain:
                            dve.wait_ge(s["hr_out"], SB * a + 2 * h + 2)
                            dve.wait_ge(s["hr_a"], SB * a + 2 * h + 2)
                        nc.vector.tensor_tensor(HR[:, hs(h)], HR[:, hs(h)], EO[:, hs(h)], ALU.mult)\
                            .then_inc(s["o_h"], 1)

            turn(0, True, False, False)
            dve.wait_ge(setup_mm, 4)
            nc.vector.tensor_copy(cols[:, NM:NV], QB[2][:, 0:NV - NM]).then_inc(setup_out, 1)
            dve.wait_ge(setup_mm, 5)
            nc.vector.tensor_copy(cols[:, NV:NV + NBN], QB[3][:, 0:NBN]).then_inc(setup_out, 1)
            dve.wait_ge(setup_out, 4)
            nc.vector.tensor_scalar(neg_bf, col("bgf"), -1.0, None, ALU.mult).then_inc(derived, 1)
            nc.vector.tensor_scalar(bias_i, col("bgi"), col("input_bias"), 0.1, ALU.add, ALU.mult).then_inc(derived, 1)
            nc.vector.tensor_scalar(neg_bo, col("bgo"), -1.0, None, ALU.mult).then_inc(derived, 1)
            nc.vector.tensor_scalar(out_scale, col("norm_scale"), RMS_SCALE ** 0.5, None, ALU.mult)\
                .then_inc(derived, 1)
            turn(1, True, True, False)
            dve.wait_ge(setup_out, 5)
            dve.wait_ge(bn_rs, 1)
            for i, (gn, bn, mn) in enumerate((("g1", "b1", "m1"), ("g2", "b2", "m2"))):
                nc.vector.tensor_tensor(bn_s[:, i, :], bn_s[:, i, :], bn_cols(gn), ALU.mult).then_inc(bn_ready, 1)
                nc.vector.tensor_tensor(bn_t[:, i, :], bn_cols(bn), bn_cols(mn), ALU.subtract).then_inc(bn_ready, 1)
            dve.wait_ge(bn_ready, 4)
            nc.vector.tensor_tensor(bn_t[:, :, :], bn_t[:, :, :], bn_s[:, :, :], ALU.mult).then_inc(bn_ready, 1)
            dve.wait_ge(bn_ready, 5)
            for i, ben in enumerate(("be1", "be2")):
                nc.vector.tensor_tensor(bn_t[:, i, :], bn_t[:, i, :], bn_cols(ben), ALU.add).then_inc(bn_ready, 1)
            dve.wait_ge(ffn_loaded, 16 * N_FFN)
            nc.vector.tensor_scalar(wr[:, :], wr[:, :], 1.0 / NB, None, ALU.mult).then_inc(bn_ready, 1)
            turn(2, True, True, True)
            with dve.Fori(3, G) as it:
                turn(it, True, True, True)
            turn(G, False, True, True)
            turn(G + 1, False, False, True)

            dve.wait_ge(s["ends_kept"], G)
            nc.vector.tensor_reduce(wide_f[:, 0:1], decay_ends[:, :], AX_X, ALU.min).then_inc(range_min, 1)
            dve.wait_ge(range_mm, 1)
            nc.vector.tensor_reduce(wide_f[0:1, 1:2], QB[0][0:1, 0:P], AX_X, ALU.min).then_inc(range_all, 1)
            dve.wait_ge(range_all, 1)
            nc.vector.tensor_scalar(wide_i[:, :], wide_f[0:1, 1:2], WIDEST, None, ALU.is_lt).then_inc(wide_ready, 1)
            plain_pass(dve, turn)

            for t in range(2):
                dve.wait_ge(b["lg_mm"], t + 1)
                nc.vector.tensor_reduce(wmx[:, t:t + 1], QB[t][:, 0:E], AX_X, ALU.max).then_inc(b["mx"], 1)
            dve.wait_ge(b["mx"], 2)
            nc.vector.tensor_scalar(wmx, wmx, -1.0, None, ALU.mult).then_inc(b["nmx"], 1)
            dve.wait_ge(b["ex"], 2)
            nc.vector.reciprocal(wrc, wsm).then_inc(b["rc"], 1)
            dve.wait_ge(b["rc"], 1)
            for t in range(2):
                nc.vector.tensor_scalar(wn[:, t, :], wx[:, t, :], wrc[:, t:t + 1], None, ALU.mult)\
                    .then_inc(b["wn"], 1)
            for t in range(2):
                dve.wait_ge(b["wn"], t + 1)
                nc.vector.tensor_copy(wb[:, t, :].rearrange("p (e c) -> p e c", c=D),
                                      wn[:, t, :].unsqueeze(2).to_broadcast([P, E, D])).then_inc(b["wb"], 1)
            dve.wait_ge(b["w_mm"], 1)
            for p in range(EP):
                nc.vector.tensor_copy(WM[:, p, :], TB[p][:, 0:T]).then_inc(b["w_out"], 1)
            dve.wait_ge(b["wt_mm"], 1)
            nc.vector.tensor_copy(wt, QB[2][0:E, 0:T]).then_inc(b["wt_out"], 1)
            dve.wait_ge(b["bo_mm"], 1)
            nc.vector.tensor_copy(BOW, QB[3][:, 0:T]).then_inc(b["bo_out"], 1)

            def weigh(g, t):
                run_ahead = isinstance(g, int) and g == 0 and t < N_AHEAD
                for k in range(2):
                    if run_ahead:
                        dve.wait_ge(ahead["h2"], 2 * t + k + 1)
                    else:
                        dve.wait_ge(b["h2"], 16 * g + 2 * t + k + 1)
                    v = rowsof((H2_AHEAD[t] if run_ahead else H2[t % 2])[:, k, :])
                    nc.vector.tensor_tensor(v, v, WM[:, t % EP, :].unsqueeze(1).to_broadcast([P, 2, T]), ALU.mult)\
                        .then_inc(b["hw"], 1)

            def finish(g, f):
                dve.wait_ge(b["l3_mm"], 2 * g + f + 1)
                dve.wait_ge(b["res_a"], 2 * g + f + 1)
                after(dve, b["tr_mm"], 2 * g - 1 + f)
                nc.vector.tensor_tensor(RES[f], QB[f][:, :], R1[f], ALU.add).then_inc(b["res"], 1)

            def token_major(g, f):
                dve.wait_ge(b["tr_mm"], 2 * g + f + 1)
                dve.wait_ge(stored[f], 32 * g)
                for k in range(2):
                    nc.vector.tensor_copy(OUTT[f][:, k].rearrange("p n (r d) -> p (n r) d", r=2),
                                          QB[2 + f][:, :].rearrange("p (m k d) -> p m k d", k=2, d=D)[:, :, k, :])\
                        .then_inc(b["tr_out"], 1)

            def experts(g, first=False):
                for t in range(2 * EP):
                    weigh(g, t)
                    if t == 1 and not first:
                        finish(g - 1, 1)
                    if t == 3 and not first:
                        token_major(g - 1, 1)
                    if t == EP + 1:
                        finish(g, 0)
                    if t == EP + 3:
                        token_major(g, 0)

            experts(0, True)
            with dve.Fori(1, G) as g:
                experts(g)
            finish(G - 1, 1)
            token_major(G - 1, 1)


_INS = ["x", "tok_W1", "tok_b1", "tok_W2", "tok_b2", "tok_W3", "tok_b3", "tok_W4", "tok_b4",
        "attn_Wq", "attn_bq", "attn_Wk", "attn_bk", "attn_Wv", "attn_bv", "attn_Wg", "attn_bg",
        "attn_input_bias", "attn_norm_scale", "ffn_Wr", "ffn_br", "ffn_W1", "ffn_b1", "ffn_g1", "ffn_be1",
        "ffn_m1", "ffn_v1", "ffn_W2", "ffn_b2", "ffn_g2", "ffn_be2", "ffn_m2", "ffn_v2", "ffn_Wo", "ffn_bo"]


def kernel(**inputs):
    import numpy as np
    import concourse.bacc as bacc
    from concourse.bass_utils import run_bass_kernel_spmd as run

    nc = bacc.Bacc("TRN2", target_bir_lowering=False, num_devices=1)
    arrays, args = {}, []
    for name in _INS:
        a = np.ascontiguousarray(inputs[name if name == "x" else "L0_" + name])
        arrays["in_" + name] = a
        args.append(nc.dram_tensor("in_" + name, a.shape, mybir.dt.from_np(a.dtype), kind="ExternalInput").ap())
    result = nc.dram_tensor("result", (NB, T, D), F32, kind="ExternalOutput").ap()
    build(nc, *args, result)
    r = run(nc, [arrays], core_ids=[0])
    return r.results[0]["result"]
```
